# Optimizing a Trainium2 kernel written in Bass

```python
import numpy as np
import jax
import jax.numpy as jnp

def _softmax(x, axis=-1):
    return jax.nn.softmax(x, axis=axis)

def _gelu(x):
    return jax.nn.gelu(x, approximate=True)

def _silu(x):
    return jax.nn.silu(x)

def _sigmoid(x):
    return jax.nn.sigmoid(x)

def _layernorm(x, axis=-1, eps=1e-05):
    m = jnp.mean(x, axis=axis, keepdims=True)
    v = jnp.var(x, axis=axis, keepdims=True)
    return (x - m) / jnp.sqrt(v + eps)

def _scatter_add(tgt, idx, src, axis=0):
    return tgt.at[idx].add(src)

def _segment_sum(src, seg, n):
    return jax.ops.segment_sum(src, seg, n)
kernel_name = 'mk_pixart_seq_d4_seqx_r4_32abc5'

def setup_inputs(seed: int=0):
    np.random.seed(seed)
    _w = jnp.asarray

    def _rec_inputs():
        import jax
        import jax.numpy as jnp
        _rk = jax.random.key(seed)
        x = -0.0002928 + 1 * jax.random.normal(jax.random.fold_in(_rk, 1), (16, 256, 256), jnp.float32)
        _lenS = 256 - jax.random.randint(jax.random.fold_in(_rk, 7), (16,), 0, max(1, 256 // 4) + 1, jnp.int32)
        _lenS2 = 77 - jax.random.randint(jax.random.fold_in(_rk, 8), (16,), 0, max(1, 77 // 4) + 1, jnp.int32)
        cond_1024 = 0.000887014 + 1.03683 * jax.random.normal(jax.random.fold_in(_rk, 11), (16, 256), jnp.float32)
        _ctx_1024P = jax.random.normal(jax.random.fold_in(_rk, 12), (16, 16, 256), jnp.float32)
        _ctx_1024c = jax.random.dirichlet(jax.random.fold_in(_rk, 512), 0.3 * jnp.ones((16,), jnp.float32), (16, 77))
        _ctx_1024t = jnp.einsum('bsk,bkd->bsd', _ctx_1024c, _ctx_1024P)
        _ctx_1024t = _ctx_1024t * jax.lax.rsqrt(jnp.mean(jnp.square(_ctx_1024t)) + 1e-12) * 0.953939
        ctx_1024 = -0.00606593 + 0.997213 * (_ctx_1024t + 0.3 * jax.random.normal(jax.random.fold_in(_rk, 612), (16, 77, 256), jnp.float32))
        _validS = jnp.arange(256)[None, :] < _lenS[:, None]
        _validS2 = jnp.arange(77)[None, :] < _lenS2[:, None]
        _causal = jnp.tril(jnp.ones((256, 256), dtype=bool))
        mask_BxS2_bf1 = jnp.ones((16, 77), dtype=bool)
        mask_SxS_bk0 = jnp.logical_not(jnp.broadcast_to(_validS[0:1, :], (256, 256)))
        return (x, cond_1024, ctx_1024, mask_BxS2_bf1, mask_SxS_bk0)
    x, cond_1024, ctx_1024, mask_BxS2_bf1, mask_SxS_bk0 = _rec_inputs()

    def _L0_xcond_setup():
        import jax, jax.numpy as jnp
        import numpy as np
        B, N, D, H, LC = (2, 256, 256, 16, 77)
        HD = D // H
        BLOCK = 16
        ROPE_BASE = 10000.0
        EPS = 1e-05

        def _block_diff_mask(n, block_size):
            idx = np.arange(2 * n)
            q = idx[:, None]
            kv = idx[None, :]
            fq = q >= n
            fkv = kv >= n
            bq = np.where(fq, (q - n) // block_size, q // block_size)
            bkv = np.where(fkv, (kv - n) // block_size, kv // block_size)
            block_diagonal = (bq == bkv) & (fq == fkv)
            offset_block_causal = (bq > bkv) & fkv & ~fq
            block_causal = (bq >= bkv) & fq & fkv
            return jnp.asarray(block_diagonal | offset_block_causal | block_causal)

        def _rope_tables(n):
            inv_freq = 1.0 / ROPE_BASE ** (np.arange(0, HD, 2, dtype=np.float32) / HD)
            freqs = np.outer(np.arange(n, dtype=np.float32), inv_freq)
            emb = np.concatenate([freqs, freqs], axis=-1)
            cos = jnp.asarray(np.cos(emb), jnp.float32)[None, :, None, :]
            sin = jnp.asarray(np.sin(emb), jnp.float32)[None, :, None, :]
            return (cos, sin)

        def _ln(x, w):
            xf = x.astype(jnp.float32)
            mu = jnp.mean(xf, axis=-1, keepdims=True)
            var = jnp.mean(jnp.square(xf - mu), axis=-1, keepdims=True)
            y = (xf - mu) * jax.lax.rsqrt(var + EPS)
            return y * w[None, None, :]

        def _apply_rope(t, cos, sin):
            t1, t2 = jnp.split(t, 2, axis=-1)
            rot = jnp.concatenate([-t2, t1], axis=-1)
            return t * cos + rot * sin

        def _attn(q, k, v, mask):
            scale = 1.0 / np.sqrt(HD)
            s = jnp.einsum('bqhd,bkhd->bhqk', q, k) * scale
            s = jnp.where(mask, s, jnp.finfo(s.dtype).min)
            a = jax.nn.softmax(s, axis=-1)
            return jnp.einsum('bhqk,bkhd->bqhd', a, v)
        key = jax.random.key(seed)
        ks = jax.random.split(key, 16)
        w = lambda k, shp: jax.random.normal(k, shp, jnp.float32) * 0.02
        inp = {'x': jax.random.normal(ks[0], (B, 2 * N, D), jnp.float32), 'cond_global': jax.random.normal(ks[1], (B, D), jnp.float32), 'cond_tokens': jax.random.normal(ks[2], (B, LC, D), jnp.float32), 'adaLN_W': w(ks[3], (D, 9 * D)), 'adaLN_b': w(ks[4], (9 * D,)), 'norm1_w': jnp.ones((D,), jnp.float32), 'qkv_W': w(ks[5], (D, 3 * D)), 'attn_out_W': w(ks[6], (D, D)), 'normc_w': jnp.ones((D,), jnp.float32), 'cq_W': w(ks[7], (D, D)), 'ck_W': w(ks[8], (D, D)), 'cv_W': w(ks[9], (D, D)), 'co_W': w(ks[10], (D, D)), 'norm2_w': jnp.ones((D,), jnp.float32), 'mlp_W1': w(ks[11], (D, 4 * D)), 'mlp_b1': w(ks[12], (4 * D,)), 'mlp_W2': w(ks[13], (4 * D, D)), 'mlp_b2': w(ks[14], (D,)), 'cond_kv_mask': jnp.ones((B, LC), bool), 'attn_mask': _block_diff_mask(N, BLOCK)}
        return inp
    _L0_xcond_all = _L0_xcond_setup()
    _L0_xcond_in = {k: v for k, v in _L0_xcond_all.items() if k in ('adaLN_W', 'adaLN_b', 'norm1_w', 'qkv_W', 'attn_out_W', 'normc_w', 'cq_W', 'ck_W', 'cv_W', 'co_W', 'norm2_w', 'mlp_W1', 'mlp_b1', 'mlp_W2', 'mlp_b2')}
    del _L0_xcond_all

    def _L1_xcond_setup():
        import jax, jax.numpy as jnp
        import numpy as np
        EPS = 1e-05

        def _ada_ln(x, c, W_ss, b_ss):
            mu = jnp.mean(x, axis=-1, keepdims=True)
            var = jnp.mean((x - mu) ** 2, axis=-1, keepdims=True)
            h = (x - mu) / jnp.sqrt(var + EPS)
            ss = jax.nn.silu(c) @ W_ss + b_ss
            scale, bias = jnp.split(ss, 2, axis=-1)
            return (1.0 + scale)[:, None, :] * h + bias[:, None, :]
        key = jax.random.key(seed)
        ks = jax.random.split(key, 12)
        B, Lq, Lkv, H = (8, 512, 128, 256)
        s = 0.02
        return {'x_q': jax.random.normal(ks[0], (B, Lq, H), jnp.float32), 'x_kv': jax.random.normal(ks[1], (B, Lkv, H), jnp.float32), 't_vec': jax.random.normal(ks[2], (B, H), jnp.float32), 'Wq': jax.random.normal(ks[3], (H, H), jnp.float32) * s, 'bq': jnp.zeros((H,), jnp.float32), 'Wkv': jax.random.normal(ks[4], (H, 2 * H), jnp.float32) * s, 'bkv': jnp.zeros((2 * H,), jnp.float32), 'Wp': jax.random.normal(ks[5], (H, H), jnp.float32) * s, 'bp': jnp.zeros((H,), jnp.float32), 'Wss_q': jax.random.normal(ks[6], (H, 2 * H), jnp.float32) * s, 'bss_q': jnp.zeros((2 * H,), jnp.float32), 'Wss_kv': jax.random.normal(ks[7], (H, 2 * H), jnp.float32) * s, 'bss_kv': jnp.zeros((2 * H,), jnp.float32)}
    _L1_xcond_all = _L1_xcond_setup()
    _L1_xcond_in = {k: v for k, v in _L1_xcond_all.items() if k in ('Wq', 'bq', 'Wkv', 'bkv', 'Wp', 'bp', 'Wss_q', 'bss_q', 'Wss_kv', 'bss_kv')}
    del _L1_xcond_all

    def _L2_xcond_setup():
        import jax, jax.numpy as jnp
        import numpy as np
        LN_EPS = 1e-06

        def _ln(x):
            mu = jnp.mean(x, axis=-1, keepdims=True)
            var = jnp.var(x, axis=-1, keepdims=True)
            return (x - mu) * jax.lax.rsqrt(var + LN_EPS)
        key = jax.random.key(seed)
        H, NH = (256, 16)
        B, N, S = (4, 256, 77)
        MLP = int(H * 4.0)
        ks = jax.random.split(key, 20)
        s = 1.0 / np.sqrt(H)
        return {'x': jax.random.normal(ks[0], (B, N, H), jnp.float32), 'c': jax.random.normal(ks[1], (B, H), jnp.float32), 'context': jax.random.normal(ks[2], (B, S, H), jnp.float32), 'W_mod': jax.random.normal(ks[3], (H, 6 * H), jnp.float32) * s, 'b_mod': jnp.zeros((6 * H,), jnp.float32), 'W_qkv': jax.random.normal(ks[4], (H, 3 * H), jnp.float32) * s, 'b_qkv': jnp.zeros((3 * H,), jnp.float32), 'W_proj': jax.random.normal(ks[5], (H, H), jnp.float32) * s, 'b_proj': jnp.zeros((H,), jnp.float32), 'W_qc': jax.random.normal(ks[6], (H, H), jnp.float32) * s, 'b_qc': jnp.zeros((H,), jnp.float32), 'W_kvc': jax.random.normal(ks[7], (H, 2 * H), jnp.float32) * s, 'b_kvc': jnp.zeros((2 * H,), jnp.float32), 'W_cproj': jax.random.normal(ks[8], (H, H), jnp.float32) * s, 'b_cproj': jnp.zeros((H,), jnp.float32), 'W_mlp1': jax.random.normal(ks[9], (H, MLP), jnp.float32) * s, 'b_mlp1': jnp.zeros((MLP,), jnp.float32), 'W_mlp2': jax.random.normal(ks[10], (MLP, H), jnp.float32) * (1.0 / np.sqrt(MLP)), 'b_mlp2': jnp.zeros((H,), jnp.float32)}
    _L2_xcond_all = _L2_xcond_setup()
    _L2_xcond_in = {k: v for k, v in _L2_xcond_all.items() if k in ('W_mod', 'b_mod', 'W_qkv', 'b_qkv', 'W_proj', 'b_proj', 'W_qc', 'b_qc', 'W_kvc', 'b_kvc', 'W_cproj', 'b_cproj', 'W_mlp1', 'b_mlp1', 'W_mlp2', 'b_mlp2')}
    del _L2_xcond_all

    def _L3_xcond_setup():
        import jax, jax.numpy as jnp
        import numpy as np
        import math
        D_MODEL = 256
        N_HEADS = 16
        HEAD_DIM = D_MODEL // N_HEADS
        D_FF = 1024
        EPS = 1e-05
        ROPE_BASE = 10000.0

        def _rope(t):
            L, Dh = (t.shape[1], t.shape[-1])
            half = Dh // 2
            inv_freq = 1.0 / ROPE_BASE ** (jnp.arange(half, dtype=t.dtype) / half)
            ang = jnp.arange(L, dtype=t.dtype)[:, None] * inv_freq[None, :]
            cos = jnp.cos(ang)[None, :, None, :]
            sin = jnp.sin(ang)[None, :, None, :]
            t1, t2 = (t[..., :half], t[..., half:])
            return jnp.concatenate([t1 * cos - t2 * sin, t2 * cos + t1 * sin], axis=-1)

        def _adaln(x, emb, w, b):
            e = emb[:, 0, :]
            gb = e @ w.T + b
            gamma, beta = jnp.split(gb, 2, axis=-1)
            mu = x.mean(-1, keepdims=True)
            var = x.var(-1, keepdims=True)
            xn = (x - mu) * jax.lax.rsqrt(var + EPS)
            return xn * (1.0 + gamma[:, None, :]) + beta[:, None, :]

        def _attn(q, k, v):
            scale = 1.0 / math.sqrt(HEAD_DIM)
            scores = jnp.einsum('bqhd,bkhd->bhqk', q, k) * scale
            w = jax.nn.softmax(scores, axis=-1)
            out = jnp.einsum('bhqk,bkhd->bqhd', w, v)
            B, Lq = (out.shape[0], out.shape[1])
            return out.reshape(B, Lq, D_MODEL)
        key = jax.random.key(seed)
        ks = jax.random.split(key, 24)
        s = 0.02
        inp = {'x': jax.random.normal(ks[0], (2, 512, D_MODEL), jnp.float32), 'noise_emb': jax.random.normal(ks[1], (2, 1, D_MODEL), jnp.float32), 'context': jax.random.normal(ks[2], (2, 256, D_MODEL), jnp.float32), 'ln1_w': jax.random.normal(ks[3], (2 * D_MODEL, D_MODEL), jnp.float32) * s, 'ln1_b': jax.random.normal(ks[4], (2 * D_MODEL,), jnp.float32) * s, 'ln2_w': jax.random.normal(ks[5], (2 * D_MODEL, D_MODEL), jnp.float32) * s, 'ln2_b': jax.random.normal(ks[6], (2 * D_MODEL,), jnp.float32) * s, 'ln3_w': jax.random.normal(ks[7], (2 * D_MODEL, D_MODEL), jnp.float32) * s, 'ln3_b': jax.random.normal(ks[8], (2 * D_MODEL,), jnp.float32) * s, 'qkv_w': jax.random.normal(ks[9], (3 * D_MODEL, D_MODEL), jnp.float32) * s, 'sa_out_w': jax.random.normal(ks[10], (D_MODEL, D_MODEL), jnp.float32) * s, 'q_w': jax.random.normal(ks[11], (D_MODEL, D_MODEL), jnp.float32) * s, 'k_w': jax.random.normal(ks[12], (D_MODEL, D_MODEL), jnp.float32) * s, 'v_w': jax.random.normal(ks[13], (D_MODEL, D_MODEL), jnp.float32) * s, 'ca_out_w': jax.random.normal(ks[14], (D_MODEL, D_MODEL), jnp.float32) * s, 'ffn_w1': jax.random.normal(ks[15], (D_FF, D_MODEL), jnp.float32) * s, 'ffn_b1': jax.random.normal(ks[16], (D_FF,), jnp.float32) * s, 'ffn_w2': jax.random.normal(ks[17], (D_MODEL, D_FF), jnp.float32) * s, 'ffn_b2': jax.random.normal(ks[18], (D_MODEL,), jnp.float32) * s}
        return inp
    _L3_xcond_all = _L3_xcond_setup()
    _L3_xcond_in = {k: v for k, v in _L3_xcond_all.items() if k in ('ln1_w', 'ln1_b', 'ln2_w', 'ln2_b', 'ln3_w', 'ln3_b', 'qkv_w', 'sa_out_w', 'q_w', 'k_w', 'v_w', 'ca_out_w', 'ffn_w1', 'ffn_b1', 'ffn_w2', 'ffn_b2')}
    del _L3_xcond_all
    return {'x': x, 'cond_1024': cond_1024, 'ctx_1024': ctx_1024, 'mask_BxS2_bf1': mask_BxS2_bf1, 'mask_SxS_bk0': mask_SxS_bk0, 'L0_xcond_adaLN_W': _L0_xcond_in['adaLN_W'], 'L0_xcond_adaLN_b': _L0_xcond_in['adaLN_b'], 'L0_xcond_norm1_w': _L0_xcond_in['norm1_w'], 'L0_xcond_qkv_W': _L0_xcond_in['qkv_W'], 'L0_xcond_attn_out_W': _L0_xcond_in['attn_out_W'], 'L0_xcond_normc_w': _L0_xcond_in['normc_w'], 'L0_xcond_cq_W': _L0_xcond_in['cq_W'], 'L0_xcond_ck_W': _L0_xcond_in['ck_W'], 'L0_xcond_cv_W': _L0_xcond_in['cv_W'], 'L0_xcond_co_W': _L0_xcond_in['co_W'], 'L0_xcond_norm2_w': _L0_xcond_in['norm2_w'], 'L0_xcond_mlp_W1': _L0_xcond_in['mlp_W1'], 'L0_xcond_mlp_b1': _L0_xcond_in['mlp_b1'], 'L0_xcond_mlp_W2': _L0_xcond_in['mlp_W2'], 'L0_xcond_mlp_b2': _L0_xcond_in['mlp_b2'], 'L1_xcond_Wq': _L1_xcond_in['Wq'], 'L1_xcond_bq': _L1_xcond_in['bq'], 'L1_xcond_Wkv': _L1_xcond_in['Wkv'], 'L1_xcond_bkv': _L1_xcond_in['bkv'], 'L1_xcond_Wp': _L1_xcond_in['Wp'], 'L1_xcond_bp': _L1_xcond_in['bp'], 'L1_xcond_Wss_q': _L1_xcond_in['Wss_q'], 'L1_xcond_bss_q': _L1_xcond_in['bss_q'], 'L1_xcond_Wss_kv': _L1_xcond_in['Wss_kv'], 'L1_xcond_bss_kv': _L1_xcond_in['bss_kv'], 'L2_xcond_W_mod': _L2_xcond_in['W_mod'], 'L2_xcond_b_mod': _L2_xcond_in['b_mod'], 'L2_xcond_W_qkv': _L2_xcond_in['W_qkv'], 'L2_xcond_b_qkv': _L2_xcond_in['b_qkv'], 'L2_xcond_W_proj': _L2_xcond_in['W_proj'], 'L2_xcond_b_proj': _L2_xcond_in['b_proj'], 'L2_xcond_W_qc': _L2_xcond_in['W_qc'], 'L2_xcond_b_qc': _L2_xcond_in['b_qc'], 'L2_xcond_W_kvc': _L2_xcond_in['W_kvc'], 'L2_xcond_b_kvc': _L2_xcond_in['b_kvc'], 'L2_xcond_W_cproj': _L2_xcond_in['W_cproj'], 'L2_xcond_b_cproj': _L2_xcond_in['b_cproj'], 'L2_xcond_W_mlp1': _L2_xcond_in['W_mlp1'], 'L2_xcond_b_mlp1': _L2_xcond_in['b_mlp1'], 'L2_xcond_W_mlp2': _L2_xcond_in['W_mlp2'], 'L2_xcond_b_mlp2': _L2_xcond_in['b_mlp2'], 'L3_xcond_ln1_w': _L3_xcond_in['ln1_w'], 'L3_xcond_ln1_b': _L3_xcond_in['ln1_b'], 'L3_xcond_ln2_w': _L3_xcond_in['ln2_w'], 'L3_xcond_ln2_b': _L3_xcond_in['ln2_b'], 'L3_xcond_ln3_w': _L3_xcond_in['ln3_w'], 'L3_xcond_ln3_b': _L3_xcond_in['ln3_b'], 'L3_xcond_qkv_w': _L3_xcond_in['qkv_w'], 'L3_xcond_sa_out_w': _L3_xcond_in['sa_out_w'], 'L3_xcond_q_w': _L3_xcond_in['q_w'], 'L3_xcond_k_w': _L3_xcond_in['k_w'], 'L3_xcond_v_w': _L3_xcond_in['v_w'], 'L3_xcond_ca_out_w': _L3_xcond_in['ca_out_w'], 'L3_xcond_ffn_w1': _L3_xcond_in['ffn_w1'], 'L3_xcond_ffn_b1': _L3_xcond_in['ffn_b1'], 'L3_xcond_ffn_w2': _L3_xcond_in['ffn_w2'], 'L3_xcond_ffn_b2': _L3_xcond_in['ffn_b2']}

def reference(x, cond_1024, ctx_1024, mask_BxS2_bf1, mask_SxS_bk0, L0_xcond_adaLN_W, L0_xcond_adaLN_b, L0_xcond_norm1_w, L0_xcond_qkv_W, L0_xcond_attn_out_W, L0_xcond_normc_w, L0_xcond_cq_W, L0_xcond_ck_W, L0_xcond_cv_W, L0_xcond_co_W, L0_xcond_norm2_w, L0_xcond_mlp_W1, L0_xcond_mlp_b1, L0_xcond_mlp_W2, L0_xcond_mlp_b2, L1_xcond_Wq, L1_xcond_bq, L1_xcond_Wkv, L1_xcond_bkv, L1_xcond_Wp, L1_xcond_bp, L1_xcond_Wss_q, L1_xcond_bss_q, L1_xcond_Wss_kv, L1_xcond_bss_kv, L2_xcond_W_mod, L2_xcond_b_mod, L2_xcond_W_qkv, L2_xcond_b_qkv, L2_xcond_W_proj, L2_xcond_b_proj, L2_xcond_W_qc, L2_xcond_b_qc, L2_xcond_W_kvc, L2_xcond_b_kvc, L2_xcond_W_cproj, L2_xcond_b_cproj, L2_xcond_W_mlp1, L2_xcond_b_mlp1, L2_xcond_W_mlp2, L2_xcond_b_mlp2, L3_xcond_ln1_w, L3_xcond_ln1_b, L3_xcond_ln2_w, L3_xcond_ln2_b, L3_xcond_ln3_w, L3_xcond_ln3_b, L3_xcond_qkv_w, L3_xcond_sa_out_w, L3_xcond_q_w, L3_xcond_k_w, L3_xcond_v_w, L3_xcond_ca_out_w, L3_xcond_ffn_w1, L3_xcond_ffn_b1, L3_xcond_ffn_w2, L3_xcond_ffn_b2):
    import jax
    import jax.numpy as jnp

    def _L0_xcond_ref(x, cond_global, cond_tokens, adaLN_W, adaLN_b, norm1_w, qkv_W, attn_out_W, normc_w, cq_W, ck_W, cv_W, co_W, norm2_w, mlp_W1, mlp_b1, mlp_W2, mlp_b2, cond_kv_mask, attn_mask):
        import jax, jax.numpy as jnp
        import numpy as np
        B, N, D, H, LC = (2, 256, 256, 16, 77)
        HD = D // H
        BLOCK = 16
        ROPE_BASE = 10000.0
        EPS = 1e-05

        def _block_diff_mask(n, block_size):
            idx = np.arange(2 * n)
            q = idx[:, None]
            kv = idx[None, :]
            fq = q >= n
            fkv = kv >= n
            bq = np.where(fq, (q - n) // block_size, q // block_size)
            bkv = np.where(fkv, (kv - n) // block_size, kv // block_size)
            block_diagonal = (bq == bkv) & (fq == fkv)
            offset_block_causal = (bq > bkv) & fkv & ~fq
            block_causal = (bq >= bkv) & fq & fkv
            return jnp.asarray(block_diagonal | offset_block_causal | block_causal)

        def _rope_tables(n):
            inv_freq = 1.0 / ROPE_BASE ** (np.arange(0, HD, 2, dtype=np.float32) / HD)
            freqs = np.outer(np.arange(n, dtype=np.float32), inv_freq)
            emb = np.concatenate([freqs, freqs], axis=-1)
            cos = jnp.asarray(np.cos(emb), jnp.float32)[None, :, None, :]
            sin = jnp.asarray(np.sin(emb), jnp.float32)[None, :, None, :]
            return (cos, sin)

        def _ln(x, w):
            xf = x.astype(jnp.float32)
            mu = jnp.mean(xf, axis=-1, keepdims=True)
            var = jnp.mean(jnp.square(xf - mu), axis=-1, keepdims=True)
            y = (xf - mu) * jax.lax.rsqrt(var + EPS)
            return y * w[None, None, :]

        def _apply_rope(t, cos, sin):
            t1, t2 = jnp.split(t, 2, axis=-1)
            rot = jnp.concatenate([-t2, t1], axis=-1)
            return t * cos + rot * sin

        def _attn(q, k, v, mask):
            scale = 1.0 / np.sqrt(HD)
            s = jnp.einsum('bqhd,bkhd->bhqk', q, k) * scale
            s = jnp.where(mask, s, jnp.finfo(s.dtype).min)
            a = jax.nn.softmax(s, axis=-1)
            return jnp.einsum('bhqk,bkhd->bqhd', a, v)
        b, s, d = x.shape
        n = s // 2
        mod = (cond_global @ adaLN_W + adaLN_b)[:, None, :]
        sh_msa, sc_msa, g_msa, sh_x, sc_x, g_x, sh_mlp, sc_mlp, g_mlp = jnp.split(mod, 9, axis=-1)
        x_norm = _ln(x, norm1_w) * (1 + sc_msa) + sh_msa
        cos, sin = _rope_tables(n)

        def qkv(h):
            t = (h @ qkv_W).reshape(b, n, 3, H, HD)
            q, k, v = (t[:, :, 0], t[:, :, 1], t[:, :, 2])
            return (_apply_rope(q, cos, sin), _apply_rope(k, cos, sin), v)
        q1, k1, v1 = qkv(x_norm[:, :n])
        q2, k2, v2 = qkv(x_norm[:, n:])
        q = jnp.concatenate([q1, q2], axis=1)
        k = jnp.concatenate([k1, k2], axis=1)
        v = jnp.concatenate([v1, v2], axis=1)
        self_out = _attn(q, k, v, attn_mask[None, None]).reshape(b, s, d) @ attn_out_W
        x = x + g_msa * self_out
        xc = _ln(x, normc_w) * (1 + sc_x) + sh_x
        qc = (xc @ cq_W).reshape(b, s, H, HD)
        kc = (cond_tokens @ ck_W).reshape(b, LC, H, HD)
        vc = (cond_tokens @ cv_W).reshape(b, LC, H, HD)
        cross = _attn(qc, kc, vc, cond_kv_mask[:, None, None, :]).reshape(b, s, d) @ co_W
        x = x + g_x * cross
        xm = _ln(x, norm2_w) * (1 + sc_mlp) + sh_mlp
        h = jax.nn.gelu(xm @ mlp_W1 + mlp_b1, approximate=True)
        mlp_out = h @ mlp_W2 + mlp_b2
        return x + g_mlp * mlp_out

    def _L1_xcond_ref(x_q, x_kv, t_vec, Wq, bq, Wkv, bkv, Wp, bp, Wss_q, bss_q, Wss_kv, bss_kv):
        import jax, jax.numpy as jnp
        import numpy as np
        EPS = 1e-05

        def _ada_ln(x, c, W_ss, b_ss):
            mu = jnp.mean(x, axis=-1, keepdims=True)
            var = jnp.mean((x - mu) ** 2, axis=-1, keepdims=True)
            h = (x - mu) / jnp.sqrt(var + EPS)
            ss = jax.nn.silu(c) @ W_ss + b_ss
            scale, bias = jnp.split(ss, 2, axis=-1)
            return (1.0 + scale)[:, None, :] * h + bias[:, None, :]
        B, Lq, H = x_q.shape
        Lkv = x_kv.shape[1]
        nh = 16
        dh = H // nh
        xq = _ada_ln(x_q, t_vec, Wss_q, bss_q)
        xkv = _ada_ln(x_kv, t_vec, Wss_kv, bss_kv)
        q = (xq @ Wq + bq).reshape(B, Lq, nh, dh)
        kv = (xkv @ Wkv + bkv).reshape(B, Lkv, 2, nh, dh)
        k = kv[:, :, 0]
        v = kv[:, :, 1]
        scores = jnp.einsum('bqhd,bkhd->bhqk', q, k) / jnp.sqrt(jnp.float32(dh))
        attn = jax.nn.softmax(scores, axis=-1)
        out = jnp.einsum('bhqk,bkhd->bqhd', attn, v).reshape(B, Lq, H)
        return x_q + (out @ Wp + bp)

    def _L2_xcond_ref(x, c, context, W_mod, b_mod, W_qkv, b_qkv, W_proj, b_proj, W_qc, b_qc, W_kvc, b_kvc, W_cproj, b_cproj, W_mlp1, b_mlp1, W_mlp2, b_mlp2):
        import jax, jax.numpy as jnp
        import numpy as np
        LN_EPS = 1e-06

        def _ln(x):
            mu = jnp.mean(x, axis=-1, keepdims=True)
            var = jnp.var(x, axis=-1, keepdims=True)
            return (x - mu) * jax.lax.rsqrt(var + LN_EPS)
        B, N, H = x.shape
        NH = 16
        hd = H // NH
        scale = hd ** (-0.5)
        c_proj = jax.nn.silu(c) @ W_mod + b_mod
        shift_a, scale_a, gate_a, shift_m, scale_m, gate_m = jnp.split(c_proj, 6, axis=-1)

        def modulate(t, shift, sc):
            return t * (1 + sc[:, None]) + shift[:, None]
        x_norm = modulate(_ln(x), shift_a, scale_a)
        qkv = x_norm @ W_qkv + b_qkv
        q, k, v = jnp.split(qkv, 3, axis=-1)
        q = q.reshape(B, N, NH, hd).transpose(0, 2, 1, 3)
        k = k.reshape(B, N, NH, hd).transpose(0, 2, 1, 3)
        v = v.reshape(B, N, NH, hd).transpose(0, 2, 1, 3)
        attn_w = jax.nn.softmax(jnp.einsum('bhqd,bhkd->bhqk', q, k) * scale, axis=-1)
        attn_out = jnp.einsum('bhqk,bhkd->bhqd', attn_w, v)
        attn_out = attn_out.transpose(0, 2, 1, 3).reshape(B, N, H)
        attn_out = attn_out @ W_proj + b_proj
        x = x + gate_a[:, None] * attn_out
        S = context.shape[1]
        q_c = _ln(x) @ W_qc + b_qc
        kv_c = _ln(context) @ W_kvc + b_kvc
        k_c, v_c = jnp.split(kv_c, 2, axis=-1)
        q_c = q_c.reshape(B, N, NH, hd).transpose(0, 2, 1, 3)
        k_c = k_c.reshape(B, S, NH, hd).transpose(0, 2, 1, 3)
        v_c = v_c.reshape(B, S, NH, hd).transpose(0, 2, 1, 3)
        c_attn_w = jax.nn.softmax(jnp.einsum('bhqd,bhsd->bhqs', q_c, k_c) * scale, axis=-1)
        c_attn_out = jnp.einsum('bhqs,bhsd->bhqd', c_attn_w, v_c)
        c_attn_out = c_attn_out.transpose(0, 2, 1, 3).reshape(B, N, H)
        c_attn_out = c_attn_out @ W_cproj + b_cproj
        x = x + c_attn_out
        x_norm2 = modulate(_ln(x), shift_m, scale_m)
        h = jax.nn.gelu(x_norm2 @ W_mlp1 + b_mlp1)
        h = h @ W_mlp2 + b_mlp2
        x = x + gate_m[:, None] * h
        return x

    def _L3_xcond_ref(x, noise_emb, context, ln1_w, ln1_b, ln2_w, ln2_b, ln3_w, ln3_b, qkv_w, sa_out_w, q_w, k_w, v_w, ca_out_w, ffn_w1, ffn_b1, ffn_w2, ffn_b2):
        import jax, jax.numpy as jnp
        import numpy as np
        import math
        D_MODEL = 256
        N_HEADS = 16
        HEAD_DIM = D_MODEL // N_HEADS
        D_FF = 1024
        EPS = 1e-05
        ROPE_BASE = 10000.0

        def _rope(t):
            L, Dh = (t.shape[1], t.shape[-1])
            half = Dh // 2
            inv_freq = 1.0 / ROPE_BASE ** (jnp.arange(half, dtype=t.dtype) / half)
            ang = jnp.arange(L, dtype=t.dtype)[:, None] * inv_freq[None, :]
            cos = jnp.cos(ang)[None, :, None, :]
            sin = jnp.sin(ang)[None, :, None, :]
            t1, t2 = (t[..., :half], t[..., half:])
            return jnp.concatenate([t1 * cos - t2 * sin, t2 * cos + t1 * sin], axis=-1)

        def _adaln(x, emb, w, b):
            e = emb[:, 0, :]
            gb = e @ w.T + b
            gamma, beta = jnp.split(gb, 2, axis=-1)
            mu = x.mean(-1, keepdims=True)
            var = x.var(-1, keepdims=True)
            xn = (x - mu) * jax.lax.rsqrt(var + EPS)
            return xn * (1.0 + gamma[:, None, :]) + beta[:, None, :]

        def _attn(q, k, v):
            scale = 1.0 / math.sqrt(HEAD_DIM)
            scores = jnp.einsum('bqhd,bkhd->bhqk', q, k) * scale
            w = jax.nn.softmax(scores, axis=-1)
            out = jnp.einsum('bhqk,bkhd->bqhd', w, v)
            B, Lq = (out.shape[0], out.shape[1])
            return out.reshape(B, Lq, D_MODEL)
        B, L, D = x.shape
        L_ctx = context.shape[1]
        res = x
        xn = _adaln(x, noise_emb, ln1_w, ln1_b)
        qkv = xn @ qkv_w.T
        q, k, v = jnp.split(qkv, 3, axis=-1)
        q = _rope(q.reshape(B, L, N_HEADS, HEAD_DIM))
        k = _rope(k.reshape(B, L, N_HEADS, HEAD_DIM))
        v = v.reshape(B, L, N_HEADS, HEAD_DIM)
        sa = _attn(q, k, v) @ sa_out_w.T
        x = res + sa
        res = x
        xn = _adaln(x, noise_emb, ln2_w, ln2_b)
        q = _rope((xn @ q_w.T).reshape(B, L, N_HEADS, HEAD_DIM))
        k = _rope((context @ k_w.T).reshape(B, L_ctx, N_HEADS, HEAD_DIM))
        v = (context @ v_w.T).reshape(B, L_ctx, N_HEADS, HEAD_DIM)
        ca = _attn(q, k, v) @ ca_out_w.T
        x = res + ca
        res = x
        xn = _adaln(x, noise_emb, ln3_w, ln3_b)
        h = jax.nn.gelu(xn @ ffn_w1.T + ffn_b1, approximate=False)
        x = res + (h @ ffn_w2.T + ffn_b2)
        return x
    x = _L0_xcond_ref(x, cond_1024, ctx_1024, L0_xcond_adaLN_W, L0_xcond_adaLN_b, L0_xcond_norm1_w, L0_xcond_qkv_W, L0_xcond_attn_out_W, L0_xcond_normc_w, L0_xcond_cq_W, L0_xcond_ck_W, L0_xcond_cv_W, L0_xcond_co_W, L0_xcond_norm2_w, L0_xcond_mlp_W1, L0_xcond_mlp_b1, L0_xcond_mlp_W2, L0_xcond_mlp_b2, mask_BxS2_bf1, mask_SxS_bk0)
    x = _L1_xcond_ref(x, ctx_1024, cond_1024, L1_xcond_Wq, L1_xcond_bq, L1_xcond_Wkv, L1_xcond_bkv, L1_xcond_Wp, L1_xcond_bp, L1_xcond_Wss_q, L1_xcond_bss_q, L1_xcond_Wss_kv, L1_xcond_bss_kv)
    x = _L2_xcond_ref(x, cond_1024, ctx_1024, L2_xcond_W_mod, L2_xcond_b_mod, L2_xcond_W_qkv, L2_xcond_b_qkv, L2_xcond_W_proj, L2_xcond_b_proj, L2_xcond_W_qc, L2_xcond_b_qc, L2_xcond_W_kvc, L2_xcond_b_kvc, L2_xcond_W_cproj, L2_xcond_b_cproj, L2_xcond_W_mlp1, L2_xcond_b_mlp1, L2_xcond_W_mlp2, L2_xcond_b_mlp2)
    x = _L3_xcond_ref(x, cond_1024[:, None, :], ctx_1024, L3_xcond_ln1_w, L3_xcond_ln1_b, L3_xcond_ln2_w, L3_xcond_ln2_b, L3_xcond_ln3_w, L3_xcond_ln3_b, L3_xcond_qkv_w, L3_xcond_sa_out_w, L3_xcond_q_w, L3_xcond_k_w, L3_xcond_v_w, L3_xcond_ca_out_w, L3_xcond_ffn_w1, L3_xcond_ffn_b1, L3_xcond_ffn_w2, L3_xcond_ffn_b2)
    return x

_drawn_inputs = setup_inputs


def setup_inputs(seed=0):
    import zlib

    import numpy as np

    out = dict(_drawn_inputs(seed))
    spreads = {'L0_xcond_norm1_w': (1.0, 0.6),
     'L0_xcond_normc_w': (1.0, 0.6),
     'L0_xcond_norm2_w': (1.0, 0.6),
     'L1_xcond_bq': (0.0, 2.0),
     'L1_xcond_bkv': (0.0, 0.317),
     'L1_xcond_bp': (0.0, 0.1),
     'L1_xcond_bss_q': (0.0, 2.0),
     'L1_xcond_bss_kv': (0.0, 0.729),
     'L2_xcond_b_mod': (0.0, 0.1),
     'L2_xcond_b_qkv': (0.0, 0.1),
     'L2_xcond_b_proj': (0.0, 0.1),
     'L2_xcond_b_qc': (0.0, 0.55),
     'L2_xcond_b_kvc': (0.0, 0.1),
     'L2_xcond_b_cproj': (0.0, 0.1),
     'L2_xcond_b_mlp1': (0.0, 0.288),
     'L2_xcond_b_mlp2': (0.0, 0.1)}
    factors = {'L0_xcond_adaLN_b': 8.0,
     'L0_xcond_qkv_W': 4.089,
     'L0_xcond_attn_out_W': 4.123,
     'L0_xcond_cq_W': 8.0,
     'L0_xcond_ck_W': 8.0,
     'L0_xcond_cv_W': 3.232,
     'L0_xcond_co_W': 3.109,
     'L0_xcond_mlp_b1': 29.027,
     'L0_xcond_mlp_b2': 8.0,
     'L1_xcond_Wq': 8.0,
     'L1_xcond_Wss_q': 8.0,
     'L3_xcond_ln1_b': 42.063,
     'L3_xcond_ln2_w': 8.0,
     'L3_xcond_ln2_b': 32.353,
     'L3_xcond_ln3_b': 28.667,
     'L3_xcond_q_w': 8.0,
     'L3_xcond_k_w': 8.0,
     'L3_xcond_ffn_b1': 8.0,
     'L3_xcond_ffn_b2': 3.908,
     'L1_xcond_Wss_kv': 2.699}
    for name, (base, spread) in spreads.items():
        noise = np.random.default_rng([zlib.crc32(name.encode()), seed]).standard_normal(out[name].shape)
        drawn = base * np.exp(spread * noise) if base else spread * noise
        out[name] = jnp.asarray(drawn.astype(out[name].dtype))
    for name, factor in factors.items():
        out[name] = (out[name] * factor).astype(out[name].dtype)
    return out
```

```python
from contextlib import ExitStack

import concourse.bass as bass
from concourse import mybir

F32 = mybir.dt.float32
F32R = mybir.dt.float32r
BF16 = mybir.dt.bfloat16
U8 = mybir.dt.uint8
ALU = mybir.AluOpType
ACT = mybir.ActivationFunctionType
AX_X = mybir.AxisListType.X

P = 128
B, S, D = 16, 256, 256
H, HD = 16, 16
CTX = 77
CTXP = CTX + 1
FF = 4 * D
TC = S // P
FC = D // P
FFC = FF // P
PAIRS = H // 2
SLOTS = 2
ITERS = B // SLOTS
SCALE = HD ** -0.5
MASKED = 2.0 ** 120
VW = HD + 1


class Block:

    def __init__(self, kind, mod=None, rope=False, mask=False, gate=None, qkv_bias=False, out_bias=False,
                 ctx=None, ctx_mod=None, gelu=None):
        self.kind, self.mod, self.rope, self.mask, self.gate = kind, mod, rope, mask, gate
        self.qkv_bias, self.out_bias, self.ctx, self.ctx_mod, self.gelu = qkv_bias, out_bias, ctx, ctx_mod, gelu


class Layer:
    def __init__(self, name, eps, rope_period, mod0, mods, gate0, gates, blocks):
        self.name, self.eps, self.rope_period, self.blocks = name, eps, rope_period, blocks
        self.mod0, self.mods, self.gate0, self.gates = mod0, mods, gate0, gates
        self.nb = len(blocks)
        self.attn = [k for k, b in enumerate(blocks) if b.kind != "mlp"]
        self.mlp = [k for k, b in enumerate(blocks) if b.kind == "mlp"]


LAYERS = [
    Layer("L0", 1e-5, P, 0, 3, 0, 3, [
        Block("self", mod=0, rope=True, mask=True, gate=0),
        Block("cross", mod=1, gate=1, mask=True, ctx="raw"),
        Block("mlp", mod=2, gate=2, out_bias=True, gelu="tanh")]),
    Layer("L1", 1e-5, None, 3, 2, None, 0, [
        Block("cross", mod=0, qkv_bias=True, out_bias=True, ctx="norm", ctx_mod=1)]),
    Layer("L2", 1e-6, None, 5, 2, 3, 2, [
        Block("self", mod=0, qkv_bias=True, out_bias=True, gate=0),
        Block("cross", qkv_bias=True, out_bias=True, ctx="norm"),
        Block("mlp", mod=1, gate=1, out_bias=True, gelu="tanh")]),
    Layer("L3", 1e-5, S, 7, 3, None, 0, [
        Block("self", mod=0, rope=True),
        Block("cross", mod=1, rope=True, ctx="raw"),
        Block("mlp", mod=2, out_bias=True, gelu="erf")]),
]
N_MOD = 10
N_GATE = 5


def score_uses(blk):
    return PAIRS if blk.kind == "self" else PAIRS // 2


def front_steps(blk):
    if blk.kind == "mlp":
        return [("ln", 0), ("nx", 0), ("xT", 0)]
    ctx = [("cn", 0), ("cT", 0)] if blk.kind == "cross" else []
    parts, k_fills = (3, 4) if blk.kind == "self" else (2, 2)
    return ([("ln", 0)] + ctx + [("nx", 0), ("xT", 0)] + [("qkv", j) for j in range(parts)] + [("stkQ", j) for j in range(4)]
            + [("stkK", j) for j in range(k_fills)] + [("S", u) for u in range(score_uses(blk))] + [("mx", 0), ("maxT", 0)])


def back_steps(blk):
    if blk.kind == "mlp":
        return [("up", j) for j in range(FFC // 2)] + [("down", 0)]
    out = []
    for u in range(score_uses(blk)):
        out += [("ST", u)] + ([("W", u - 1)] if u else [])
    return out + [("W", score_uses(blk) - 1), ("at", 0), ("atT", 0), ("out", 0)]


def merge(back, front):
    out, n = [], 0
    for i, step in enumerate(back):
        out.append(step)
        while n < len(front) and n * len(back) < (i + 1) * len(front):
            out.append(front[n])
            n += 1
    return out + front[n:]


def schedule(layer):
    def front(k, s):
        return [(k, s, *step) for step in front_steps(layer.blocks[k])]

    def back(k, s):
        return [(k, s, *step) for step in back_steps(layer.blocks[k])]

    out = front(0, 0)
    for k in range(layer.nb):
        out += merge(back(k, 0), front(k, 1))
        out += merge(back(k, 1), front(k + 1, 0) if k + 1 < layer.nb else [])
    return out


FROM_ONE = ("gen", "max0", "max1", "exp0", "exp1", "probs", "pv", "split")
GEN_STEPS = ("xT", "cT", "qkv", "stkQ", "stkK", "maxT", "atT", "out", "up", "down")


class Plan:

    def __init__(self, layer):
        self.layer, self.steps = layer, schedule(layer)
        self.gen = {}
        self.score = {}
        self.probs = {}
        self.pv = {}
        n_gen, n_probs, users, done = 0, 0, [], {(q, b): 0 for q in ("S", "ST") for b in range(2)}
        for step in self.steps:
            k, s, name, j = step
            if name in GEN_STEPS:
                self.gen[step] = (n_gen % 2, n_gen // 2)
                n_gen += 1
            if name in ("S", "ST"):
                b = len(users) % 2
                before = users[-2] if len(users) > 1 else "ST"
                self.score[step] = (b, done["S", b], done["ST", b], before)
                done[name, b] += 1
                users.append(name)
            if name == "ST":
                self.probs[step] = (n_probs % 2, n_probs // 2)
                n_probs += 1
                if j == 0:
                    self.pv[(k, s)] = len(self.pv)
        assert n_gen % 2 == 0 and len(users) % 2 == 0 and n_probs % 2 == 0 and users[-2:] == ["ST", "ST"]
        links = sum(links_of(layer, b) for b in layer.blocks) * SLOTS
        self.count = {"gen": n_gen // 2, "max0": done["S", 0], "max1": done["S", 1], "exp0": done["ST", 0], "exp1": done["ST", 1],
                      "score": len(users) // 2, "probs": n_probs // 2, "pv": len(self.pv), "link": links, "block": layer.nb,
                      "attn": len(layer.attn), "split": 2 * len(layer.attn), "cnorm": sum(b.ctx == "norm" for b in layer.blocks),
                      "copies": 3 if layer.name == "L0" else 1, "gated": sum(b.gate is not None and b.out_bias for b in layer.blocks)}


def links_of(layer, blk):
    n = 2
    if blk.kind == "mlp":
        return n
    parts = 2
    n += parts * ((1 if blk.rope else 0) + 1)
    if blk.rope and blk.kind == "cross":
        n += 1
    if blk.ctx == "norm":
        n += 2
    return n + 1 + 1


def dit_stack(nc, a):
    plans = [Plan(layer) for layer in LAYERS]

    base, total = [], {key: 0 for key in plans[0].count}
    for plan in plans:
        base.append(dict(total))
        for key in total:
            total[key] += ITERS * plan.count[key]

    keep = ExitStack()
    with keep:
        def sb(name, shape, dt=F32, stack=keep):
            return stack.enter_context(nc.sbuf_tensor(name, shape, dt))

        def sem(name):
            return keep.enter_context(nc.semaphore(name))

        score = [keep.enter_context(nc.psum_tensor(f"score{b}", [P, 2, 512], F32)) for b in range(2)]
        pv = keep.enter_context(nc.psum_tensor("pv", [P, TC, 512], F32))
        gen = [keep.enter_context(nc.psum_tensor(f"gen{b}", [P, 512], F32)) for b in range(2)]

        ident = sb("ident", [P, P])
        ident_bf = sb("ident_bf", [P, P], BF16)
        ones_bf = sb("ones_bf", [1, P], BF16)
        minus_half = sb("minus_half", [P, TC])
        cos_t = sb("cos_t", [P, TC, HD])
        sin_t = sb("sin_t", [P, TC, HD])
        mod_all = sb("mod_all", [P, B, N_MOD * 2 * FC])
        maskq = sb("maskq", [P, TC, 2, S], BF16)
        maskk = sb("maskk", [P, TC, S], BF16)
        kbias_row = sb("kbias_row", [1, B, CTX], BF16)
        kbias_col = sb("kbias_col", [CTX, B])
        gates_dram = nc.dram_tensor("gates_scratch", (B, N_GATE * D), F32, kind="Internal").ap()
        x_dram = nc.dram_tensor("x_scratch", (B, S, D), F32, kind="Internal").ap()

        const_loaded = sem("const_loaded")
        adaln_loaded = sem("adaln_loaded")
        silu_exp_done = sem("silu_exp_done")
        cond_ready = sem("cond_ready")
        pro_link = sem("pro_link")
        mod_sum_done = sem("mod_sum_done")
        gate_sum_done = sem("gate_sum_done")
        gates_ready = sem("gates_ready")
        gates_stored = sem("gates_stored")

        with ExitStack() as pro:
            condT = sb("condT", [P, FC, B], F32, pro)
            siluT = sb("siluT", [P, FC, B], F32, pro)
            expT = sb("expT", [P, FC, B], F32, pro)
            ada = {"L0": sb("ada0", [P, FC, 9 * D], F32, pro), "L1q": sb("ada1q", [P, FC, 2 * D], F32, pro),
                   "L1kv": sb("ada1kv", [P, FC, 2 * D], F32, pro), "L2": sb("ada2", [P, FC, 6 * D], F32, pro),
                   "L3a": sb("ada3a", [P, FC, 2 * D], F32, pro), "L3b": sb("ada3b", [P, FC, 2 * D], F32, pro),
                   "L3c": sb("ada3c", [P, FC, 2 * D], F32, pro)}
            mod_bias = sb("mod_bias", [P, N_MOD * 2 * FC], F32, pro)
            norm_w = sb("norm_w", [P, 3, FC], F32, pro)
            gate_bias = sb("gate_bias", [1, N_GATE * D], F32, pro)
            ones16 = sb("ones16", [1, B], F32, pro)
            gates = sb("gates", [B, N_GATE * D], F32, pro)
            mask_u8 = sb("mask_u8", [P, TC, S], U8, pro)
            maskT_u8 = sb("maskT_u8", [P, TC, S], U8, pro)
            krow_u8 = sb("krow_u8", [1, B, CTX], U8, pro)
            kcol_u8 = sb("kcol_u8", [CTX, B], U8, pro)

            mod_src = [("L0", D, 0, False), ("L0", 4 * D, 3 * D, False), ("L0", 7 * D, 6 * D, False),
                       ("L1q", 0, D, True), ("L1kv", 0, D, True),
                       ("L2", D, 0, True), ("L2", 4 * D, 3 * D, True),
                       ("L3a", 0, D, False), ("L3b", 0, D, False), ("L3c", 0, D, False)]
            gate_src = [("L0", 2 * D, False), ("L0", 5 * D, False), ("L0", 8 * D, False),
                        ("L2", 2 * D, True), ("L2", 5 * D, True)]
            const_loads = [(ident[:, :], a["ident"]), (cos_t[:, :, :], a["cos"]), (sin_t[:, :, :], a["sin"]),
                           (condT[:, :, :], a["condT"].rearrange("(c p) b -> p c b", p=P)),
                           (mod_bias[:, :], a["mod_bias"]), (norm_w[:, :, :], a["norm_w"]),
                           (gate_bias[:, :], a["gate_bias"]),
                           (mask_u8[:, :, :], a["mask"].rearrange("(c p) k -> p c k", p=P)),
                           (maskT_u8[:, :, :], a["maskT"].rearrange("(c p) k -> p c k", p=P)),
                           (krow_u8[:, :, :], a["kmask"].rearrange("(o b) k -> o b k", o=1)),
                           (kcol_u8[:, :], a["kmaskT"])]
            ada_loads = [("L0", "adaln0"), ("L1q", "adaln1q"), ("L1kv", "adaln1kv"), ("L2", "adaln2"),
                         ("L3a", "adaln3a"), ("L3b", "adaln3b"), ("L3c", "adaln3c")]

            with nc.Block() as block:
                @block.sync
                def _(sp):
                    for dst, src in const_loads:
                        sp.dma_start(dst, src).then_inc(const_loaded, 16)
                    for key, name in ada_loads:
                        sp.dma_start(ada[key][:, :, :], a[name].rearrange("(c p) n -> p c n", p=P)).then_inc(adaln_loaded, 16)
                    sp.wait_ge(gates_ready, 3)
                    sp.dma_start(gates_dram, gates[:, :]).then_inc(gates_stored, 16)
                    sp.wait_ge(gates_stored, 16)

                @block.scalar
                def _(act):
                    act.wait_ge(const_loaded, 16 * len(const_loads))
                    act.activation(expT[:, :, :], condT[:, :, :], ACT.Exp, scale=-1.0).then_inc(silu_exp_done, 1)

                @block.vector
                def _(dve):
                    links = [0]

                    def link(ins):
                        links[0] += 1
                        ins.then_inc(pro_link, 1)
                        dve.wait_ge(pro_link, links[0])

                    dve.memset(ones_bf[:, :], 1.0)
                    dve.memset(minus_half[:, :], -0.5)
                    dve.memset(ones16[:, :], 1.0)
                    dve.wait_ge(const_loaded, 16 * len(const_loads))
                    dve.wait_ge(silu_exp_done, 1)
                    link(dve.tensor_scalar(expT[:, :, :], expT[:, :, :], 1.0, None, ALU.add))
                    link(dve.reciprocal(siluT[:, :, :], expT[:, :, :]))
                    dve.tensor_tensor(siluT[:, :, :], siluT[:, :, :], condT[:, :, :], ALU.mult).then_inc(cond_ready, 1)
                    dve.tensor_copy(ident_bf[:, :], ident[:, :])
                    for dup in range(2):
                        dve.tensor_scalar(maskq[:, :, dup, :], mask_u8[:, :, :], -1.0, MASKED, ALU.add, ALU.mult)
                    dve.tensor_scalar(maskk[:, :, :], maskT_u8[:, :, :], -1.0, MASKED, ALU.add, ALU.mult)
                    dve.tensor_scalar(kbias_row[:, :, :], krow_u8[:, :, :], -1.0, MASKED, ALU.add, ALU.mult)
                    dve.tensor_scalar(kbias_col[:, :], kcol_u8[:, :], -1.0, MASKED * SCALE, ALU.add, ALU.mult)
                    half = N_MOD * 2 * FC // 2
                    for i in range(2):
                        dve.wait_ge(mod_sum_done, i + 1)
                        cols = slice(i * half, (i + 1) * half)
                        bias = mod_bias[:, cols].unsqueeze(1).to_broadcast([P, B, half])
                        link(dve.tensor_tensor(mod_all[:, :, cols], gen[i][:, 0:half * B].rearrange("p (n b) -> p b n", b=B),
                                               bias, ALU.add))
                    pairs = mod_all[:, :, :].rearrange("p b (m two c) -> p b m two c", two=2, c=FC)
                    for m in range(N_MOD):
                        scale = pairs[:, :, m, 0, :]
                        link(dve.tensor_scalar(scale, scale, 1.0, None, ALU.add))
                        if m < 3:
                            w = norm_w[:, m, :].unsqueeze(1).to_broadcast([P, B, FC])
                            link(dve.tensor_tensor(scale, scale, w, ALU.mult))
                    for i, (bank, lo, hi) in enumerate(((pv[:, 0], 0, 512), (pv[:, 1], 512, 1024), (score[0][:, 0], 1024, 1280))):
                        dve.wait_ge(gate_sum_done, i + 1)
                        dve.tensor_copy(gates[:, lo:hi], bank[0:B, 0:hi - lo]).then_inc(gates_ready, 1)

                @block.tensor
                def _(pe):
                    pe.wait_ge(const_loaded, 16 * len(const_loads))
                    pe.wait_ge(adaln_loaded, 16 * len(ada_loads))
                    pe.wait_ge(cond_ready, 1)
                    half = N_MOD * 2 * FC // 2
                    for n in range(N_MOD * 2 * FC):
                        m, kind, fc = n // (2 * FC), n // FC % 2, n % FC
                        key, scale0, shift0, silu = mod_src[m]
                        col = (shift0 if kind else scale0) + fc * P
                        c = siluT if silu else condT
                        out = gen[n // half][:, n % half * B:n % half * B + B]
                        for kc in range(FC):
                            mm = pe.matmul(out, ada[key][:, kc, col:col + P], c[:, kc, :], start=kc == 0, stop=kc == FC - 1)
                        if n % half == half - 1:
                            mm.then_inc(mod_sum_done, 1)
                    banks = [pv[:, 0], pv[:, 1], score[0][:, 0]]
                    for g, (key, col, silu) in enumerate(gate_src):
                        c = siluT if silu else condT
                        out = banks[g // 2][0:B, g % 2 * D:g % 2 * D + D]
                        for kc in range(FC):
                            pe.matmul(out, c[:, kc, :], ada[key][:, kc, col:col + D], start=kc == 0, stop=False)
                        mm = pe.matmul(out, ones16[:, :], gate_bias[:, g * D:g * D + D], start=False, stop=True)
                        if g % 2 or g == N_GATE - 1:
                            mm.then_inc(gate_sum_done, 1)

        w = {"qkv": sb("w_qkv", [P, FC, 3 * D]), "so": sb("w_so", [P, FC, D]), "cq": sb("w_cq", [P, FC, D]),
             "ckv": sb("w_ckv", [P, FC, 2 * D]), "co": sb("w_co", [P, FC, D]),
             "w1": sb("w_w1", [P, FC, FF]), "w2": sb("w_w2", [P, FFC, D])}
        bias = {"qkv": sb("b_qkv", [P, 3 * D]), "so": sb("b_so", [P, D]), "cq": sb("b_cq", [P, D]),
                "ckv": sb("b_ckv", [P, 2 * D]), "co": sb("b_co", [P, D]), "b2": sb("b_b2", [P, D])}
        b1 = sb("b_b1", [P, FFC])

        def per_slot(name, shape, dt=F32):
            return [sb(f"{name}{s}", shape, dt) for s in range(SLOTS)]

        x_in = per_slot("x_in", [P, TC, D])
        x = per_slot("x", [P, TC, D])
        stats = per_slot("stats", [P, TC, 6])
        mean_var = per_slot("mean_var", [P, TC, 2])
        var_eps = per_slot("var_eps", [P, TC])
        rstd = per_slot("rstd", [P, TC])
        xhat = per_slot("xhat", [P, TC, D])
        xnT = per_slot("xnT", [P, FC, S])
        ctx_in = per_slot("ctx_in", [CTX, D])
        c_stats = per_slot("c_stats", [CTX, 6])
        c_mean_var = per_slot("c_mean_var", [CTX, 2])
        c_var_eps = per_slot("c_var_eps", [CTX, 1])
        c_rstd = per_slot("c_rstd", [CTX, 1])
        chat = per_slot("chat", [CTX, D])
        ctxT = per_slot("ctxT", [P, FC, CTX])
        mod = per_slot("mod", [P, 3 * 2 * FC])
        krow = per_slot("krow", [1, 4, CTXP], BF16)
        kcol = per_slot("kcol", [CTX, 1])
        gate = per_slot("gate", [P, 3, D])
        qk_tok = per_slot("qk_tok", [P, TC, 2, H, 4, HD], F32R)
        q_stack = per_slot("q_stack", [P, PAIRS, S], F32R)
        k_stack = per_slot("k_stack", [P, PAIRS, 2, S], F32R)
        v_one = per_slot("v_one", [P, TC, H, VW])
        row_max = per_slot("row_max", [P, TC, H])
        max_tok = per_slot("max_tok", [P, TC, P], F32R)
        maxT = per_slot("maxT", [P, S], F32R)
        rsum = per_slot("rsum", [P, TC, H])
        at = per_slot("at", [P, TC, D])
        atT = xnT
        hT = per_slot("hT", [P, FFC, S])
        delta = at
        pause = sb("pause", [P, 1])
        rope_a = sb("rope_a", [P, 2 * H, HD])
        rope_b = sb("rope_b", [P, 2 * H, HD])
        qk_f32 = sb("qk_f32", [P, 2 * H, HD])
        probs = [sb(f"probs{b}", [P, 4, S]) for b in range(2)]

        weight_loads = [
            {"qkv": ["L0_qkv"], "so": ["L0_so"], "cq": ["L0_cq"], "ckv": ["L0_ck", "L0_cv"], "co": ["L0_co"],
             "w1": ["L0_w1"], "w2": ["L0_w2"]},
            {"cq": ["L1_cq"], "ckv": ["L1_ckv"], "co": ["L1_co"]},
            {"qkv": ["L2_qkv"], "so": ["L2_so"], "cq": ["L2_cq"], "ckv": ["L2_ckv"], "co": ["L2_co"],
             "w1": ["L2_w1"], "w2": ["L2_w2"]},
            {"qkv": ["L3_qkv"], "so": ["L3_so"], "cq": ["L3_cq"], "ckv": ["L3_ck", "L3_cv"], "co": ["L3_co"],
             "w1": ["L3_w1"], "w2": ["L3_w2"]}]
        bias_loads = [
            {"b2": "L0_b2", "b1": "L0_b1"},
            {"cq": "L1_bq", "ckv": "L1_bkv", "co": "L1_bo"},
            {"qkv": "L2_bqkv", "so": "L2_bso", "cq": "L2_bq", "ckv": "L2_bkv", "co": "L2_bo", "b2": "L2_b2", "b1": "L2_b1"},
            {"b2": "L3_b2", "b1": "L3_b1"}]
        block_of = {"qkv": "self", "so": "self", "cq": "cross", "ckv": "cross", "co": "cross", "w1": "mlp", "w2": "mlp",
                    "b2": "mlp", "b1": "mlp"}
        out_bias = {"self": "so", "cross": "co", "mlp": "b2"}
        kinds = ["self", "cross", "mlp"]

        w_loaded = {kind: sem(f"w_loaded_{kind}") for kind in kinds}
        x_loaded = [sem(f"x_loaded{s}") for s in range(SLOTS)]
        ctx_loaded = [sem(f"ctx_loaded{s}") for s in range(SLOTS)]
        gate_loaded = [sem(f"gate_loaded{s}") for s in range(SLOTS)]
        x_stored = [sem(f"x_stored{s}") for s in range(SLOTS)]
        init_done = sem("init_done")
        init_zeroed = sem("init_zeroed")
        copies_done = [sem(f"copies_done{s}") for s in range(SLOTS)]
        x_ready = [sem(f"x_ready{s}") for s in range(SLOTS)]
        var_ready = [sem(f"var_ready{s}") for s in range(SLOTS)]
        rstd_ready = [sem(f"rstd_ready{s}") for s in range(SLOTS)]
        xhat_ready = [sem(f"xhat_ready{s}") for s in range(SLOTS)]
        c_var_ready = [sem(f"c_var_ready{s}") for s in range(SLOTS)]
        c_rstd_ready = [sem(f"c_rstd_ready{s}") for s in range(SLOTS)]
        chat_ready = [sem(f"chat_ready{s}") for s in range(SLOTS)]
        split_ready = [sem(f"split_ready{s}") for s in range(SLOTS)]
        max_tok_ready = [sem(f"max_tok_ready{s}") for s in range(SLOTS)]
        max_rows_ready = [sem(f"max_rows_ready{s}") for s in range(SLOTS)]
        gated = [sem(f"gated{s}") for s in range(SLOTS)]
        gen_full = [sem(f"gen_full{b}") for b in range(2)]
        gen_moved = [sem(f"gen_moved{b}") for b in range(2)]
        score_full = [sem(f"score_full{b}") for b in range(2)]
        max_done = [sem(f"max_done{b}") for b in range(2)]
        exp_done = [sem(f"exp_done{b}") for b in range(2)]
        probs_used = [sem(f"probs_used{b}") for b in range(2)]
        pv_moved = sem("pv_moved")
        dve_link = sem("dve_link")

        def weight_dmas(li, kind):
            out = []
            for key, names in weight_loads[li].items():
                if block_of[key] == kind:
                    width = w[key].shape[2] // len(names)
                    for i, name in enumerate(names):
                        out.append((w[key][:, :, i * width:(i + 1) * width], a[name].rearrange("(c p) n -> p c n", p=P)))
            for key, name in bias_loads[li].items():
                if block_of[key] == kind:
                    out.append((b1[:, :], a[name]) if key == "b1" else (bias[key][:, :], a[name].partition_broadcast(P)))
            return out

        loads_through = {kind: [16 * sum(len(weight_dmas(j, kind)) for j in range(li + 1)) for li in range(len(LAYERS))]
                         for kind in kinds}

        class Counts:

            def __init__(self, li, it):
                self.li, self.it, self.layer, self.plan = li, it, LAYERS[li], plans[li]

            def val(self, what, n):
                start = 1 if what in FROM_ONE else 0
                return self.it * self.plan.count[what] + (base[self.li][what] + n + start)

            def loads(self):
                return self.it * 16 + 16 * (self.li * ITERS + 1)

            def attn(self, k):
                return self.layer.attn.index(k)

            def wait_moved(self, eng, step):
                b, n = self.plan.gen[step]
                eng.wait_ge(gen_moved[b], self.val("gen", n + 1))

            def wait_filled(self, eng, step):
                b, n = self.plan.gen[step]
                eng.wait_ge(gen_full[b], self.val("gen", n + 1))
                return gen[b], gen_moved[b]

            def wait_scores(self, eng, step):
                b, n_max, n_exp, _ = self.plan.score[step]
                eng.wait_ge(score_full[b], self.val("score", n_max + n_exp + 1))
                return b

        def gates_through(counts):
            before = sum(layer.gates > 0 for layer in LAYERS[0:counts.li])
            return counts.it * 16 + 16 * (before * ITERS + 1)

        with nc.Block() as block:
            @block.sync
            def _(sp):
                def load_kind(li, kind):
                    if not weight_dmas(li, kind):
                        return
                    before = [j for j in range(li) if weight_dmas(j, kind)]
                    if before:
                        j = before[-1]
                        k = [b.kind for b in LAYERS[j].blocks].index(kind)
                        for s in range(SLOTS):
                            sp.wait_ge(x_ready[s], base[j]["block"] + (ITERS - 1) * LAYERS[j].nb + k + 1)
                    for dst, src in weight_dmas(li, kind):
                        sp.dma_start(dst, src).then_inc(w_loaded[kind], 16)

                def load_x(li, s, it):
                    src = a["x"] if li == 0 else x_dram
                    sp.dma_start(x_in[s][:, :, :], src[it * SLOTS + s].rearrange("(c p) d -> p c d", p=P)).then_inc(x_loaded[s], 16)

                def load_ctx(s, it):
                    sp.dma_start(ctx_in[s][:, :], a["ctx"][it * SLOTS + s]).then_inc(ctx_loaded[s], 16)

                def load_gate(layer, s, it):
                    src = gates_dram[it * SLOTS + s, layer.gate0 * D:(layer.gate0 + layer.gates) * D].partition_broadcast(P)
                    sp.dma_start(gate[s][:, 0:layer.gates, :].rearrange("p g d -> p (g d)"), src).then_inc(gate_loaded[s], 16)

                def store_x(li, s, it):
                    dst = a["out"] if li == len(LAYERS) - 1 else x_dram
                    sp.dma_start(dst[it * SLOTS + s].rearrange("(c p) d -> p c d", p=P), x[s][:, :, :]).then_inc(x_stored[s], 16)

                def context_read(counts, s):
                    k = [b.kind for b in counts.layer.blocks].index("cross")
                    counts.wait_moved(sp, (k, s, "cT", 0))

                for li, layer in enumerate(LAYERS):
                    nb = layer.nb
                    last = Counts(li, ITERS - 1)
                    for s in range(SLOTS):
                        if li:
                            prev = LAYERS[li - 1]
                            sp.wait_ge(x_ready[s], base[li - 1]["block"] + (ITERS - 1) * prev.nb + 1)
                            sp.wait_ge(x_stored[s], 16 * ((li - 1) * ITERS + 2))
                        load_x(li, s, 0)
                    if li == 0:
                        load_kind(li, "self")
                    for s in range(SLOTS):
                        if li:
                            context_read(Counts(li - 1, ITERS - 1), s)
                        load_ctx(s, 0)
                    for s in range(SLOTS):
                        if layer.gates:
                            if li:
                                sp.wait_ge(x_ready[s], base[li]["block"])
                            load_gate(layer, s, 0)
                    for kind in kinds:
                        if li or kind != "self":
                            load_kind(li, kind)
                    with sp.Fori(0, ITERS - 1) as it:
                        counts = Counts(li, it)
                        for s in range(SLOTS):
                            sp.wait_ge(x_ready[s], counts.val("block", 1))
                            if li:
                                sp.wait_ge(x_stored[s], it * 16 + 16 * ((li - 1) * ITERS + 3))
                            load_x(li, s, it + 1)
                        for s in range(SLOTS):
                            context_read(counts, s)
                            load_ctx(s, it + 1)
                        for s in range(SLOTS):
                            sp.wait_ge(x_ready[s], counts.val("block", nb))
                            store_x(li, s, it)
                            if layer.gates:
                                load_gate(layer, s, it + 1)
                    for s in range(SLOTS):
                        sp.wait_ge(x_ready[s], last.val("block", nb))
                        store_x(li, s, ITERS - 1)
                for s in range(SLOTS):
                    sp.wait_ge(x_stored[s], 16 * (len(LAYERS) * ITERS + 1))

            @block.tensor
            def _(pe):
                pe.wait_ge(init_done, 1)

                def fill(counts, step):
                    b, n = counts.plan.gen[step]
                    pe.wait_ge(gen_moved[b], counts.val("gen", n))
                    return gen[b], gen_full[b]

                def fill_scores(counts, step):
                    b, n_max, n_exp, before = counts.plan.score[step]
                    if before == "S":
                        pe.wait_ge(max_done[b], counts.val(f"max{b}", n_max))
                    else:
                        pe.wait_ge(exp_done[b], counts.val(f"exp{b}", n_exp))
                    return score[b], score_full[b]

                def project(out, xT, weight, cols):
                    for fc in range(FC):
                        mm = pe.matmul(out, xT[:, fc], weight[:, fc, cols], start=fc == 0, stop=fc == FC - 1)
                    return mm

                def transpose_tokens(counts, step, src):
                    buf, full = fill(counts, step)
                    for fc in range(FC):
                        for c in range(TC):
                            mm = pe.transpose(buf[:, fc * S + c * P:fc * S + c * P + P], src[:, c, fc * P:fc * P + P], ident[:, :])
                    mm.then_inc(full, 1)

                def transpose_ctx(counts, k, s, blk):
                    if blk.ctx == "norm":
                        pe.wait_ge(chat_ready[s], counts.val("cnorm", 1))
                        src = chat[s]
                    else:
                        pe.wait_ge(ctx_loaded[s], counts.loads())
                        src = ctx_in[s]
                    buf, full = fill(counts, (k, s, "cT", 0))
                    for fc in range(FC):
                        mm = pe.transpose(buf[:, fc * P:fc * P + CTX], src[:, fc * P:fc * P + P], ident[0:CTX, 0:CTX])
                    mm.then_inc(full, 1)

                def project_in(counts, k, s, blk, j):
                    if j == 0:
                        counts.wait_moved(pe, (k, s, "xT", 0))
                        pe.wait_ge(w_loaded[blk.kind], loads_through[blk.kind][counts.li])
                    if blk.kind == "cross" and j == 1:
                        counts.wait_moved(pe, (k, s, "cT", 0))
                    buf, full = fill(counts, (k, s, "qkv", j))
                    if blk.kind == "self" and j < TC:
                        mm = project(buf[:, :], xnT[s][:, :, j * P:j * P + P], w["qkv"], slice(0, 2 * D))
                    elif blk.kind == "cross" and j == 1:
                        mm = project(buf[0:CTX, :], ctxT[s], w["ckv"], slice(0, 2 * D))
                    else:
                        weight, cols = (w["qkv"], slice(2 * D, 3 * D)) if blk.kind == "self" else (w["cq"], slice(0, D))
                        for c in range(TC):
                            mm = project(buf[:, c * D:c * D + D], xnT[s][:, :, c * P:c * P + P], weight, cols)
                    mm.then_inc(full, 1)

                def stack(counts, k, s, blk, name, j):
                    tok = qk_tok[s][:, :, :, :, :, :].bitcast(F32).rearrange("p c t (q two) r d -> p c t q (two r d)", two=2)
                    if name == "stkQ" and j == 0:
                        pe.wait_ge(split_ready[s], counts.val("split", 2 * counts.attn(k) + 2))
                    buf, full = fill(counts, (k, s, name, j))
                    if name == "stkK" and blk.kind == "cross":
                        for i in range(4):
                            mm = pe.transpose(buf[:, i * P:i * P + CTX], tok[0:CTX, 0, 1, 4 * j + i, :], ident[0:CTX, 0:CTX])
                    else:
                        for i in range(2):
                            for c in range(TC):
                                mm = pe.transpose(buf[:, i * S + c * P:i * S + c * P + P],
                                                  tok[:, c, 0 if name == "stkQ" else 1, 2 * j + i, :], ident[:, :])
                    mm.then_inc(full, 1)

                def score_rows(counts, k, s, blk, u):
                    if u == 0:
                        counts.wait_moved(pe, (k, s, "stkK", 3 if blk.kind == "self" else 1))
                        if blk.mask and blk.kind == "cross":
                            pe.wait_ge(copies_done[s], counts.val("copies", 3))
                    buf, full = fill_scores(counts, (k, s, "S", u))
                    for c in range(TC):
                        q = slice(c * P, c * P + P)
                        if blk.kind == "self":
                            if blk.mask:
                                pe.matmul(buf[:, c, :], ident_bf[:, :], maskq[:, c, :, :].rearrange("p t k -> p (t k)"), start=True, stop=False)
                            mm = pe.matmul(buf[:, c, :], q_stack[s][:, u, q], k_stack[s][:, u, :, :].rearrange("p t k -> p (t k)"),
                                           start=not blk.mask, stop=True)
                        else:
                            if blk.mask:
                                pe.matmul(buf[:, c, 0:4 * CTXP], ones_bf[:, :], krow[s][:, :, :].rearrange("p t k -> p (t k)"),
                                          start=True, stop=False, skip_group_check=True)
                            for i in range(2):
                                mm = pe.matmul(buf[:, c, 2 * i * CTXP:2 * (i + 1) * CTXP], q_stack[s][:, 2 * u + i, q],
                                               k_stack[s][:, 2 * u + i, :, 0:CTXP], start=not blk.mask, stop=True, skip_group_check=True)
                    mm.then_inc(full, 1)

                def score_columns(counts, k, s, blk, u):
                    if u == 0:
                        pe.wait_ge(max_rows_ready[s], counts.val("attn", counts.attn(k) + 1))
                    buf, full = fill_scores(counts, (k, s, "ST", u))
                    heads = 2 if blk.kind == "self" else 4
                    for i in range(heads):
                        p, t = (heads * u + i) // 2, i % 2
                        if blk.kind == "self":
                            if blk.mask:
                                pe.matmul(buf[:, i, :], ident_bf[:, :], maskk[:, :, :].rearrange("p c q -> p (c q)"),
                                          start=True, stop=False, skip_group_check=True)
                            for kc in range(TC):
                                mm = pe.matmul(buf[:, i, kc * S:kc * S + S], k_stack[s][:, p, t, kc * P:kc * P + P], q_stack[s][:, p, :],
                                               start=not blk.mask, stop=True, skip_group_check=True)
                        else:
                            mm = pe.matmul(buf[0:CTX, i // 2, i % 2 * S:i % 2 * S + S], k_stack[s][:, p, t, 0:CTX], q_stack[s][:, p, :],
                                           start=True, stop=True, skip_group_check=True)
                    mm.then_inc(full, 1)

                def weigh(counts, k, s, blk, u):
                    keys, chunks, heads = (P, TC, 2) if blk.kind == "self" else (CTX, 1, 4)
                    b, _, n_exp, _ = counts.plan.score[(k, s, "ST", u)]
                    pe.wait_ge(exp_done[b], counts.val(f"exp{b}", n_exp + 1))
                    if u == 0:
                        counts.wait_moved(pe, (k, s, "qkv", 2 if blk.kind == "self" else 1))
                        pe.wait_ge(pv_moved, counts.val("pv", counts.plan.pv[(k, s)]))
                    pb, _ = counts.plan.probs[(k, s, "ST", u)]
                    for i in range(heads):
                        head = heads * u + i
                        for c in range(TC):
                            for kc in range(chunks):
                                mm = pe.matmul(pv[:, c, head * VW:head * VW + VW], probs[pb][0:keys, i * chunks + kc, c * P:c * P + P],
                                               v_one[s][0:keys, kc, head, :], start=kc == 0, stop=kc == chunks - 1, skip_group_check=True)
                    mm.then_inc(probs_used[pb], 1)

                def project_out(counts, k, s, blk):
                    counts.wait_moved(pe, (k, s, "atT", 0))
                    buf, full = fill(counts, (k, s, "out", 0))
                    for c in range(TC):
                        mm = project(buf[:, c * D:c * D + D], atT[s][:, :, c * P:c * P + P], w["so" if blk.kind == "self" else "co"], slice(0, D))
                    mm.then_inc(full, 1)

                def mlp_up(counts, k, s, j):
                    if j == 0:
                        counts.wait_moved(pe, (k, s, "xT", 0))
                        pe.wait_ge(w_loaded["mlp"], loads_through["mlp"][counts.li])
                    buf, full = fill(counts, (k, s, "up", j))
                    for i in range(2):
                        col = (2 * j + i) * P
                        for fc in range(FC):
                            mm = pe.matmul(buf[:, i * S:i * S + S], w["w1"][:, fc, col:col + P], xnT[s][:, fc, :],
                                           start=fc == 0, stop=fc == FC - 1)
                    mm.then_inc(full, 1)

                def mlp_down(counts, k, s):
                    counts.wait_moved(pe, (k, s, "up", FFC // 2 - 1))
                    buf, full = fill(counts, (k, s, "down", 0))
                    for c in range(TC):
                        for j in range(FFC):
                            mm = pe.matmul(buf[:, c * D:c * D + D], hT[s][:, j, c * P:c * P + P], w["w2"][:, j, :],
                                           start=j == 0, stop=j == FFC - 1)
                    mm.then_inc(full, 1)

                for li in range(len(LAYERS)):
                    with pe.Fori(0, ITERS) as it:
                        counts = Counts(li, it)
                        for k, s, name, j in counts.plan.steps:
                            blk = counts.layer.blocks[k]
                            if name == "xT":
                                pe.wait_ge(xhat_ready[s], counts.val("block", k + 1))
                                transpose_tokens(counts, (k, s, name, j), xhat[s])
                            elif name == "cT":
                                transpose_ctx(counts, k, s, blk)
                            elif name == "qkv":
                                project_in(counts, k, s, blk, j)
                            elif name in ("stkQ", "stkK"):
                                stack(counts, k, s, blk, name, j)
                            elif name == "S":
                                score_rows(counts, k, s, blk, j)
                            elif name == "maxT":
                                pe.wait_ge(max_tok_ready[s], counts.val("attn", counts.attn(k) + 1))
                                buf, full = fill(counts, (k, s, name, j))
                                for c in range(TC):
                                    mm = pe.transpose(buf[:, c * P:c * P + P], max_tok[s][:, c, :].bitcast(F32), ident[:, :])
                                mm.then_inc(full, 1)
                            elif name == "ST":
                                score_columns(counts, k, s, blk, j)
                            elif name == "W":
                                weigh(counts, k, s, blk, j)
                            elif name == "atT":
                                pe.wait_ge(pv_moved, counts.val("pv", counts.plan.pv[(k, s)] + 1))
                                transpose_tokens(counts, (k, s, name, j), at[s])
                            elif name == "out":
                                project_out(counts, k, s, blk)
                            elif name == "up":
                                mlp_up(counts, k, s, j)
                            elif name == "down":
                                mlp_down(counts, k, s)

            @block.scalar
            def _(act):
                act.wait_ge(init_done, 1)

                def modulated(counts, out, buf, s, pair, width, stride, moved):
                    for fc in range(FC):
                        col = (pair * 2) * FC + fc
                        ins = act.activation(out[:, fc, :], buf[:, fc * stride:fc * stride + width], ACT.Identity,
                                             bias=mod[s][:, col + FC:col + FC + 1], scale=mod[s][:, col:col + 1])
                    ins.then_inc(moved, 1)

                for li in range(len(LAYERS)):
                    with act.Fori(0, ITERS) as it:
                        counts = Counts(li, it)
                        for step in counts.plan.steps:
                            k, s, name, j = step
                            blk = counts.layer.blocks[k]
                            if name in ("xT", "cT") and (blk.mod if name == "xT" else blk.ctx_mod) is not None:
                                act.wait_ge(copies_done[s], counts.val("copies", counts.plan.count["copies"]))
                                buf, moved = counts.wait_filled(act, step)
                                if name == "xT":
                                    modulated(counts, xnT[s], buf, s, blk.mod, S, S, moved)
                                else:
                                    modulated(counts, ctxT[s], buf, s, blk.ctx_mod, CTX, P, moved)
                            elif name == "xT":
                                buf, moved = counts.wait_filled(act, step)
                                act.copy(xnT[s][:, :, :], buf[:, :].rearrange("p (f t) -> p f t", f=FC)).then_inc(moved, 1)
                            elif name == "cT":
                                buf, moved = counts.wait_filled(act, step)
                                act.copy(ctxT[s][:, :, :], buf[:, 0:FC * P].rearrange("p (f t) -> p f t", f=FC)[:, :, 0:CTX]).then_inc(moved, 1)
                            elif name == "qkv" and j == 2 and not blk.qkv_bias:
                                buf, moved = counts.wait_filled(act, step)
                                act.copy(v_one[s][:, :, :, 0:HD], buf[:, :].rearrange("p (c h d) -> p c h d", c=TC, h=H)).then_inc(moved, 1)
                            elif name == "stkQ":
                                buf, moved = counts.wait_filled(act, step)
                                act.copy(q_stack[s][:, 2 * j:2 * j + 2, :], buf[:, :].rearrange("p (i t) -> p i t", i=2)).then_inc(moved, 1)
                            elif name == "stkK":
                                buf, moved = counts.wait_filled(act, step)
                                n, width = (2, S) if blk.kind == "self" else (4, CTX)
                                src = buf[:, :].rearrange("p (i t) -> p i t", i=n)
                                for t in range(2):
                                    half = slice(64 * t, 64 * t + 64)
                                    ins = act.copy(k_stack[s][half, n * j:n * j + n, t, 0:width], src[half, :, 0:width])
                                ins.then_inc(moved, 1)
                            elif name == "ST":
                                if blk.mask and blk.kind == "cross" and j == 0:
                                    act.wait_ge(copies_done[s], counts.val("copies", 3))
                                b = counts.wait_scores(act, step)
                                pb, n = counts.plan.probs[step]
                                act.wait_ge(probs_used[pb], counts.val("probs", n))
                                keys = P if blk.kind == "self" else CTX
                                kbias = kcol[s][:, 0:1] if blk.mask and blk.kind == "cross" else 0.0
                                act.activation(probs[pb][0:keys, :, :], score[b][0:keys, :, :].rearrange("p a (r q) -> p (a r) q", r=2), ACT.Exp,
                                               bias=kbias, scale=SCALE).then_inc(exp_done[b], 1)
                            elif name == "atT":
                                buf, moved = counts.wait_filled(act, step)
                                act.copy(atT[s][:, :, :], buf[:, :].rearrange("p (f t) -> p f t", f=FC)).then_inc(moved, 1)
                            elif name == "up":
                                if j == 0:
                                    act.wait_ge(w_loaded["mlp"], loads_through["mlp"][li])
                                buf, moved = counts.wait_filled(act, step)
                                for i in range(2):
                                    fn = ACT.Gelu_apprx_tanh if blk.gelu == "tanh" else ACT.Gelu
                                    ins = act.activation(hT[s][:, 2 * j + i, :], buf[:, i * S:i * S + S], fn, bias=b1[:, 2 * j + i:2 * j + i + 1])
                                ins.then_inc(moved, 1)

            @block.gpsimd
            def _(pool):
                def finish_block(counts, k, s, blk):
                    layer = counts.layer
                    counts.wait_moved(pool, (k, s, "down" if blk.kind == "mlp" else "out", 0))
                    old = x_in[s] if k == 0 else x[s]
                    if blk.gate is None and not blk.out_bias:
                        pool.sem_inc(x_ready[s], 1)
                        return
                    if k == 0:
                        pool.wait_ge(x_stored[s], counts.it * 16 + 16 * (counts.li * ITERS + 1))
                    if blk.gate is not None and blk.out_bias:
                        pool.wait_ge(gate_loaded[s], gates_through(counts))
                        n = sum(b.gate is not None and b.out_bias for b in layer.blocks[0:k + 1])
                        pool.tensor_tensor(delta[s][:, :, :], delta[s][:, :, :],
                                           gate[s][:, blk.gate, :].unsqueeze(1).to_broadcast([P, TC, D]), ALU.mult).then_inc(gated[s], 1)
                        pool.wait_ge(gated[s], counts.val("gated", n))
                    if blk.gate is None:
                        other = bias[out_bias[blk.kind]][:, :].unsqueeze(1).to_broadcast([P, TC, D])
                        pool.wait_ge(w_loaded[blk.kind], loads_through[blk.kind][counts.li])
                    else:
                        other = old[:, :, :]
                    pool.tensor_tensor(x[s][:, :, :], delta[s][:, :, :], other, ALU.add).then_inc(x_ready[s], 1)

                for li, layer in enumerate(LAYERS):
                    with pool.Fori(0, ITERS) as it:
                        counts = Counts(li, it)
                        width = layer.mods * 2 * FC
                        for s in range(SLOTS):
                            if li == 0:
                                pool.wait_ge(init_done, 1)
                            pool.tensor_copy(mod[s][:, 0:width], mod_all[:, it * SLOTS + s, layer.mod0 * 2 * FC:layer.mod0 * 2 * FC + width]).then_inc(copies_done[s], 1)
                            if li == 0:
                                pool.tensor_copy(krow[s][:, :, 0:CTX], kbias_row[:, it * SLOTS + s, :].unsqueeze(1).to_broadcast([1, 4, CTX])).then_inc(copies_done[s], 1)
                                pool.tensor_copy(kcol[s][:, :], kbias_col[:, bass.ds(it * SLOTS + s, 1)]).then_inc(copies_done[s], 1)
                        for k, s, name, j in counts.plan.steps:
                            blk = layer.blocks[k]
                            if name == "ln":
                                pool.wait_ge(var_ready[s], counts.val("block", k + 1))
                                pool.tensor_tensor(rstd[s][:, :], var_eps[s][:, :], minus_half[:, :], ALU.pow).then_inc(rstd_ready[s], 1)
                            elif name == "cn" and blk.ctx == "norm":
                                pool.wait_ge(c_var_ready[s], counts.val("cnorm", 1))
                                pool.tensor_tensor(c_rstd[s][:, :], c_var_eps[s][:, :], minus_half[0:CTX, 0:1], ALU.pow).then_inc(c_rstd_ready[s], 1)
                            elif name in ("out", "down"):
                                finish_block(counts, k, s, blk)

            @block.vector
            def _(dve):
                for s in range(SLOTS):
                    dve.memset(qk_tok[s][:, :, :, :, :, :].bitcast(F32), 0.0)
                    dve.memset(k_stack[s][:, :, :, :].bitcast(F32), 0.0)
                    dve.memset(max_tok[s][:, :, :].bitcast(F32), 0.0)
                    dve.memset(krow[s][:, :, :], 0.0)
                    dve.memset(v_one[s][:, :, :, :], 1.0).then_inc(init_zeroed, 1)
                dve.wait_ge(init_zeroed, SLOTS)
                for s in range(SLOTS):
                    sel = qk_tok[s][:, :, :, :, :, :].bitcast(F32)
                    for p in range(PAIRS):
                        for part in range(2):
                            ins = dve.memset(sel[:, :, 1, 2 * p:2 * p + 2, 0, part * PAIRS + p], 1.0)
                ins.then_inc(init_done, 1)
                for signal in gen_full + gen_moved + max_done + exp_done + probs_used + split_ready + [pv_moved]:
                    dve.sem_inc(signal, 1)
                for s in range(SLOTS):
                    dve.sem_inc(x_stored[s], 16)

                links = {"n": 0}
                splits = {"last": SLOTS - 1}

                def link(counts, ins):
                    links["n"] += 1
                    ins.then_inc(dve_link, 1)
                    dve.wait_ge(dve_link, counts.val("link", links["n"]))

                def statistics(counts, k, s):
                    src = x_in[s] if k == 0 else x[s]
                    if k == 0:
                        dve.wait_ge(x_loaded[s], counts.loads())
                    else:
                        dve.wait_ge(x_ready[s], counts.val("block", k))
                    for c in range(TC):
                        ins = dve.bn_stats(stats[s][:, c, :], src[:, c, :])
                    link(counts, ins)
                    dve.memset(pause[:, :], 0.0)
                    for c in range(TC):
                        ins = dve.bn_aggr(mean_var[s][:, c, :], stats[s][:, c, :])
                    link(counts, ins)
                    dve.tensor_scalar(var_eps[s][:, :], mean_var[s][:, :, 1], counts.layer.eps, None, ALU.add).then_inc(var_ready[s], 1)

                def normalise(counts, k, s):
                    src = x_in[s] if k == 0 else x[s]
                    dve.wait_ge(rstd_ready[s], counts.val("block", k + 1))
                    for c in range(TC):
                        ins = dve.tensor_scalar(xhat[s][:, c, :], src[:, c, :], mean_var[s][:, c, 0:1], rstd[s][:, c:c + 1],
                                                ALU.subtract, ALU.mult)
                    ins.then_inc(xhat_ready[s], 1)

                def context_norm(counts, s):
                    dve.wait_ge(ctx_loaded[s], counts.loads())
                    link(counts, dve.bn_stats(c_stats[s][:, :], ctx_in[s][:, :]))
                    dve.memset(pause[:, :], 0.0)
                    link(counts, dve.bn_aggr(c_mean_var[s][:, :], c_stats[s][:, :]))
                    dve.tensor_scalar(c_var_eps[s][:, :], c_mean_var[s][:, 1:2], counts.layer.eps, None, ALU.add).then_inc(c_var_ready[s], 1)
                    dve.wait_ge(c_rstd_ready[s], counts.val("cnorm", 1))
                    dve.tensor_scalar(chat[s][:, :], ctx_in[s][:, :], c_mean_var[s][:, 0:1], c_rstd[s][:, 0:1],
                                      ALU.subtract, ALU.mult).then_inc(chat_ready[s], 1)

                def rotate(counts, out, src, cos, sin, moved):
                    n = len(src.shape)
                    lo, hi = (slice(None),) * (n - 1) + (slice(0, HD // 2),), (slice(None),) * (n - 1) + (slice(HD // 2, HD),)
                    ra, rb = like(rope_a, src), like(rope_b, src)
                    dve.tensor_tensor(ra, src, cos, ALU.mult)
                    dve.tensor_tensor(rb[lo], src[hi], sin[lo], ALU.mult)
                    ins = dve.tensor_tensor(rb[hi], src[lo], sin[hi], ALU.mult)
                    if moved is not None:
                        ins.then_inc(moved[0], 1)
                        dve.wait_ge(moved[0], moved[1])
                    else:
                        link(counts, ins)
                    link(counts, dve.tensor_tensor(out, ra, rb, ALU.add))

                def like(t, src):
                    if len(src.shape) == 3:
                        return t[0:src.shape[0], 0:src.shape[1], :]
                    return t[:, :, :].rearrange("p (c h) d -> p c h d", c=src.shape[1])

                def moved_value(counts, step):
                    b, n = counts.plan.gen[step]
                    return gen_moved[b], counts.val("gen", n + 1)

                def split(counts, s, jobs):
                    tok = qk_tok[s]
                    for src, n, c, t in jobs:
                        rows = slice(1, 3) if t == 0 else slice(1, 4, 2)
                        ins = dve.tensor_copy(tok[0:n, c, t, :, rows, :], src.unsqueeze(2).to_broadcast([n, H, 2, HD]))
                    link(counts, ins)
                    for src, n, c, t in jobs:
                        ins = dve.tensor_tensor(tok[0:n, c, t, :, 3 if t == 0 else 2, :], src, tok[0:n, c, t, :, 1, :].bitcast(F32), ALU.subtract)
                    ins.then_inc(split_ready[s], 1)
                    splits[s] += 1
                    splits["last"] = s

                def inputs(counts, k, s, blk, j):
                    step = (k, s, "qkv", j)
                    before = splits["last"]
                    dve.wait_ge(split_ready[before], counts.val("split", splits[before]))
                    if blk.kind == "self" and j < TC:
                        buf, moved = counts.wait_filled(dve, step)
                        src = buf[:, :].rearrange("p (h d) -> p h d", d=HD)
                        if blk.rope:
                            at_chunk = j if counts.layer.rope_period == S else 0
                            cos, sin = (t[:, at_chunk, :].unsqueeze(1).to_broadcast([P, 2 * H, HD]) for t in (cos_t, sin_t))
                            rotate(counts, qk_f32[:, :, :], src, cos, sin, moved_value(counts, step))
                        else:
                            dve.wait_ge(w_loaded["self"], loads_through["self"][counts.li])
                            dve.tensor_tensor(qk_f32[:, :, :], src, bias["qkv"][:, 0:2 * D].rearrange("p (h d) -> p h d", d=HD), ALU.add).then_inc(moved, 1)
                            counts.wait_moved(dve, step)
                        split(counts, s, [(qk_f32[:, t * H:t * H + H, :], P, j, t) for t in range(2)])
                    elif blk.kind == "self" and blk.qkv_bias:
                        buf, moved = counts.wait_filled(dve, step)
                        vb = bias["qkv"][:, 2 * D:3 * D].rearrange("p (h d) -> p h d", d=HD)
                        for c in range(TC):
                            ins = dve.tensor_tensor(v_one[s][:, c, :, 0:HD], buf[:, c * D:c * D + D].rearrange("p (h d) -> p h d", d=HD), vb, ALU.add)
                        ins.then_inc(moved, 1)
                    elif blk.kind == "cross" and j == 0:
                        buf, moved = counts.wait_filled(dve, step)
                        q = qk_f32[:, :, :].rearrange("p (c h) d -> p c h d", c=TC)
                        src = buf[:, :].rearrange("p (c h d) -> p c h d", c=TC, d=HD)
                        if blk.rope:
                            cos, sin = (t[:, :, :].unsqueeze(2).to_broadcast([P, TC, H, HD]) for t in (cos_t, sin_t))
                            rotate(counts, q, src, cos, sin, moved_value(counts, step))
                        elif blk.qkv_bias:
                            dve.wait_ge(w_loaded["cross"], loads_through["cross"][counts.li])
                            qb = bias["cq"][:, :].rearrange("p (h d) -> p h d", d=HD).unsqueeze(1).to_broadcast([P, TC, H, HD])
                            dve.tensor_tensor(q, src, qb, ALU.add).then_inc(moved, 1)
                            counts.wait_moved(dve, step)
                        else:
                            dve.tensor_copy(q, src).then_inc(moved, 1)
                            counts.wait_moved(dve, step)
                        split(counts, s, [(q[:, c, :, :], P, c, 0) for c in range(TC)])
                    elif blk.kind == "cross":
                        buf, moved = counts.wait_filled(dve, step)
                        src = buf[0:CTX, 0:D].rearrange("p (h d) -> p h d", d=HD)
                        v = buf[0:CTX, D:2 * D].rearrange("p (h d) -> p h d", d=HD)
                        ck = qk_f32[0:CTX, 0:H, :]
                        if blk.qkv_bias:
                            cb = bias["ckv"][0:CTX, :].rearrange("p (h d) -> p h d", d=HD)
                            dve.tensor_tensor(ck, src, cb[:, 0:H, :], ALU.add)
                            dve.tensor_tensor(v_one[s][0:CTX, 0, :, 0:HD], v, cb[:, H:2 * H, :], ALU.add).then_inc(moved, 1)
                        elif blk.rope:
                            cos, sin = (t[0:CTX, 0, :].unsqueeze(1).to_broadcast([CTX, H, HD]) for t in (cos_t, sin_t))
                            rotate(counts, ck, src, cos, sin, None)
                            dve.tensor_copy(v_one[s][0:CTX, 0, :, 0:HD], v).then_inc(moved, 1)
                        else:
                            dve.tensor_copy(ck, src)
                            dve.tensor_copy(v_one[s][0:CTX, 0, :, 0:HD], v).then_inc(moved, 1)
                        counts.wait_moved(dve, step)
                        split(counts, s, [(ck, CTX, 0, 1)])

                def maximum(counts, k, s, blk, u):
                    step = (k, s, "S", u)
                    b = counts.wait_scores(dve, step)
                    if blk.kind == "self":
                        src, n = score[b][:, :, :].rearrange("p c (h k) -> p c h k", h=2), 2
                    else:
                        src, n = score[b][:, :, 0:4 * CTXP].rearrange("p c (h k) -> p c h k", h=4)[:, :, :, 0:CTX], 4
                    dve.tensor_reduce(row_max[s][:, :, n * u:n * u + n], src, AX_X, ALU.max).then_inc(max_done[b], 1)

                def negate_maximum(counts, k, s, blk):
                    for u in (score_uses(blk) - 2, score_uses(blk) - 1):
                        b, n_max, _, _ = counts.plan.score[(k, s, "S", u)]
                        dve.wait_ge(max_done[b], counts.val(f"max{b}", n_max + 1))
                    src = row_max[s][:, :, :].rearrange("p c (q two) -> p c two q", two=2)
                    dst = max_tok[s][:, :, :].rearrange("p c (two n) -> p c two n", two=2)
                    link(counts, dve.tensor_scalar(dst[:, :, :, 0:PAIRS], src, -1.0, None, ALU.mult))
                    for c in range(TC):
                        ins = dve.scalar_tensor_tensor(out=dst[:, c, :, PAIRS:2 * PAIRS], in0=src[:, c], scalar=-1.0,
                                                       in1=dst[:, c, :, 0:PAIRS].bitcast(F32), op0=ALU.mult, op1=ALU.subtract)
                    ins.then_inc(max_tok_ready[s], 1)

                def spread_maximum(counts, k, s):
                    step = (k, s, "maxT", 0)
                    buf, moved = counts.wait_filled(dve, step)
                    dve.tensor_copy(maxT[s][:, :], buf[:, 0:S]).then_inc(moved, 1)
                    counts.wait_moved(dve, step)
                    for t in range(2):
                        rows = slice(64 * t, 64 * t + 2 * PAIRS)
                        ins = dve.tensor_copy(q_stack[s][rows, :, :], maxT[s][rows, :].bitcast(F32).unsqueeze(1).to_broadcast([2 * PAIRS, PAIRS, S]))
                    ins.then_inc(max_rows_ready[s], 1)

                def divide(counts, k, s, blk):
                    pb, n = counts.plan.probs[(k, s, "ST", score_uses(blk) - 1)]
                    dve.wait_ge(probs_used[pb], counts.val("probs", n + 1))
                    heads = pv[:, :, 0:H * VW].rearrange("p c (h v) -> p c h v", v=VW)
                    link(counts, dve.reciprocal(rsum[s][:, :, :], heads[:, :, :, HD]))
                    dve.tensor_tensor(at[s][:, :, :].rearrange("p c (h d) -> p c h d", d=HD), heads[:, :, :, 0:HD],
                                      rsum[s][:, :, :].unsqueeze(3).to_broadcast([P, TC, H, HD]), ALU.mult).then_inc(pv_moved, 1)

                def residual(counts, k, s, blk):
                    step = (k, s, "down" if blk.kind == "mlp" else "out", 0)
                    buf, moved = counts.wait_filled(dve, step)
                    src = buf[:, :].rearrange("p (c d) -> p c d", c=TC)
                    old = x_in[s] if k == 0 else x[s]
                    if blk.out_bias and blk.gate is not None:
                        dve.wait_ge(w_loaded[blk.kind], loads_through[blk.kind][counts.li])
                        dve.tensor_tensor(delta[s][:, :, :], src, bias[out_bias[blk.kind]][:, :].unsqueeze(1).to_broadcast([P, TC, D]), ALU.add).then_inc(moved, 1)
                    elif blk.out_bias:
                        dve.tensor_tensor(delta[s][:, :, :], src, old[:, :, :], ALU.add).then_inc(moved, 1)
                    elif blk.gate is not None:
                        dve.wait_ge(gate_loaded[s], gates_through(counts))
                        dve.tensor_tensor(delta[s][:, :, :], src, gate[s][:, blk.gate, :].unsqueeze(1).to_broadcast([P, TC, D]), ALU.mult).then_inc(moved, 1)
                    else:
                        if k == 0:
                            dve.wait_ge(x_stored[s], counts.it * 16 + 16 * (counts.li * ITERS + 1))
                        dve.tensor_tensor(x[s][:, :, :], src, old[:, :, :], ALU.add).then_inc(moved, 1)

                for li in range(len(LAYERS)):
                    with dve.Fori(0, ITERS) as it:
                        counts = Counts(li, it)
                        links["n"] = 0
                        splits.update({s: 0 for s in range(SLOTS)})
                        for k, s, name, j in counts.plan.steps:
                            blk = counts.layer.blocks[k]
                            if name == "ln":
                                statistics(counts, k, s)
                            elif name == "nx":
                                normalise(counts, k, s)
                            elif name == "cn" and blk.ctx == "norm":
                                context_norm(counts, s)
                            elif name == "qkv":
                                inputs(counts, k, s, blk, j)
                            elif name == "S":
                                maximum(counts, k, s, blk, j)
                            elif name == "mx":
                                negate_maximum(counts, k, s, blk)
                            elif name == "maxT":
                                spread_maximum(counts, k, s)
                            elif name == "at":
                                divide(counts, k, s, blk)
                            elif name in ("out", "down"):
                                residual(counts, k, s, blk)
                        assert links["n"] == counts.plan.count["link"], (li, links["n"], counts.plan.count["link"])


def kernel(**inputs):
    import numpy as np
    import concourse.bacc as bacc
    from concourse.bass_utils import run_bass_kernel_spmd

    def get(name):
        return np.ascontiguousarray(inputs[name])

    def turned(name):
        return np.ascontiguousarray(np.asarray(inputs[name]).T)

    def columns(v):
        return np.ascontiguousarray(np.asarray(v).reshape(-1, P).T)

    L = {n: f"L{n}_xcond_" for n in range(4)}
    inv_freq = 1.0 / 10000.0 ** (np.arange(0, HD, 2, dtype=np.float32) / HD)
    angle = np.outer(np.arange(S, dtype=np.float32), inv_freq).astype(np.float32)
    cos = np.concatenate([np.cos(angle)] * 2, axis=-1).astype(np.float32)
    sin = np.concatenate([-np.sin(angle), np.sin(angle)], axis=-1).astype(np.float32)

    ada_b, mod_b = np.asarray(inputs[L[0] + "adaLN_b"]), np.asarray(inputs[L[2] + "b_mod"])
    ssq, sskv = np.asarray(inputs[L[1] + "bss_q"]), np.asarray(inputs[L[1] + "bss_kv"])
    ln_b = [np.asarray(inputs[L[3] + f"ln{i}_b"]) for i in (1, 2, 3)]

    def part(v, i):
        return v[i * D:(i + 1) * D]

    mod_bias = np.concatenate([part(ada_b, 1), part(ada_b, 0), part(ada_b, 4), part(ada_b, 3), part(ada_b, 7), part(ada_b, 6),
                               ssq, sskv, part(mod_b, 1), part(mod_b, 0), part(mod_b, 4), part(mod_b, 3)] + ln_b)
    gate_bias = np.concatenate([part(ada_b, 2), part(ada_b, 5), part(ada_b, 8), part(mod_b, 2), part(mod_b, 5)])
    norm_w = np.concatenate([np.asarray(inputs[L[0] + n]) for n in ("norm1_w", "normc_w", "norm2_w")])
    mask = np.asarray(inputs["mask_SxS_bk0"])
    kmask = np.asarray(inputs["mask_BxS2_bf1"])

    arrays = {
        "x": get("x"), "ctx": get("ctx_1024"), "condT": turned("cond_1024"),
        "mask": np.ascontiguousarray(mask), "maskT": np.ascontiguousarray(mask.T),
        "kmask": np.ascontiguousarray(kmask), "kmaskT": np.ascontiguousarray(kmask.T),
        "ident": np.eye(P, dtype=np.float32),
        "cos": np.ascontiguousarray(cos.reshape(TC, P, HD).transpose(1, 0, 2)),
        "sin": np.ascontiguousarray(sin.reshape(TC, P, HD).transpose(1, 0, 2)),
        "mod_bias": columns(mod_bias), "gate_bias": gate_bias.reshape(1, -1), "norm_w": columns(norm_w).reshape(P, 3, FC),
        "adaln0": get(L[0] + "adaLN_W"), "adaln1q": get(L[1] + "Wss_q"), "adaln1kv": get(L[1] + "Wss_kv"), "adaln2": get(L[2] + "W_mod"),
        "adaln3a": turned(L[3] + "ln1_w"), "adaln3b": turned(L[3] + "ln2_w"), "adaln3c": turned(L[3] + "ln3_w"),
        "L0_qkv": get(L[0] + "qkv_W"), "L0_so": get(L[0] + "attn_out_W"), "L0_cq": get(L[0] + "cq_W"), "L0_ck": get(L[0] + "ck_W"),
        "L0_cv": get(L[0] + "cv_W"), "L0_co": get(L[0] + "co_W"), "L0_w1": get(L[0] + "mlp_W1"), "L0_w2": get(L[0] + "mlp_W2"),
        "L0_b1": columns(inputs[L[0] + "mlp_b1"]), "L0_b2": get(L[0] + "mlp_b2"),
        "L1_cq": get(L[1] + "Wq"), "L1_ckv": get(L[1] + "Wkv"), "L1_co": get(L[1] + "Wp"),
        "L1_bq": get(L[1] + "bq"), "L1_bkv": get(L[1] + "bkv"), "L1_bo": get(L[1] + "bp"),
        "L2_qkv": get(L[2] + "W_qkv"), "L2_so": get(L[2] + "W_proj"), "L2_cq": get(L[2] + "W_qc"), "L2_ckv": get(L[2] + "W_kvc"),
        "L2_co": get(L[2] + "W_cproj"), "L2_w1": get(L[2] + "W_mlp1"), "L2_w2": get(L[2] + "W_mlp2"),
        "L2_bqkv": get(L[2] + "b_qkv"), "L2_bso": get(L[2] + "b_proj"), "L2_bq": get(L[2] + "b_qc"), "L2_bkv": get(L[2] + "b_kvc"),
        "L2_bo": get(L[2] + "b_cproj"), "L2_b1": columns(inputs[L[2] + "b_mlp1"]), "L2_b2": get(L[2] + "b_mlp2"),
        "L3_qkv": turned(L[3] + "qkv_w"), "L3_so": turned(L[3] + "sa_out_w"), "L3_cq": turned(L[3] + "q_w"), "L3_ck": turned(L[3] + "k_w"),
        "L3_cv": turned(L[3] + "v_w"), "L3_co": turned(L[3] + "ca_out_w"), "L3_w1": turned(L[3] + "ffn_w1"), "L3_w2": turned(L[3] + "ffn_w2"),
        "L3_b1": columns(inputs[L[3] + "ffn_b1"]), "L3_b2": get(L[3] + "ffn_b2"),
    }
    nc = bacc.Bacc("TRN2", target_bir_lowering=False, num_devices=1)
    feed, aps = {}, {}
    for name, v in arrays.items():
        feed[f"in_{name}"] = v
        aps[name] = nc.dram_tensor(f"in_{name}", v.shape, mybir.dt.from_np(v.dtype), kind="ExternalInput").ap()
    aps["out"] = nc.dram_tensor("out_x", (B, S, D), F32, kind="ExternalOutput").ap()
    dit_stack(nc, aps)
    r = run_bass_kernel_spmd(nc, [feed], core_ids=[0])
    return r.results[0]["out_x"]
```

```python
from contextlib import ExitStack

import concourse.bass as bass
from concourse import mybir

F32 = mybir.dt.float32
F32R = mybir.dt.float32r
BF16 = mybir.dt.bfloat16
U8 = mybir.dt.uint8
ALU = mybir.AluOpType
ACT = mybir.ActivationFunctionType
AX_X = mybir.AxisListType.X

P = 128
B, S, D = 16, 256, 256
H, HD = 16, 16
CTX = 77
CTXP = CTX + 1
FF = 4 * D
TC = S // P
FC = D // P
FFC = FF // P
PAIRS = H // 2
SLOTS = 2
ROUNDS = B // SLOTS
PER_LOOP = 2
ITERS = ROUNDS // PER_LOOP
SCALE = HD ** -0.5
MASKED = 2.0 ** 120
VW = 32
HG = P // VW
NG = H // HG


class Block:

    def __init__(self, kind, mod=None, rope=False, mask=False, gate=None, qkv_bias=False, out_bias=False,
                 ctx=None, ctx_mod=None, gelu=None):
        self.kind, self.mod, self.rope, self.mask, self.gate = kind, mod, rope, mask, gate
        self.qkv_bias, self.out_bias, self.ctx, self.ctx_mod, self.gelu = qkv_bias, out_bias, ctx, ctx_mod, gelu


class Layer:
    def __init__(self, name, eps, rope_period, mod0, mods, gate0, gates, blocks):
        self.name, self.eps, self.rope_period, self.blocks = name, eps, rope_period, blocks
        self.mod0, self.mods, self.gate0, self.gates = mod0, mods, gate0, gates
        self.nb = len(blocks)
        self.all = blocks * PER_LOOP
        self.attn = [k for k, b in enumerate(self.all) if b.kind != "mlp"]


LAYERS = [
    Layer("L0", 1e-5, P, 0, 3, 0, 3, [
        Block("self", mod=0, rope=True, mask=True, gate=0),
        Block("cross", mod=1, gate=1, mask=True, ctx="raw"),
        Block("mlp", mod=2, gate=2, out_bias=True, gelu="tanh")]),
    Layer("L1", 1e-5, None, 3, 2, None, 0, [
        Block("cross", mod=0, qkv_bias=True, out_bias=True, ctx="norm", ctx_mod=1)]),
    Layer("L2", 1e-6, None, 5, 2, 3, 2, [
        Block("self", mod=0, qkv_bias=True, out_bias=True, gate=0),
        Block("cross", qkv_bias=True, out_bias=True, ctx="norm"),
        Block("mlp", mod=1, gate=1, out_bias=True, gelu="tanh")]),
    Layer("L3", 1e-5, S, 7, 3, None, 0, [
        Block("self", mod=0, rope=True),
        Block("cross", mod=1, rope=True, ctx="raw"),
        Block("mlp", mod=2, out_bias=True, gelu="erf")]),
]
N_MOD = 10
N_GATE = 5


def score_uses(blk):
    return PAIRS if blk.kind == "self" else PAIRS // 2


NOMINAL = {"cp": 0.3, "ln": 2.0, "nx": 1.0, "xT": 2.0, "cn": 0.5, "cT": 0.5, "qkv": 2.5, "stkQ": 1.0, "stkK": 1.2, "S": 1.5, "mx": 0.5,
           "maxT": 3.0, "ST": 1.5, "W": 1.0, "pv": 1.5, "oX": 1.0, "atT": 1.5, "out": 3.0, "up": 2.5, "down": 8.0}
LAG = 24.0


def block_steps(blk, first):
    steps = [("cp", 0)] if first else []
    if blk.kind == "cross":
        steps += [("cn", 0), ("cT", 0)]
    steps += [("ln", 0), ("nx", 0), ("xT", 0)]
    if blk.kind == "mlp":
        return steps + [("up", j) for j in range(FFC // 2)] + [("down", 0)]
    parts, k_fills = (3, 4) if blk.kind == "self" else (2, 2)
    steps += [("qkv", j) for j in range(parts)]
    steps += [("stkQ", j) for j in range(4)] + [("stkK", j) for j in range(k_fills)]
    steps += [("S", u) for u in range(score_uses(blk))] + [("mx", 0), ("maxT", 0)]
    late = []
    for u in range(score_uses(blk)):
        steps.append(("ST", u))
        steps += late
        late = [("W", head_group(blk, u))] if group_complete(blk, u) else []
    return steps + late + [("pv", 0), ("oX", 0), ("oX", 1), ("atT", 0), ("out", 0)]


def head_group(blk, u):
    return u // 2 if blk.kind == "self" else u


def group_complete(blk, u):
    return blk.kind == "cross" or u % 2 == 1


def group_fills(blk, g):
    return (2 * g, 2 * g + 1) if blk.kind == "self" else (g,)


def schedule(layer):
    timed = []
    for s in range(SLOTS):
        t = LAG * s
        for k, blk in enumerate(layer.all):
            for name, j in block_steps(blk, k % layer.nb == 0):
                timed.append((t, s, len(timed), (k, s, name, j)))
                t += NOMINAL[name]
    return [step for *_, step in sorted(timed)]


FROM_ONE = ("gen", "max0", "max1", "exp0", "exp1", "weighed", "pv", "split")
GEN_STEPS = ("xT", "cT", "qkv", "stkQ", "stkK", "maxT", "oX", "atT", "out", "up", "down")
PROBS = 4


class Plan:

    def __init__(self, layer):
        self.layer, self.steps = layer, schedule(layer)
        self.gen = {}
        self.score = {}
        self.probs = {}
        self.weighed = {}
        self.pv = {}
        n_gen, users, done = 0, [], {(q, b): 0 for q in ("S", "ST") for b in range(2)}
        fills, reader = [], {}
        for step in self.steps:
            k, s, name, j = step
            if name in GEN_STEPS:
                self.gen[step] = (n_gen % 2, n_gen // 2)
                n_gen += 1
            if name in ("S", "ST"):
                b = len(users) % 2
                before = users[-2] if len(users) > 1 else "ST"
                self.score[step] = (b, done["S", b], done["ST", b], before)
                done[name, b] += 1
                users.append(name)
            if name == "ST":
                n = len(fills)
                self.probs[step] = (n % PROBS, reader[fills[n - PROBS]] + 1 if n >= PROBS else 0)
                fills.append(step)
            if name == "W":
                for u in group_fills(layer.all[k], j):
                    reader[(k, s, "ST", u)] = len(self.weighed)
                self.weighed[step] = len(self.weighed)
                if j == 0:
                    self.pv[(k, s)] = len(self.pv)
        assert n_gen % 2 == 0 and len(users) % 2 == 0 and len(fills) % PROBS == 0 and users[-2:] == ["ST", "ST"]
        links = sum(links_of(layer, b) for b in layer.all) * SLOTS
        self.count = {"gen": n_gen // 2, "max0": done["S", 0], "max1": done["S", 1], "exp0": done["ST", 0], "exp1": done["ST", 1],
                      "score": len(users) // 2, "weighed": len(self.weighed), "pv": len(self.pv), "link": links, "block": len(layer.all),
                      "attn": len(layer.attn), "split": 2 * len(layer.attn), "cnorm": sum(b.ctx == "norm" for b in layer.all),
                      "copies": COPIES[layer.name] * PER_LOOP, "gated": sum(b.gate is not None and b.out_bias for b in layer.all)}


COPIES = {"L0": 3, "L1": 1, "L2": 1, "L3": 1}


def links_of(layer, blk):
    n = 2
    if blk.kind == "mlp":
        return n
    parts = 2
    n += parts * ((1 if blk.rope else 0) + 1)
    if blk.rope and blk.kind == "cross":
        n += 1
    if blk.ctx == "norm":
        n += 2
    return n + 1 + TC


def dit_stack(nc, a):
    plans = [Plan(layer) for layer in LAYERS]

    base, total = [], {key: 0 for key in plans[0].count}
    for plan in plans:
        base.append(dict(total))
        for key in total:
            total[key] += ITERS * plan.count[key]

    keep = ExitStack()
    with keep:
        def sb(name, shape, dt=F32, stack=keep):
            return stack.enter_context(nc.sbuf_tensor(name, shape, dt))

        def sem(name):
            return keep.enter_context(nc.semaphore(name))

        score = [keep.enter_context(nc.psum_tensor(f"score{b}", [P, 2, 512], F32)) for b in range(2)]
        pv = keep.enter_context(nc.psum_tensor("pv", [P, NG, S], F32))
        gen = [keep.enter_context(nc.psum_tensor(f"gen{b}", [P, 512], F32)) for b in range(2)]

        ident = sb("ident", [P, P])
        ident_bf = sb("ident_bf", [P, P], BF16)
        ones_bf = sb("ones_bf", [1, P], BF16)
        minus_half = sb("minus_half", [P, TC])
        cos_t = sb("cos_t", [P, TC, HD])
        sin_t = sb("sin_t", [P, TC, HD])
        mod_all = sb("mod_all", [P, B, N_MOD * 2 * FC])
        maskq = sb("maskq", [P, TC, S], BF16)
        maskk = sb("maskk", [P, TC, S], BF16)
        kbias_row = sb("kbias_row", [1, B, CTX], BF16)
        kbias_col = sb("kbias_col", [CTX, B])
        gates_dram = nc.dram_tensor("gates_scratch", (B, N_GATE * D), F32, kind="Internal").ap()
        x_dram = nc.dram_tensor("x_scratch", (B, S, D), F32, kind="Internal").ap()

        const_loaded = sem("const_loaded")
        adaln_loaded = sem("adaln_loaded")
        silu_exp_done = sem("silu_exp_done")
        cond_ready = sem("cond_ready")
        pro_link = sem("pro_link")
        mod_sum_done = sem("mod_sum_done")
        gate_sum_done = sem("gate_sum_done")
        gates_ready = sem("gates_ready")
        gates_stored = sem("gates_stored")

        with ExitStack() as pro:
            condT = sb("condT", [P, FC, B], F32, pro)
            siluT = sb("siluT", [P, FC, B], F32, pro)
            expT = sb("expT", [P, FC, B], F32, pro)
            ada = {"L0": sb("ada0", [P, FC, 9 * D], F32, pro), "L1q": sb("ada1q", [P, FC, 2 * D], F32, pro),
                   "L1kv": sb("ada1kv", [P, FC, 2 * D], F32, pro), "L2": sb("ada2", [P, FC, 6 * D], F32, pro),
                   "L3a": sb("ada3a", [P, FC, 2 * D], F32, pro), "L3b": sb("ada3b", [P, FC, 2 * D], F32, pro),
                   "L3c": sb("ada3c", [P, FC, 2 * D], F32, pro)}
            mod_bias = sb("mod_bias", [P, N_MOD * 2 * FC], F32, pro)
            norm_w = sb("norm_w", [P, 3, FC], F32, pro)
            gate_bias = sb("gate_bias", [1, N_GATE * D], F32, pro)
            ones16 = sb("ones16", [1, B], F32, pro)
            gates = sb("gates", [B, N_GATE * D], F32, pro)
            mask_u8 = sb("mask_u8", [P, TC, S], U8, pro)
            maskT_u8 = sb("maskT_u8", [P, TC, S], U8, pro)
            krow_u8 = sb("krow_u8", [1, B, CTX], U8, pro)
            kcol_u8 = sb("kcol_u8", [CTX, B], U8, pro)

            mod_src = [("L0", D, 0, False), ("L0", 4 * D, 3 * D, False), ("L0", 7 * D, 6 * D, False),
                       ("L1q", 0, D, True), ("L1kv", 0, D, True),
                       ("L2", D, 0, True), ("L2", 4 * D, 3 * D, True),
                       ("L3a", 0, D, False), ("L3b", 0, D, False), ("L3c", 0, D, False)]
            gate_src = [("L0", 2 * D, False), ("L0", 5 * D, False), ("L0", 8 * D, False),
                        ("L2", 2 * D, True), ("L2", 5 * D, True)]
            const_loads = [(ident[:, :], a["ident"]), (cos_t[:, :, :], a["cos"]), (sin_t[:, :, :], a["sin"]),
                           (condT[:, :, :], a["condT"].rearrange("(c p) b -> p c b", p=P)),
                           (mod_bias[:, :], a["mod_bias"]), (norm_w[:, :, :], a["norm_w"]),
                           (gate_bias[:, :], a["gate_bias"]),
                           (mask_u8[:, :, :], a["mask"].rearrange("(c p) k -> p c k", p=P)),
                           (maskT_u8[:, :, :], a["maskT"].rearrange("(c p) k -> p c k", p=P)),
                           (krow_u8[:, :, :], a["kmask"].rearrange("(o b) k -> o b k", o=1)),
                           (kcol_u8[:, :], a["kmaskT"])]
            ada_loads = [("L0", "adaln0"), ("L1q", "adaln1q"), ("L1kv", "adaln1kv"), ("L2", "adaln2"),
                         ("L3a", "adaln3a"), ("L3b", "adaln3b"), ("L3c", "adaln3c")]

            with nc.Block() as block:
                @block.sync
                def _(sp):
                    for dst, src in const_loads:
                        sp.dma_start(dst, src).then_inc(const_loaded, 16)
                    for key, name in ada_loads:
                        sp.dma_start(ada[key][:, :, :], a[name].rearrange("(c p) n -> p c n", p=P)).then_inc(adaln_loaded, 16)
                    sp.wait_ge(gates_ready, 3)
                    sp.dma_start(gates_dram, gates[:, :]).then_inc(gates_stored, 16)
                    sp.wait_ge(gates_stored, 16)

                @block.scalar
                def _(act):
                    act.wait_ge(const_loaded, 16 * len(const_loads))
                    act.activation(expT[:, :, :], condT[:, :, :], ACT.Exp, scale=-1.0).then_inc(silu_exp_done, 1)

                @block.vector
                def _(dve):
                    links = [0]

                    def link(ins):
                        links[0] += 1
                        ins.then_inc(pro_link, 1)
                        dve.wait_ge(pro_link, links[0])

                    dve.memset(ones_bf[:, :], 1.0)
                    dve.memset(minus_half[:, :], -0.5)
                    dve.memset(ones16[:, :], 1.0)
                    dve.wait_ge(const_loaded, 16 * len(const_loads))
                    dve.wait_ge(silu_exp_done, 1)
                    link(dve.tensor_scalar(expT[:, :, :], expT[:, :, :], 1.0, None, ALU.add))
                    link(dve.reciprocal(siluT[:, :, :], expT[:, :, :]))
                    dve.tensor_tensor(siluT[:, :, :], siluT[:, :, :], condT[:, :, :], ALU.mult).then_inc(cond_ready, 1)
                    dve.tensor_copy(ident_bf[:, :], ident[:, :])
                    dve.tensor_scalar(maskq[:, :, :], mask_u8[:, :, :], -1.0, MASKED, ALU.add, ALU.mult)
                    dve.tensor_scalar(maskk[:, :, :], maskT_u8[:, :, :], -1.0, MASKED, ALU.add, ALU.mult)
                    dve.tensor_scalar(kbias_row[:, :, :], krow_u8[:, :, :], -1.0, MASKED, ALU.add, ALU.mult)
                    dve.tensor_scalar(kbias_col[:, :], kcol_u8[:, :], -1.0, MASKED * SCALE, ALU.add, ALU.mult)
                    half = N_MOD * 2 * FC // 2
                    for i in range(2):
                        dve.wait_ge(mod_sum_done, i + 1)
                        cols = slice(i * half, (i + 1) * half)
                        bias = mod_bias[:, cols].unsqueeze(1).to_broadcast([P, B, half])
                        link(dve.tensor_tensor(mod_all[:, :, cols], gen[i][:, 0:half * B].rearrange("p (n b) -> p b n", b=B),
                                               bias, ALU.add))
                    pairs = mod_all[:, :, :].rearrange("p b (m two c) -> p b m two c", two=2, c=FC)
                    for m in range(N_MOD):
                        scale = pairs[:, :, m, 0, :]
                        link(dve.tensor_scalar(scale, scale, 1.0, None, ALU.add))
                        if m < 3:
                            w = norm_w[:, m, :].unsqueeze(1).to_broadcast([P, B, FC])
                            link(dve.tensor_tensor(scale, scale, w, ALU.mult))
                    for i, (bank, lo, hi) in enumerate(((score[1][:, 0], 0, 512), (score[1][:, 1], 512, 1024), (score[0][:, 0], 1024, 1280))):
                        dve.wait_ge(gate_sum_done, i + 1)
                        dve.tensor_copy(gates[:, lo:hi], bank[0:B, 0:hi - lo]).then_inc(gates_ready, 1)

                @block.tensor
                def _(pe):
                    pe.wait_ge(const_loaded, 16 * len(const_loads))
                    pe.wait_ge(adaln_loaded, 16 * len(ada_loads))
                    pe.wait_ge(cond_ready, 1)
                    half = N_MOD * 2 * FC // 2
                    for n in range(N_MOD * 2 * FC):
                        m, kind, fc = n // (2 * FC), n // FC % 2, n % FC
                        key, scale0, shift0, silu = mod_src[m]
                        col = (shift0 if kind else scale0) + fc * P
                        c = siluT if silu else condT
                        out = gen[n // half][:, n % half * B:n % half * B + B]
                        for kc in range(FC):
                            mm = pe.matmul(out, ada[key][:, kc, col:col + P], c[:, kc, :], start=kc == 0, stop=kc == FC - 1)
                        if n % half == half - 1:
                            mm.then_inc(mod_sum_done, 1)
                    banks = [score[1][:, 0], score[1][:, 1], score[0][:, 0]]
                    for g, (key, col, silu) in enumerate(gate_src):
                        c = siluT if silu else condT
                        out = banks[g // 2][0:B, g % 2 * D:g % 2 * D + D]
                        for kc in range(FC):
                            pe.matmul(out, c[:, kc, :], ada[key][:, kc, col:col + D], start=kc == 0, stop=False)
                        mm = pe.matmul(out, ones16[:, :], gate_bias[:, g * D:g * D + D], start=False, stop=True)
                        if g % 2 or g == N_GATE - 1:
                            mm.then_inc(gate_sum_done, 1)

        w = {"qkv": sb("w_qkv", [P, FC, 3 * D]), "so": sb("w_so", [P, FC, D]), "cq": sb("w_cq", [P, FC, D]),
             "ckv": sb("w_ckv", [P, FC, 2 * D]), "co": sb("w_co", [P, FC, D]),
             "w1": sb("w_w1", [P, FC, FF]), "w2": sb("w_w2", [P, FFC, D])}
        bias = {"qkv": sb("b_qkv", [P, 3 * D]), "so": sb("b_so", [P, D]), "cq": sb("b_cq", [P, D]),
                "ckv": sb("b_ckv", [P, 2 * D]), "co": sb("b_co", [P, D]), "b2": sb("b_b2", [P, D])}
        b1 = sb("b_b1", [P, FFC])

        def per_slot(name, shape, dt=F32):
            return [sb(f"{name}{s}", shape, dt) for s in range(SLOTS)]

        x_in = per_slot("x_in", [P, TC, D])
        x = per_slot("x", [P, TC, D])
        stats = per_slot("stats", [P, TC, 6])
        mean_var = per_slot("mean_var", [P, TC, 2])
        var_eps = per_slot("var_eps", [P, TC])
        rstd = per_slot("rstd", [P, TC])
        xhat = per_slot("xhat", [P, TC, D])
        xnT = per_slot("xnT", [P, FC, S])
        ctx_in = per_slot("ctx_in", [CTX, D])
        c_stats = per_slot("c_stats", [CTX, 6])
        c_mean_var = per_slot("c_mean_var", [CTX, 2])
        c_var_eps = per_slot("c_var_eps", [CTX, 1])
        c_rstd = per_slot("c_rstd", [CTX, 1])
        chat = per_slot("chat", [CTX, D])
        ctxT = per_slot("ctxT", [P, FC, CTX])
        mod = per_slot("mod", [P, 3 * 2 * FC])
        krow = per_slot("krow", [1, 4, CTXP], BF16)
        kcol = per_slot("kcol", [CTX, 1])
        gate = per_slot("gate", [P, 3, D])
        qk_tok = per_slot("qk_tok", [P, TC, 2, H, 4, HD], F32R)
        q_stack = per_slot("q_stack", [P, PAIRS, S], F32R)
        k_stack = per_slot("k_stack", [P, PAIRS, 2, S], F32R)
        v_one = per_slot("v_one", [P, TC, H, VW])
        row_max = per_slot("row_max", [P, TC, H])
        max_tok = per_slot("max_tok", [P, TC, P], F32R)
        maxT = per_slot("maxT", [P, S], F32R)
        rsum = per_slot("rsum", [P, TC, H])
        at = xhat
        atT = xnT
        hT = per_slot("hT", [P, FFC, S])
        oT = hT
        delta = at
        pause = sb("pause", [P, 1])
        rope_a = bias["qkv"][:, 0:2 * D].rearrange("p (h d) -> p h d", d=HD)
        rope_b = sb("rope_b", [P, 2 * H, HD])
        qk_f32 = sb("qk_f32", [P, 2 * H, HD])
        probs = [sb(f"probs{b}", [P, 4, S]) for b in range(PROBS)]

        weight_loads = [
            {"qkv": ["L0_qkv"], "so": ["L0_so"], "cq": ["L0_cq"], "ckv": ["L0_ck", "L0_cv"], "co": ["L0_co"],
             "w1": ["L0_w1"], "w2": ["L0_w2"]},
            {"cq": ["L1_cq"], "ckv": ["L1_ckv"], "co": ["L1_co"]},
            {"qkv": ["L2_qkv"], "so": ["L2_so"], "cq": ["L2_cq"], "ckv": ["L2_ckv"], "co": ["L2_co"],
             "w1": ["L2_w1"], "w2": ["L2_w2"]},
            {"qkv": ["L3_qkv"], "so": ["L3_so"], "cq": ["L3_cq"], "ckv": ["L3_ck", "L3_cv"], "co": ["L3_co"],
             "w1": ["L3_w1"], "w2": ["L3_w2"]}]
        bias_loads = [
            {"b2": "L0_b2", "b1": "L0_b1"},
            {"cq": "L1_bq", "ckv": "L1_bkv", "co": "L1_bo"},
            {"qkv": "L2_bqkv", "so": "L2_bso", "cq": "L2_bq", "ckv": "L2_bkv", "co": "L2_bo", "b2": "L2_b2", "b1": "L2_b1"},
            {"b2": "L3_b2", "b1": "L3_b1"}]
        block_of = {"qkv": "self", "so": "self", "cq": "cross", "ckv": "cross", "co": "cross", "w1": "mlp", "w2": "mlp",
                    "b2": "mlp", "b1": "mlp"}
        out_bias = {"self": "so", "cross": "co", "mlp": "b2"}
        kinds = ["self", "cross", "mlp"]

        w_loaded = {kind: sem(f"w_loaded_{kind}") for kind in kinds}
        x_loaded = [sem(f"x_loaded{s}") for s in range(SLOTS)]
        ctx_loaded = [sem(f"ctx_loaded{s}") for s in range(SLOTS)]
        gate_loaded = [sem(f"gate_loaded{s}") for s in range(SLOTS)]
        x_stored = [sem(f"x_stored{s}") for s in range(SLOTS)]
        init_done = sem("init_done")
        init_zeroed = sem("init_zeroed")
        copies_done = [sem(f"copies_done{s}") for s in range(SLOTS)]
        x_ready = [sem(f"x_ready{s}") for s in range(SLOTS)]
        var_ready = [sem(f"var_ready{s}") for s in range(SLOTS)]
        rstd_ready = [sem(f"rstd_ready{s}") for s in range(SLOTS)]
        xhat_ready = [sem(f"xhat_ready{s}") for s in range(SLOTS)]
        c_var_ready = [sem(f"c_var_ready{s}") for s in range(SLOTS)]
        c_rstd_ready = [sem(f"c_rstd_ready{s}") for s in range(SLOTS)]
        chat_ready = [sem(f"chat_ready{s}") for s in range(SLOTS)]
        split_ready = [sem(f"split_ready{s}") for s in range(SLOTS)]
        max_tok_ready = [sem(f"max_tok_ready{s}") for s in range(SLOTS)]
        max_rows_ready = [sem(f"max_rows_ready{s}") for s in range(SLOTS)]
        gated = [sem(f"gated{s}") for s in range(SLOTS)]
        gen_full = [sem(f"gen_full{b}") for b in range(2)]
        gen_moved = [sem(f"gen_moved{b}") for b in range(2)]
        score_full = [sem(f"score_full{b}") for b in range(2)]
        max_done = [sem(f"max_done{b}") for b in range(2)]
        exp_done = [sem(f"exp_done{b}") for b in range(2)]
        weighed = sem("weighed")
        pv_moved = sem("pv_moved")
        dve_link = sem("dve_link")

        def weight_dmas(li, kind):
            out = []
            for key, names in weight_loads[li].items():
                if block_of[key] == kind:
                    width = w[key].shape[2] // len(names)
                    for i, name in enumerate(names):
                        out.append((w[key][:, :, i * width:(i + 1) * width], a[name].rearrange("(c p) n -> p c n", p=P)))
            for key, name in bias_loads[li].items():
                if block_of[key] == kind:
                    out.append((b1[:, :], a[name]) if key == "b1" else (bias[key][:, :], a[name].partition_broadcast(P)))
            return out

        loads_through = {kind: [16 * sum(len(weight_dmas(j, kind)) for j in range(li + 1)) for li in range(len(LAYERS))]
                         for kind in kinds}

        class Counts:

            def __init__(self, li, it):
                self.li, self.it, self.layer, self.plan = li, it, LAYERS[li], plans[li]

            def val(self, what, n):
                start = 1 if what in FROM_ONE else 0
                return self.it * self.plan.count[what] + (base[self.li][what] + n + start)

            def loads(self, k):
                return self.it * (16 * PER_LOOP) + 16 * (self.li * ROUNDS + k // self.layer.nb + 1)

            def copies(self, k):
                return self.val("copies", COPIES[self.layer.name] * (k // self.layer.nb + 1))

            def batch(self, k, s):
                return self.it * (PER_LOOP * SLOTS) + ((k // self.layer.nb) * SLOTS + s)

            def first(self, k):
                return k % self.layer.nb == 0

            def cnorm(self, k):
                return sum(b.ctx == "norm" for b in self.layer.all[0:k + 1])

            def attn(self, k):
                return self.layer.attn.index(k)

            def wait_moved(self, eng, step):
                b, n = self.plan.gen[step]
                eng.wait_ge(gen_moved[b], self.val("gen", n + 1))

            def wait_filled(self, eng, step):
                b, n = self.plan.gen[step]
                eng.wait_ge(gen_full[b], self.val("gen", n + 1))
                return gen[b], gen_moved[b]

            def wait_scores(self, eng, step):
                b, n_max, n_exp, _ = self.plan.score[step]
                eng.wait_ge(score_full[b], self.val("score", n_max + n_exp + 1))
                return b

        def gates_through(counts, k):
            before = sum(layer.gates > 0 for layer in LAYERS[0:counts.li])
            return counts.it * (16 * PER_LOOP) + 16 * (before * ROUNDS + k // counts.layer.nb + 1)

        def stored_before(counts, k):
            return counts.it * (16 * PER_LOOP) + 16 * (counts.li * ROUNDS + k // counts.layer.nb + 1)

        with nc.Block() as block:
            @block.sync
            def _(sp):
                def load_kind(li, kind):
                    if not weight_dmas(li, kind):
                        return
                    before = [j for j in range(li) if weight_dmas(j, kind)]
                    if before:
                        j = before[-1]
                        k = [b.kind for b in LAYERS[j].blocks].index(kind)
                        for s in range(SLOTS):
                            sp.wait_ge(x_ready[s], base[j]["block"] + (ROUNDS - 1) * LAYERS[j].nb + k + 1)
                    for dst, src in weight_dmas(li, kind):
                        sp.dma_start(dst, src).then_inc(w_loaded[kind], 16)

                def load_x(li, s, it):
                    src = a["x"] if li == 0 else x_dram
                    sp.dma_start(x_in[s][:, :, :], src[it * SLOTS + s].rearrange("(c p) d -> p c d", p=P)).then_inc(x_loaded[s], 16)

                def load_ctx(s, it):
                    sp.dma_start(ctx_in[s][:, :], a["ctx"][it * SLOTS + s]).then_inc(ctx_loaded[s], 16)

                def load_gate(layer, s, it):
                    src = gates_dram[it * SLOTS + s, layer.gate0 * D:(layer.gate0 + layer.gates) * D].partition_broadcast(P)
                    sp.dma_start(gate[s][:, 0:layer.gates, :].rearrange("p g d -> p (g d)"), src).then_inc(gate_loaded[s], 16)

                def store_x(li, s, it):
                    dst = a["out"] if li == len(LAYERS) - 1 else x_dram
                    sp.dma_start(dst[it * SLOTS + s].rearrange("(c p) d -> p c d", p=P), x[s][:, :, :]).then_inc(x_stored[s], 16)

                blocks_before = [0]
                for layer in LAYERS:
                    blocks_before.append(blocks_before[-1] + ROUNDS * layer.nb)

                for li, layer in enumerate(LAYERS):
                    nb, start = layer.nb, blocks_before[li]
                    cross = [b.kind for b in layer.blocks].index("cross")
                    for s in range(SLOTS):
                        if li:
                            prev = LAYERS[li - 1]
                            last = blocks_before[li - 1] + (ROUNDS - 1) * prev.nb
                            sp.wait_ge(x_ready[s], last + 1)
                            sp.wait_ge(x_stored[s], 16 * ((li - 1) * ROUNDS + 2))
                        load_x(li, s, 0)
                    if li == 0:
                        load_kind(li, "self")
                    for s in range(SLOTS):
                        if li:
                            sp.wait_ge(x_ready[s], last + 1 + [b.kind for b in prev.blocks].index("cross"))
                        load_ctx(s, 0)
                    for s in range(SLOTS):
                        if layer.gates:
                            if li:
                                sp.wait_ge(x_ready[s], start)
                            load_gate(layer, s, 0)
                    for kind in kinds:
                        if li or kind != "self":
                            load_kind(li, kind)
                    with sp.Fori(0, ROUNDS - 1) as r:
                        for k in range(nb):
                            for s in range(SLOTS):
                                sp.wait_ge(x_ready[s], r * nb + (start + k + 1))
                                if k == 0:
                                    if li:
                                        sp.wait_ge(x_stored[s], r * 16 + 16 * ((li - 1) * ROUNDS + 3))
                                    load_x(li, s, r + 1)
                                if k == cross:
                                    load_ctx(s, r + 1)
                                if k == nb - 1:
                                    store_x(li, s, r)
                                    if layer.gates:
                                        load_gate(layer, s, r + 1)
                    for s in range(SLOTS):
                        sp.wait_ge(x_ready[s], start + ROUNDS * nb)
                        store_x(li, s, ROUNDS - 1)
                for s in range(SLOTS):
                    sp.wait_ge(x_stored[s], 16 * (len(LAYERS) * ROUNDS + 1))

            @block.tensor
            def _(pe):
                pe.wait_ge(init_done, 1)

                def fill(counts, step):
                    b, n = counts.plan.gen[step]
                    pe.wait_ge(gen_moved[b], counts.val("gen", n))
                    return gen[b], gen_full[b]

                def fill_scores(counts, step):
                    b, n_max, n_exp, before = counts.plan.score[step]
                    if before == "S":
                        pe.wait_ge(max_done[b], counts.val(f"max{b}", n_max))
                    else:
                        pe.wait_ge(exp_done[b], counts.val(f"exp{b}", n_exp))
                    return score[b], score_full[b]

                def project(out, xT, weight, cols):
                    for fc in range(FC):
                        mm = pe.matmul(out, xT[:, fc], weight[:, fc, cols], start=fc == 0, stop=fc == FC - 1)
                    return mm

                def transpose_tokens(counts, step, src):
                    buf, full = fill(counts, step)
                    for fc in range(FC):
                        for c in range(TC):
                            mm = pe.transpose(buf[:, fc * S + c * P:fc * S + c * P + P], src[:, c, fc * P:fc * P + P], ident[:, :])
                    mm.then_inc(full, 1)

                def transpose_ctx(counts, k, s, blk):
                    if blk.ctx == "norm":
                        pe.wait_ge(chat_ready[s], counts.val("cnorm", counts.cnorm(k)))
                        src = chat[s]
                    else:
                        pe.wait_ge(ctx_loaded[s], counts.loads(k))
                        src = ctx_in[s]
                    buf, full = fill(counts, (k, s, "cT", 0))
                    for fc in range(FC):
                        mm = pe.transpose(buf[:, fc * P:fc * P + CTX], src[:, fc * P:fc * P + P], ident[0:CTX, 0:CTX])
                    mm.then_inc(full, 1)

                def project_in(counts, k, s, blk, j):
                    if j == 0:
                        counts.wait_moved(pe, (k, s, "xT", 0))
                        pe.wait_ge(w_loaded[blk.kind], loads_through[blk.kind][counts.li])
                    if blk.kind == "cross" and j == 1:
                        counts.wait_moved(pe, (k, s, "cT", 0))
                    buf, full = fill(counts, (k, s, "qkv", j))
                    if blk.kind == "self" and j < TC:
                        mm = project(buf[:, :], xnT[s][:, :, j * P:j * P + P], w["qkv"], slice(0, 2 * D))
                    elif blk.kind == "cross" and j == 1:
                        mm = project(buf[0:CTX, :], ctxT[s], w["ckv"], slice(0, 2 * D))
                    else:
                        weight, cols = (w["qkv"], slice(2 * D, 3 * D)) if blk.kind == "self" else (w["cq"], slice(0, D))
                        for c in range(TC):
                            mm = project(buf[:, c * D:c * D + D], xnT[s][:, :, c * P:c * P + P], weight, cols)
                    mm.then_inc(full, 1)

                def stack(counts, k, s, blk, name, j):
                    tok = qk_tok[s][:, :, :, :, :, :].bitcast(F32).rearrange("p c t (q two) r d -> p c t q (two r d)", two=2)
                    if name == "stkQ" and j == 0:
                        pe.wait_ge(split_ready[s], counts.val("split", 2 * counts.attn(k) + 2))
                    buf, full = fill(counts, (k, s, name, j))
                    if name == "stkK" and blk.kind == "cross":
                        for i in range(4):
                            mm = pe.transpose(buf[:, i * P:i * P + CTX], tok[0:CTX, 0, 1, 4 * j + i, :], ident[0:CTX, 0:CTX])
                    else:
                        for i in range(2):
                            for c in range(TC):
                                mm = pe.transpose(buf[:, i * S + c * P:i * S + c * P + P],
                                                  tok[:, c, 0 if name == "stkQ" else 1, 2 * j + i, :], ident[:, :])
                    mm.then_inc(full, 1)

                def score_rows(counts, k, s, blk, u):
                    if u == 0:
                        counts.wait_moved(pe, (k, s, "stkK", 3 if blk.kind == "self" else 1))
                        if blk.mask and blk.kind == "cross":
                            pe.wait_ge(copies_done[s], counts.copies(k))
                    buf, full = fill_scores(counts, (k, s, "S", u))
                    for c in range(TC):
                        q = slice(c * P, c * P + P)
                        if blk.kind == "self":
                            if blk.mask:
                                pe.matmul(buf[:, c, :], ident_bf[:, :], maskq[:, c, :].unsqueeze(1).to_broadcast([P, 2, S]), start=True, stop=False)
                            mm = pe.matmul(buf[:, c, :], q_stack[s][:, u, q], k_stack[s][:, u, :, :].rearrange("p t k -> p (t k)"),
                                           start=not blk.mask, stop=True)
                        else:
                            if blk.mask:
                                pe.matmul(buf[:, c, 0:4 * CTXP], ones_bf[:, :], krow[s][:, :, :].rearrange("p t k -> p (t k)"),
                                          start=True, stop=False, skip_group_check=True)
                            for i in range(2):
                                mm = pe.matmul(buf[:, c, 2 * i * CTXP:2 * (i + 1) * CTXP], q_stack[s][:, 2 * u + i, q],
                                               k_stack[s][:, 2 * u + i, :, 0:CTXP], start=not blk.mask, stop=True, skip_group_check=True)
                    mm.then_inc(full, 1)

                def score_columns(counts, k, s, blk, u):
                    if u == 0:
                        pe.wait_ge(max_rows_ready[s], counts.val("attn", counts.attn(k) + 1))
                    buf, full = fill_scores(counts, (k, s, "ST", u))
                    heads = 2 if blk.kind == "self" else 4
                    for i in range(heads):
                        p, t = (heads * u + i) // 2, i % 2
                        if blk.kind == "self":
                            if blk.mask:
                                pe.matmul(buf[:, i, :], ident_bf[:, :], maskk[:, :, :].rearrange("p c q -> p (c q)"),
                                          start=True, stop=False, skip_group_check=True)
                            for kc in range(TC):
                                mm = pe.matmul(buf[:, i, kc * S:kc * S + S], k_stack[s][:, p, t, kc * P:kc * P + P], q_stack[s][:, p, :],
                                               start=not blk.mask, stop=True, skip_group_check=True)
                        else:
                            mm = pe.matmul(buf[0:CTX, i // 2, i % 2 * S:i % 2 * S + S], k_stack[s][:, p, t, 0:CTX], q_stack[s][:, p, :],
                                           start=True, stop=True, skip_group_check=True)
                    mm.then_inc(full, 1)

                def weigh(counts, k, s, blk, g):
                    keys, chunks = (P, TC) if blk.kind == "self" else (CTX, 1)
                    fills = group_fills(blk, g)
                    b, _, n_exp, _ = counts.plan.score[(k, s, "ST", fills[-1])]
                    pe.wait_ge(exp_done[b], counts.val(f"exp{b}", n_exp + 1))
                    if g == 0:
                        counts.wait_moved(pe, (k, s, "qkv", 2 if blk.kind == "self" else 1))
                        pe.wait_ge(pv_moved, counts.val("pv", counts.plan.pv[(k, s)]))
                    for kc in range(chunks):
                        for i in range(HG):
                            per_fill = HG // len(fills)
                            pb, _ = counts.plan.probs[(k, s, "ST", fills[i // per_fill])]
                            mm = pe.matmul(pv[VW * i:VW * i + VW, g, :], v_one[s][0:keys, kc, HG * g + i, :],
                                           probs[pb][0:keys, i % per_fill * chunks + kc, :], start=kc == 0, stop=kc == chunks - 1,
                                           skip_group_check=True)
                    mm.then_inc(weighed, 1)

                def transpose_back(counts, k, s, c):
                    if c == 0:
                        pe.wait_ge(pv_moved, counts.val("pv", counts.plan.pv[(k, s)] + 1))
                    buf, full = fill(counts, (k, s, "oX", c))
                    for g in range(NG):
                        mm = pe.transpose(buf[:, g * P:g * P + P], oT[s][:, g, c * P:c * P + P], ident[:, :])
                    mm.then_inc(full, 1)

                def project_out(counts, k, s, blk):
                    counts.wait_moved(pe, (k, s, "atT", 0))
                    buf, full = fill(counts, (k, s, "out", 0))
                    for c in range(TC):
                        mm = project(buf[:, c * D:c * D + D], atT[s][:, :, c * P:c * P + P], w["so" if blk.kind == "self" else "co"], slice(0, D))
                    mm.then_inc(full, 1)

                def mlp_up(counts, k, s, j):
                    if j == 0:
                        counts.wait_moved(pe, (k, s, "xT", 0))
                        pe.wait_ge(w_loaded["mlp"], loads_through["mlp"][counts.li])
                    buf, full = fill(counts, (k, s, "up", j))
                    for i in range(2):
                        col = (2 * j + i) * P
                        for fc in range(FC):
                            mm = pe.matmul(buf[:, i * S:i * S + S], w["w1"][:, fc, col:col + P], xnT[s][:, fc, :],
                                           start=fc == 0, stop=fc == FC - 1)
                    mm.then_inc(full, 1)

                def mlp_down(counts, k, s):
                    counts.wait_moved(pe, (k, s, "up", FFC // 2 - 1))
                    buf, full = fill(counts, (k, s, "down", 0))
                    for c in range(TC):
                        for j in range(FFC):
                            mm = pe.matmul(buf[:, c * D:c * D + D], hT[s][:, j, c * P:c * P + P], w["w2"][:, j, :],
                                           start=j == 0, stop=j == FFC - 1)
                    mm.then_inc(full, 1)

                for li in range(len(LAYERS)):
                    with pe.Fori(0, ITERS) as it:
                        counts = Counts(li, it)
                        for k, s, name, j in counts.plan.steps:
                            blk = counts.layer.all[k]
                            if name == "xT":
                                pe.wait_ge(xhat_ready[s], counts.val("block", k + 1))
                                transpose_tokens(counts, (k, s, name, j), xhat[s])
                            elif name == "cT":
                                transpose_ctx(counts, k, s, blk)
                            elif name == "qkv":
                                project_in(counts, k, s, blk, j)
                            elif name in ("stkQ", "stkK"):
                                stack(counts, k, s, blk, name, j)
                            elif name == "S":
                                score_rows(counts, k, s, blk, j)
                            elif name == "maxT":
                                pe.wait_ge(max_tok_ready[s], counts.val("attn", counts.attn(k) + 1))
                                buf, full = fill(counts, (k, s, name, j))
                                for c in range(TC):
                                    mm = pe.transpose(buf[:, c * P:c * P + P], max_tok[s][:, c, :].bitcast(F32), ident[:, :])
                                mm.then_inc(full, 1)
                            elif name == "ST":
                                score_columns(counts, k, s, blk, j)
                            elif name == "W":
                                weigh(counts, k, s, blk, j)
                            elif name == "oX":
                                transpose_back(counts, k, s, j)
                            elif name == "atT":
                                for c in range(TC):
                                    counts.wait_moved(pe, (k, s, "oX", c))
                                transpose_tokens(counts, (k, s, name, j), at[s])
                            elif name == "out":
                                project_out(counts, k, s, blk)
                            elif name == "up":
                                mlp_up(counts, k, s, j)
                            elif name == "down":
                                mlp_down(counts, k, s)

            @block.scalar
            def _(act):
                act.wait_ge(init_done, 1)

                def modulated(counts, out, buf, s, pair, width, stride, moved):
                    for fc in range(FC):
                        col = (pair * 2) * FC + fc
                        ins = act.activation(out[:, fc, :], buf[:, fc * stride:fc * stride + width], ACT.Identity,
                                             bias=mod[s][:, col + FC:col + FC + 1], scale=mod[s][:, col:col + 1])
                    ins.then_inc(moved, 1)

                for li in range(len(LAYERS)):
                    with act.Fori(0, ITERS) as it:
                        counts = Counts(li, it)
                        for step in counts.plan.steps:
                            k, s, name, j = step
                            blk = counts.layer.all[k]
                            if name in ("xT", "cT") and (blk.mod if name == "xT" else blk.ctx_mod) is not None:
                                act.wait_ge(copies_done[s], counts.copies(k))
                                buf, moved = counts.wait_filled(act, step)
                                if name == "xT":
                                    modulated(counts, xnT[s], buf, s, blk.mod, S, S, moved)
                                else:
                                    modulated(counts, ctxT[s], buf, s, blk.ctx_mod, CTX, P, moved)
                            elif name == "xT":
                                buf, moved = counts.wait_filled(act, step)
                                act.copy(xnT[s][:, :, :], buf[:, :].rearrange("p (f t) -> p f t", f=FC)).then_inc(moved, 1)
                            elif name == "cT":
                                buf, moved = counts.wait_filled(act, step)
                                act.copy(ctxT[s][:, :, :], buf[:, 0:FC * P].rearrange("p (f t) -> p f t", f=FC)[:, :, 0:CTX]).then_inc(moved, 1)
                            elif name == "qkv" and j == 2 and not blk.qkv_bias:
                                buf, moved = counts.wait_filled(act, step)
                                act.copy(v_one[s][:, :, :, 0:HD], buf[:, :].rearrange("p (c h d) -> p c h d", c=TC, h=H)).then_inc(moved, 1)
                            elif name == "stkQ":
                                buf, moved = counts.wait_filled(act, step)
                                act.copy(q_stack[s][:, 2 * j:2 * j + 2, :], buf[:, :].rearrange("p (i t) -> p i t", i=2)).then_inc(moved, 1)
                            elif name == "stkK":
                                buf, moved = counts.wait_filled(act, step)
                                n, width = (2, S) if blk.kind == "self" else (4, CTX)
                                src = buf[:, :].rearrange("p (i t) -> p i t", i=n)
                                for t in range(2):
                                    half = slice(64 * t, 64 * t + 64)
                                    ins = act.copy(k_stack[s][half, n * j:n * j + n, t, 0:width], src[half, :, 0:width])
                                ins.then_inc(moved, 1)
                            elif name == "ST":
                                if blk.mask and blk.kind == "cross" and j == 0:
                                    act.wait_ge(copies_done[s], counts.copies(k))
                                b = counts.wait_scores(act, step)
                                pb, n = counts.plan.probs[step]
                                act.wait_ge(weighed, counts.val("weighed", n))
                                keys = P if blk.kind == "self" else CTX
                                kbias = kcol[s][:, 0:1] if blk.mask and blk.kind == "cross" else 0.0
                                act.activation(probs[pb][0:keys, :, :], score[b][0:keys, :, :].rearrange("p a (r q) -> p (a r) q", r=2), ACT.Exp,
                                               bias=kbias, scale=SCALE).then_inc(exp_done[b], 1)
                            elif name == "pv":
                                act.wait_ge(weighed, counts.val("weighed", counts.plan.weighed[(k, s, "W", NG - 1)] + 1))
                                act.copy(oT[s][:, 0:NG, :], pv[:, :, :]).then_inc(pv_moved, 1)
                            elif name == "atT":
                                buf, moved = counts.wait_filled(act, step)
                                act.copy(atT[s][:, :, :], buf[:, :].rearrange("p (f t) -> p f t", f=FC)).then_inc(moved, 1)
                            elif name == "up":
                                if j == 0:
                                    act.wait_ge(w_loaded["mlp"], loads_through["mlp"][li])
                                buf, moved = counts.wait_filled(act, step)
                                for i in range(2):
                                    fn = ACT.Gelu_apprx_tanh if blk.gelu == "tanh" else ACT.Gelu
                                    ins = act.activation(hT[s][:, 2 * j + i, :], buf[:, i * S:i * S + S], fn, bias=b1[:, 2 * j + i:2 * j + i + 1])
                                ins.then_inc(moved, 1)

            @block.gpsimd
            def _(pool):
                def finish_block(counts, k, s, blk):
                    layer = counts.layer
                    counts.wait_moved(pool, (k, s, "down" if blk.kind == "mlp" else "out", 0))
                    old = x_in[s] if counts.first(k) else x[s]
                    if blk.gate is None and not blk.out_bias:
                        pool.sem_inc(x_ready[s], 1)
                        return
                    if counts.first(k):
                        pool.wait_ge(x_stored[s], stored_before(counts, k))
                    if blk.gate is not None and blk.out_bias:
                        pool.wait_ge(gate_loaded[s], gates_through(counts, k))
                        n = sum(b.gate is not None and b.out_bias for b in layer.all[0:k + 1])
                        pool.tensor_tensor(delta[s][:, :, :], delta[s][:, :, :],
                                           gate[s][:, blk.gate, :].unsqueeze(1).to_broadcast([P, TC, D]), ALU.mult).then_inc(gated[s], 1)
                        pool.wait_ge(gated[s], counts.val("gated", n))
                    if blk.gate is None:
                        other = bias[out_bias[blk.kind]][:, :].unsqueeze(1).to_broadcast([P, TC, D])
                        pool.wait_ge(w_loaded[blk.kind], loads_through[blk.kind][counts.li])
                    else:
                        other = old[:, :, :]
                    pool.tensor_tensor(x[s][:, :, :], delta[s][:, :, :], other, ALU.add).then_inc(x_ready[s], 1)

                for li, layer in enumerate(LAYERS):
                    with pool.Fori(0, ITERS) as it:
                        counts = Counts(li, it)
                        width = layer.mods * 2 * FC
                        for k, s, name, j in counts.plan.steps:
                            blk = layer.all[k]
                            if name == "cp":
                                if li == 0 and k == 0:
                                    pool.wait_ge(init_done, 1)
                                seq = counts.batch(k, s)
                                pool.tensor_copy(mod[s][:, 0:width], mod_all[:, seq, layer.mod0 * 2 * FC:layer.mod0 * 2 * FC + width]).then_inc(copies_done[s], 1)
                                if li == 0:
                                    pool.tensor_copy(krow[s][:, :, 0:CTX], kbias_row[:, seq, :].unsqueeze(1).to_broadcast([1, 4, CTX])).then_inc(copies_done[s], 1)
                                    pool.tensor_copy(kcol[s][:, :], kbias_col[:, bass.ds(seq, 1)]).then_inc(copies_done[s], 1)
                            if name == "ln":
                                pool.wait_ge(var_ready[s], counts.val("block", k + 1))
                                pool.tensor_tensor(rstd[s][:, :], var_eps[s][:, :], minus_half[:, :], ALU.pow).then_inc(rstd_ready[s], 1)
                            elif name == "cn" and blk.ctx == "norm":
                                pool.wait_ge(c_var_ready[s], counts.val("cnorm", counts.cnorm(k)))
                                pool.tensor_tensor(c_rstd[s][:, :], c_var_eps[s][:, :], minus_half[0:CTX, 0:1], ALU.pow).then_inc(c_rstd_ready[s], 1)
                            elif name in ("out", "down"):
                                finish_block(counts, k, s, blk)

            @block.vector
            def _(dve):
                for s in range(SLOTS):
                    dve.memset(qk_tok[s][:, :, :, :, :, :].bitcast(F32), 0.0)
                    dve.memset(k_stack[s][:, :, :, :].bitcast(F32), 0.0)
                    dve.memset(max_tok[s][:, :, :].bitcast(F32), 0.0)
                    dve.memset(krow[s][:, :, :], 0.0)
                    dve.memset(v_one[s][:, :, :, :], 0.0).then_inc(init_zeroed, 1)
                dve.wait_ge(init_zeroed, SLOTS)
                for s in range(SLOTS):
                    dve.memset(v_one[s][:, :, :, HD:HD + 1], 1.0)
                    sel = qk_tok[s][:, :, :, :, :, :].bitcast(F32)
                    for p in range(PAIRS):
                        for part in range(2):
                            ins = dve.memset(sel[:, :, 1, 2 * p:2 * p + 2, 0, part * PAIRS + p], 1.0)
                ins.then_inc(init_done, 1)
                for signal in gen_full + gen_moved + max_done + exp_done + split_ready + [weighed, pv_moved]:
                    dve.sem_inc(signal, 1)
                for s in range(SLOTS):
                    dve.sem_inc(x_stored[s], 16)

                links = {"n": 0}
                splits = {"last": SLOTS - 1}

                def link(counts, ins):
                    links["n"] += 1
                    ins.then_inc(dve_link, 1)
                    dve.wait_ge(dve_link, counts.val("link", links["n"]))

                def statistics(counts, k, s):
                    src = x_in[s] if counts.first(k) else x[s]
                    if counts.first(k):
                        dve.wait_ge(x_loaded[s], counts.loads(k))
                    else:
                        dve.wait_ge(x_ready[s], counts.val("block", k))
                    for c in range(TC):
                        ins = dve.bn_stats(stats[s][:, c, :], src[:, c, :])
                    link(counts, ins)
                    dve.memset(pause[:, :], 0.0)
                    for c in range(TC):
                        ins = dve.bn_aggr(mean_var[s][:, c, :], stats[s][:, c, :])
                    link(counts, ins)
                    dve.tensor_scalar(var_eps[s][:, :], mean_var[s][:, :, 1], counts.layer.eps, None, ALU.add).then_inc(var_ready[s], 1)

                def normalise(counts, k, s):
                    src = x_in[s] if counts.first(k) else x[s]
                    dve.wait_ge(rstd_ready[s], counts.val("block", k + 1))
                    for c in range(TC):
                        ins = dve.tensor_scalar(xhat[s][:, c, :], src[:, c, :], mean_var[s][:, c, 0:1], rstd[s][:, c:c + 1],
                                                ALU.subtract, ALU.mult)
                    ins.then_inc(xhat_ready[s], 1)

                def context_norm(counts, k, s):
                    dve.wait_ge(ctx_loaded[s], counts.loads(k))
                    link(counts, dve.bn_stats(c_stats[s][:, :], ctx_in[s][:, :]))
                    dve.memset(pause[:, :], 0.0)
                    link(counts, dve.bn_aggr(c_mean_var[s][:, :], c_stats[s][:, :]))
                    dve.tensor_scalar(c_var_eps[s][:, :], c_mean_var[s][:, 1:2], counts.layer.eps, None, ALU.add).then_inc(c_var_ready[s], 1)
                    dve.wait_ge(c_rstd_ready[s], counts.val("cnorm", counts.cnorm(k)))
                    dve.tensor_scalar(chat[s][:, :], ctx_in[s][:, :], c_mean_var[s][:, 0:1], c_rstd[s][:, 0:1],
                                      ALU.subtract, ALU.mult).then_inc(chat_ready[s], 1)

                def rotate(counts, out, src, cos, sin, moved):
                    n = len(src.shape)
                    lo, hi = (slice(None),) * (n - 1) + (slice(0, HD // 2),), (slice(None),) * (n - 1) + (slice(HD // 2, HD),)
                    ra, rb = like(rope_a, src), like(rope_b, src)
                    dve.tensor_tensor(ra, src, cos, ALU.mult)
                    dve.tensor_tensor(rb[lo], src[hi], sin[lo], ALU.mult)
                    ins = dve.tensor_tensor(rb[hi], src[lo], sin[hi], ALU.mult)
                    if moved is not None:
                        ins.then_inc(moved[0], 1)
                        dve.wait_ge(moved[0], moved[1])
                    else:
                        link(counts, ins)
                    link(counts, dve.tensor_tensor(out, ra, rb, ALU.add))

                def like(t, src):
                    if len(src.shape) == 3:
                        return t[0:src.shape[0], 0:src.shape[1], :]
                    return t[:, :, :].rearrange("p (c h) d -> p c h d", c=src.shape[1])

                def moved_value(counts, step):
                    b, n = counts.plan.gen[step]
                    return gen_moved[b], counts.val("gen", n + 1)

                def split(counts, s, jobs):
                    tok = qk_tok[s]
                    for src, n, c, t in jobs:
                        rows = slice(1, 3) if t == 0 else slice(1, 4, 2)
                        ins = dve.tensor_copy(tok[0:n, c, t, :, rows, :], src.unsqueeze(2).to_broadcast([n, H, 2, HD]))
                    link(counts, ins)
                    for src, n, c, t in jobs:
                        ins = dve.tensor_tensor(tok[0:n, c, t, :, 3 if t == 0 else 2, :], src, tok[0:n, c, t, :, 1, :].bitcast(F32), ALU.subtract)
                    ins.then_inc(split_ready[s], 1)
                    splits[s] += 1
                    splits["last"] = s

                def inputs(counts, k, s, blk, j):
                    step = (k, s, "qkv", j)
                    before = splits["last"]
                    dve.wait_ge(split_ready[before], counts.val("split", splits[before]))
                    if blk.kind == "self" and j < TC:
                        buf, moved = counts.wait_filled(dve, step)
                        src = buf[:, :].rearrange("p (h d) -> p h d", d=HD)
                        if blk.rope:
                            at_chunk = j if counts.layer.rope_period == S else 0
                            cos, sin = (t[:, at_chunk, :].unsqueeze(1).to_broadcast([P, 2 * H, HD]) for t in (cos_t, sin_t))
                            rotate(counts, qk_f32[:, :, :], src, cos, sin, moved_value(counts, step))
                        else:
                            dve.wait_ge(w_loaded["self"], loads_through["self"][counts.li])
                            dve.tensor_tensor(qk_f32[:, :, :], src, bias["qkv"][:, 0:2 * D].rearrange("p (h d) -> p h d", d=HD), ALU.add).then_inc(moved, 1)
                            counts.wait_moved(dve, step)
                        split(counts, s, [(qk_f32[:, t * H:t * H + H, :], P, j, t) for t in range(2)])
                    elif blk.kind == "self" and blk.qkv_bias:
                        buf, moved = counts.wait_filled(dve, step)
                        vb = bias["qkv"][:, 2 * D:3 * D].rearrange("p (h d) -> p h d", d=HD)
                        for c in range(TC):
                            ins = dve.tensor_tensor(v_one[s][:, c, :, 0:HD], buf[:, c * D:c * D + D].rearrange("p (h d) -> p h d", d=HD), vb, ALU.add)
                        ins.then_inc(moved, 1)
                    elif blk.kind == "cross" and j == 0:
                        buf, moved = counts.wait_filled(dve, step)
                        q = qk_f32[:, :, :].rearrange("p (c h) d -> p c h d", c=TC)
                        src = buf[:, :].rearrange("p (c h d) -> p c h d", c=TC, d=HD)
                        if blk.rope:
                            cos, sin = (t[:, :, :].unsqueeze(2).to_broadcast([P, TC, H, HD]) for t in (cos_t, sin_t))
                            rotate(counts, q, src, cos, sin, moved_value(counts, step))
                        elif blk.qkv_bias:
                            dve.wait_ge(w_loaded["cross"], loads_through["cross"][counts.li])
                            qb = bias["cq"][:, :].rearrange("p (h d) -> p h d", d=HD).unsqueeze(1).to_broadcast([P, TC, H, HD])
                            dve.tensor_tensor(q, src, qb, ALU.add).then_inc(moved, 1)
                            counts.wait_moved(dve, step)
                        else:
                            dve.tensor_copy(q, src).then_inc(moved, 1)
                            counts.wait_moved(dve, step)
                        split(counts, s, [(q[:, c, :, :], P, c, 0) for c in range(TC)])
                    elif blk.kind == "cross":
                        buf, moved = counts.wait_filled(dve, step)
                        src = buf[0:CTX, 0:D].rearrange("p (h d) -> p h d", d=HD)
                        v = buf[0:CTX, D:2 * D].rearrange("p (h d) -> p h d", d=HD)
                        ck = qk_f32[0:CTX, 0:H, :]
                        if blk.qkv_bias:
                            cb = bias["ckv"][0:CTX, :].rearrange("p (h d) -> p h d", d=HD)
                            dve.tensor_tensor(ck, src, cb[:, 0:H, :], ALU.add)
                            dve.tensor_tensor(v_one[s][0:CTX, 0, :, 0:HD], v, cb[:, H:2 * H, :], ALU.add).then_inc(moved, 1)
                        elif blk.rope:
                            cos, sin = (t[0:CTX, 0, :].unsqueeze(1).to_broadcast([CTX, H, HD]) for t in (cos_t, sin_t))
                            rotate(counts, ck, src, cos, sin, None)
                            dve.tensor_copy(v_one[s][0:CTX, 0, :, 0:HD], v).then_inc(moved, 1)
                        else:
                            dve.tensor_copy(ck, src)
                            dve.tensor_copy(v_one[s][0:CTX, 0, :, 0:HD], v).then_inc(moved, 1)
                        counts.wait_moved(dve, step)
                        split(counts, s, [(ck, CTX, 0, 1)])

                def maximum(counts, k, s, blk, u):
                    step = (k, s, "S", u)
                    b = counts.wait_scores(dve, step)
                    if blk.kind == "self":
                        src, n = score[b][:, :, :].rearrange("p c (h k) -> p c h k", h=2), 2
                    else:
                        src, n = score[b][:, :, 0:4 * CTXP].rearrange("p c (h k) -> p c h k", h=4)[:, :, :, 0:CTX], 4
                    dve.tensor_reduce(row_max[s][:, :, n * u:n * u + n], src, AX_X, ALU.max).then_inc(max_done[b], 1)

                def negate_maximum(counts, k, s, blk):
                    for u in (score_uses(blk) - 2, score_uses(blk) - 1):
                        b, n_max, _, _ = counts.plan.score[(k, s, "S", u)]
                        dve.wait_ge(max_done[b], counts.val(f"max{b}", n_max + 1))
                    src = row_max[s][:, :, :].rearrange("p c (q two) -> p c two q", two=2)
                    dst = max_tok[s][:, :, :].rearrange("p c (two n) -> p c two n", two=2)
                    link(counts, dve.tensor_scalar(dst[:, :, :, 0:PAIRS], src, -1.0, None, ALU.mult))
                    for c in range(TC):
                        ins = dve.scalar_tensor_tensor(out=dst[:, c, :, PAIRS:2 * PAIRS], in0=src[:, c], scalar=-1.0,
                                                       in1=dst[:, c, :, 0:PAIRS].bitcast(F32), op0=ALU.mult, op1=ALU.subtract)
                    ins.then_inc(max_tok_ready[s], 1)

                def spread_maximum(counts, k, s):
                    step = (k, s, "maxT", 0)
                    buf, moved = counts.wait_filled(dve, step)
                    dve.tensor_copy(maxT[s][:, :], buf[:, 0:S]).then_inc(moved, 1)
                    counts.wait_moved(dve, step)
                    for t in range(2):
                        rows = slice(64 * t, 64 * t + 2 * PAIRS)
                        ins = dve.tensor_copy(q_stack[s][rows, :, :], maxT[s][rows, :].bitcast(F32).unsqueeze(1).to_broadcast([2 * PAIRS, PAIRS, S]))
                    ins.then_inc(max_rows_ready[s], 1)

                def divide(counts, k, s, c):
                    buf, moved = counts.wait_filled(dve, (k, s, "oX", c))
                    heads = buf[:, :].rearrange("p (h v) -> p h v", v=VW)
                    link(counts, dve.reciprocal(rsum[s][:, c, :], heads[:, :, HD]))
                    dve.tensor_tensor(at[s][:, c, :].rearrange("p (h d) -> p h d", d=HD), heads[:, :, 0:HD],
                                      rsum[s][:, c, :].unsqueeze(2).to_broadcast([P, H, HD]), ALU.mult).then_inc(moved, 1)

                def residual(counts, k, s, blk):
                    step = (k, s, "down" if blk.kind == "mlp" else "out", 0)
                    buf, moved = counts.wait_filled(dve, step)
                    src = buf[:, :].rearrange("p (c d) -> p c d", c=TC)
                    old = x_in[s] if counts.first(k) else x[s]
                    if blk.out_bias and blk.gate is not None:
                        dve.wait_ge(w_loaded[blk.kind], loads_through[blk.kind][counts.li])
                        dve.tensor_tensor(delta[s][:, :, :], src, bias[out_bias[blk.kind]][:, :].unsqueeze(1).to_broadcast([P, TC, D]), ALU.add).then_inc(moved, 1)
                    elif blk.out_bias:
                        dve.tensor_tensor(delta[s][:, :, :], src, old[:, :, :], ALU.add).then_inc(moved, 1)
                    elif blk.gate is not None:
                        dve.wait_ge(gate_loaded[s], gates_through(counts, k))
                        dve.tensor_tensor(delta[s][:, :, :], src, gate[s][:, blk.gate, :].unsqueeze(1).to_broadcast([P, TC, D]), ALU.mult).then_inc(moved, 1)
                    else:
                        if counts.first(k):
                            dve.wait_ge(x_stored[s], stored_before(counts, k))
                        dve.tensor_tensor(x[s][:, :, :], src, old[:, :, :], ALU.add).then_inc(moved, 1)

                for li in range(len(LAYERS)):
                    with dve.Fori(0, ITERS) as it:
                        counts = Counts(li, it)
                        links["n"] = 0
                        splits.update({s: 0 for s in range(SLOTS)})
                        for k, s, name, j in counts.plan.steps:
                            blk = counts.layer.all[k]
                            if name == "ln":
                                statistics(counts, k, s)
                            elif name == "nx":
                                normalise(counts, k, s)
                            elif name == "cn" and blk.ctx == "norm":
                                context_norm(counts, k, s)
                            elif name == "qkv":
                                inputs(counts, k, s, blk, j)
                            elif name == "S":
                                maximum(counts, k, s, blk, j)
                            elif name == "mx":
                                negate_maximum(counts, k, s, blk)
                            elif name == "maxT":
                                spread_maximum(counts, k, s)
                            elif name == "oX":
                                divide(counts, k, s, j)
                            elif name in ("out", "down"):
                                residual(counts, k, s, blk)
                        assert links["n"] == counts.plan.count["link"], (li, links["n"], counts.plan.count["link"])


def kernel(**inputs):
    import numpy as np
    import concourse.bacc as bacc
    from concourse.bass_utils import run_bass_kernel_spmd

    def get(name):
        return np.ascontiguousarray(inputs[name])

    def turned(name):
        return np.ascontiguousarray(np.asarray(inputs[name]).T)

    def columns(v):
        return np.ascontiguousarray(np.asarray(v).reshape(-1, P).T)

    L = {n: f"L{n}_xcond_" for n in range(4)}
    inv_freq = 1.0 / 10000.0 ** (np.arange(0, HD, 2, dtype=np.float32) / HD)
    angle = np.outer(np.arange(S, dtype=np.float32), inv_freq).astype(np.float32)
    cos = np.concatenate([np.cos(angle)] * 2, axis=-1).astype(np.float32)
    sin = np.concatenate([-np.sin(angle), np.sin(angle)], axis=-1).astype(np.float32)

    ada_b, mod_b = np.asarray(inputs[L[0] + "adaLN_b"]), np.asarray(inputs[L[2] + "b_mod"])
    ssq, sskv = np.asarray(inputs[L[1] + "bss_q"]), np.asarray(inputs[L[1] + "bss_kv"])
    ln_b = [np.asarray(inputs[L[3] + f"ln{i}_b"]) for i in (1, 2, 3)]

    def part(v, i):
        return v[i * D:(i + 1) * D]

    mod_bias = np.concatenate([part(ada_b, 1), part(ada_b, 0), part(ada_b, 4), part(ada_b, 3), part(ada_b, 7), part(ada_b, 6),
                               ssq, sskv, part(mod_b, 1), part(mod_b, 0), part(mod_b, 4), part(mod_b, 3)] + ln_b)
    gate_bias = np.concatenate([part(ada_b, 2), part(ada_b, 5), part(ada_b, 8), part(mod_b, 2), part(mod_b, 5)])
    norm_w = np.concatenate([np.asarray(inputs[L[0] + n]) for n in ("norm1_w", "normc_w", "norm2_w")])
    mask = np.asarray(inputs["mask_SxS_bk0"])
    kmask = np.asarray(inputs["mask_BxS2_bf1"])

    arrays = {
        "x": get("x"), "ctx": get("ctx_1024"), "condT": turned("cond_1024"),
        "mask": np.ascontiguousarray(mask), "maskT": np.ascontiguousarray(mask.T),
        "kmask": np.ascontiguousarray(kmask), "kmaskT": np.ascontiguousarray(kmask.T),
        "ident": np.eye(P, dtype=np.float32),
        "cos": np.ascontiguousarray(cos.reshape(TC, P, HD).transpose(1, 0, 2)),
        "sin": np.ascontiguousarray(sin.reshape(TC, P, HD).transpose(1, 0, 2)),
        "mod_bias": columns(mod_bias), "gate_bias": gate_bias.reshape(1, -1), "norm_w": columns(norm_w).reshape(P, 3, FC),
        "adaln0": get(L[0] + "adaLN_W"), "adaln1q": get(L[1] + "Wss_q"), "adaln1kv": get(L[1] + "Wss_kv"), "adaln2": get(L[2] + "W_mod"),
        "adaln3a": turned(L[3] + "ln1_w"), "adaln3b": turned(L[3] + "ln2_w"), "adaln3c": turned(L[3] + "ln3_w"),
        "L0_qkv": get(L[0] + "qkv_W"), "L0_so": get(L[0] + "attn_out_W"), "L0_cq": get(L[0] + "cq_W"), "L0_ck": get(L[0] + "ck_W"),
        "L0_cv": get(L[0] + "cv_W"), "L0_co": get(L[0] + "co_W"), "L0_w1": get(L[0] + "mlp_W1"), "L0_w2": get(L[0] + "mlp_W2"),
        "L0_b1": columns(inputs[L[0] + "mlp_b1"]), "L0_b2": get(L[0] + "mlp_b2"),
        "L1_cq": get(L[1] + "Wq"), "L1_ckv": get(L[1] + "Wkv"), "L1_co": get(L[1] + "Wp"),
        "L1_bq": get(L[1] + "bq"), "L1_bkv": get(L[1] + "bkv"), "L1_bo": get(L[1] + "bp"),
        "L2_qkv": get(L[2] + "W_qkv"), "L2_so": get(L[2] + "W_proj"), "L2_cq": get(L[2] + "W_qc"), "L2_ckv": get(L[2] + "W_kvc"),
        "L2_co": get(L[2] + "W_cproj"), "L2_w1": get(L[2] + "W_mlp1"), "L2_w2": get(L[2] + "W_mlp2"),
        "L2_bqkv": get(L[2] + "b_qkv"), "L2_bso": get(L[2] + "b_proj"), "L2_bq": get(L[2] + "b_qc"), "L2_bkv": get(L[2] + "b_kvc"),
        "L2_bo": get(L[2] + "b_cproj"), "L2_b1": columns(inputs[L[2] + "b_mlp1"]), "L2_b2": get(L[2] + "b_mlp2"),
        "L3_qkv": turned(L[3] + "qkv_w"), "L3_so": turned(L[3] + "sa_out_w"), "L3_cq": turned(L[3] + "q_w"), "L3_ck": turned(L[3] + "k_w"),
        "L3_cv": turned(L[3] + "v_w"), "L3_co": turned(L[3] + "ca_out_w"), "L3_w1": turned(L[3] + "ffn_w1"), "L3_w2": turned(L[3] + "ffn_w2"),
        "L3_b1": columns(inputs[L[3] + "ffn_b1"]), "L3_b2": get(L[3] + "ffn_b2"),
    }
    nc = bacc.Bacc("TRN2", target_bir_lowering=False, num_devices=1)
    feed, aps = {}, {}
    for name, v in arrays.items():
        feed[f"in_{name}"] = v
        aps[name] = nc.dram_tensor(f"in_{name}", v.shape, mybir.dt.from_np(v.dtype), kind="ExternalInput").ap()
    aps["out"] = nc.dram_tensor("out_x", (B, S, D), F32, kind="ExternalOutput").ap()
    dit_stack(nc, aps)
    r = run_bass_kernel_spmd(nc, [feed], core_ids=[0])
    return r.results[0]["out_x"]
```

```python
from contextlib import ExitStack

import concourse.bass as bass
from concourse import mybir

F32 = mybir.dt.float32
F32R = mybir.dt.float32r
BF16 = mybir.dt.bfloat16
U8 = mybir.dt.uint8
ALU = mybir.AluOpType
ACT = mybir.ActivationFunctionType
AX_X = mybir.AxisListType.X

P = 128
B, S, D = 16, 256, 256
H, HD = 16, 16
CTX = 77
CTXP = CTX + 1
FF = 4 * D
TC = S // P
FC = D // P
FFC = FF // P
PAIRS = H // 2
SLOTS = 2
ROUNDS = B // SLOTS
PER_LOOP = 4
ITERS = ROUNDS // PER_LOOP
SCALE = HD ** -0.5
MASKED = 2.0 ** 120
VW = 32
HG = P // VW
NG = H // HG
HALVES = 2


class Block:

    def __init__(self, kind, mod=None, rope=False, mask=False, gate=None, qkv_bias=False, out_bias=False,
                 ctx=None, ctx_mod=None, gelu=None):
        self.kind, self.mod, self.rope, self.mask, self.gate = kind, mod, rope, mask, gate
        self.qkv_bias, self.out_bias, self.ctx, self.ctx_mod, self.gelu = qkv_bias, out_bias, ctx, ctx_mod, gelu


class Layer:
    def __init__(self, name, eps, rope_period, mod0, mods, gate0, gates, blocks):
        self.name, self.eps, self.rope_period, self.blocks = name, eps, rope_period, blocks
        self.mod0, self.mods, self.gate0, self.gates = mod0, mods, gate0, gates
        self.nb = len(blocks)
        self.all = blocks * PER_LOOP
        self.attn = [k for k, b in enumerate(self.all) if b.kind != "mlp"]


LAYERS = [
    Layer("L0", 1e-5, P, 0, 3, 0, 3, [
        Block("self", mod=0, rope=True, mask=True, gate=0),
        Block("cross", mod=1, gate=1, mask=True, ctx="raw"),
        Block("mlp", mod=2, gate=2, out_bias=True, gelu="tanh")]),
    Layer("L1", 1e-5, None, 3, 2, None, 0, [
        Block("cross", mod=0, qkv_bias=True, out_bias=True, ctx="norm", ctx_mod=1)]),
    Layer("L2", 1e-6, None, 5, 2, 3, 2, [
        Block("self", mod=0, qkv_bias=True, out_bias=True, gate=0),
        Block("cross", qkv_bias=True, out_bias=True, ctx="norm"),
        Block("mlp", mod=1, gate=1, out_bias=True, gelu="tanh")]),
    Layer("L3", 1e-5, S, 7, 3, None, 0, [
        Block("self", mod=0, rope=True),
        Block("cross", mod=1, rope=True, ctx="raw"),
        Block("mlp", mod=2, out_bias=True, gelu="erf")]),
]
N_MOD = 10
N_GATE = 5


def score_uses(blk):
    return PAIRS if blk.kind == "self" else PAIRS // 2


def block_parts(layer, k):
    blk = layer.all[k]
    entry = [("cp", 0)] if k % layer.nb == 0 else []
    entry += [("ln", 0), ("nx", 0), ("xT", 0)]
    if blk.kind == "mlp":
        return [], entry, [("up", 0), ("up", 1), ("xb", 0)] + [("up", j) for j in range(2, FFC // 2)], [("down", c) for c in range(TC)]
    n = score_uses(blk) // HALVES
    if blk.kind == "cross":
        context = [("cn", 0), ("cT", 0), ("qkv", 1)] + [("stkK", j) for j in range(2)]
        middle = [("qkv", 0), ("stkQ", 0), ("stkQ", 1), ("S", 0), ("S", 1), ("stkQ", 2), ("stkQ", 3), ("mx", 0)]
        middle += [("S", 2), ("maxT", 0), ("S", 3), ("mx", 1), ("ST", 0), ("maxT", 1), ("ST", 1)]
    else:
        context = []
        middle = [("qkv", 0), ("qkv", 1)] + [(name, j) for j in range(2) for name in ("stkQ", "stkK")]
        middle += [("S", 0), ("S", 1), ("qkv", 2), ("stkQ", 2), ("stkK", 2), ("S", 2), ("S", 3), ("mx", 0), ("stkQ", 3), ("stkK", 3)]
        middle += [("S", 4), ("maxT", 0), ("S", 5), ("S", 6), ("ST", 0), ("S", 7), ("mx", 1), ("ST", 1), ("ST", 2), ("maxT", 1), ("ST", 3)]
    if blk.out_bias:
        middle.insert(middle.index(("S", 0)), ("xb", 0))
    if blk.kind == "cross":
        middle += [("W", 0), ("ST", 2), ("W", 1), ("pv", 0), ("ST", 3), ("W", 2), ("oX", 0), ("W", 3)]
    else:
        middle += [("W", 0), ("ST", 4), ("ST", 5), ("W", 1), ("pv", 0), ("ST", 6), ("oX", 0), ("W", 2), ("ST", 7), ("atT", 0), ("W", 3)]
    return context, entry, middle, [("pv", 1), ("oX", 1), ("atT", 1), ("out", 0)]


def chain(layer):
    parts = [[[(k, *step) for step in part] for part in block_parts(layer, k)] for k in range(len(layer.all))]
    out, entered = [], set()
    for k, (context, entry, middle, last) in enumerate(parts):
        blk = layer.all[k]
        if k not in entered:
            out += entry[:-1] + context + entry[-1:]
        elif blk.kind != "cross":
            pass
        else:
            out += entry
        out += middle
        if k + 1 < len(parts) and blk.kind == "mlp":
            out += parts[k + 1][1]
            entered.add(k + 1)
        if blk.kind == "self":
            norm, products, stacks = parts[k + 1][0][:2], parts[k + 1][0][2:3], parts[k + 1][0][3:]
            out[-1:-1] = norm
            out += last[:2] + products + last[2:] + stacks
            entered.add(k + 1)
        else:
            out += last
    return out


def needs(layer, k, name, j):
    blk = layer.all[k]
    n = score_uses(blk) // HALVES if blk.kind != "mlp" else 0
    entry = (k, "xT", 0)
    if name == "ln":
        return [] if k % layer.nb == 0 else [(k - 1, "out", 0)]
    if name == "qkv":
        return [(k, "cT", 0)] if blk.kind == "cross" and j == 1 else [entry]
    if name == "ST":
        return [(k, "maxT", j // n)]
    if name == "W":
        return [(k, "ST", group_fills(blk, j)[-1])] + ([(k, "pv", j // 2 - 1)] if j == 2 else [])
    if name == "S":
        return [(k, "stkQ", j // 2 if blk.kind == "self" else j), (k, "stkK", j // 2)]
    return {"nx": [(k, "ln", 0)], "xT": [(k, "nx", 0)], "cT": [(k, "cn", 0)], "up": [entry], "down": [(k, "up", FFC // 2 - 1)],
            "stkQ": [(k, "qkv", 1 if blk.kind == "self" else 0)], "stkK": [(k, "qkv", 1)],
            "mx": [(k, "S", (j + 1) * n - 1)], "maxT": [(k, "mx", j)],
            "pv": [(k, "W", 2 * j + 1)], "oX": [(k, "pv", j)], "atT": [(k, "oX", j)], "out": [(k, "atT", 1)]}.get(name, [])


def shares(layer, k, name, j):
    blk = layer.all[k]
    whole = blk.kind == "self"
    mask = 0.5 if blk.mask else 0.0
    if name == "qkv":
        if whole and j == 2:
            return [("pe", 1.8), ("dve", 0.7) if blk.qkv_bias else ("act", 0.6)]
        if not whole and j == 1:
            return [("pe", 1.8), ("dve", 2.2 if blk.rope else 1.5)]
        return [("pe", 1.8), ("dve", 3.3 if blk.rope else 2.0)]
    return {"cp": [("act", 0.2)], "ln": [("dve", 1.2), ("pool", 0.7)], "nx": [("dve", 0.7)],
            "xT": [("pe", 0.5), ("act", 0.6 if blk.mod is None else 1.0)],
            "cn": [("dve", 1.8 if blk.ctx == "norm" else 0.0)], "cT": [("pe", 0.2), ("act", 0.3)],
            "stkQ": [("pe", 0.45), ("act", 0.5)], "stkK": [("pe", 0.45), ("act", 1.0)] if whole else [("pe", 0.3), ("act", 0.7)],
            "S": [("pe", 0.45 + 0.9 * mask), ("dve", 1.15)] if whole else [("pe", 0.3 + mask / 2), ("dve", 0.75)], "mx": [("dve", 0.35)],
            "maxT": [("pe", 0.3), ("dve", 1.0), ("act", 0.4)], "ST": [("pe", 0.45 + 0.9 * mask * whole), ("act", 0.95)], "W": [("pe", 1.0 if whole else 0.5)],
            "pv": [("act", 0.5)], "oX": [("pe", 0.5), ("dve", 0.65)], "atT": [("pe", 0.3), ("act", 0.4)] if whole else [("pe", 0.5), ("act", 0.6)],
            "out": [("pe", 1.8), ("dve", 0.7 if blk.gate is None else 1.3)], "xb": [("pool", 2.0)],
            "up": [("pe", 1.8), ("act", 0.8)], "down": [("pe", 3.5), ("dve", 0.4 if blk.gate is None else 0.7)]}[name]


HOP = 0.25
TABLE = 1.3
GEN = 3
SCORES = 2
BEAM = 40
ENGINES = ("pe", "act", "dve", "pool")


class Merge:

    def __init__(self):
        self.order = ()
        self.done = (0,) * SLOTS
        self.end = ((),) * SLOTS
        self.free = {engine: 0.0 for engine in ENGINES}
        self.rings = {"gen": (-HOP,) * GEN, "score": (-HOP,) * SCORES}
        self.owner = None
        self.table = None

    def then(self, s, step):
        if step.name == "ST" and self.owner not in (None, s):
            return None
        new = Merge()
        new.order = (self.order, s)
        t = max([0.0] + [self.end[s][i] + HOP for i in step.needs])
        if step.ring:
            t = max(t, self.rings[step.ring][0] + HOP)
        change = step.name in ("ST", "up") and self.table not in (None, step.name)
        new.free = dict(self.free)
        for engine, share in step.shares:
            t = max(t, new.free[engine]) + share + (TABLE if change and engine == "act" else 0.0)
            new.free[engine] = t
            t += HOP
        t -= HOP
        new.rings = {**self.rings, step.ring: self.rings[step.ring][1:] + (t,)} if step.ring else self.rings
        new.table = step.name if step.name in ("ST", "up") else self.table
        new.owner = s if step.name == "ST" else None if (step.name, step.j) == ("pv", 1) else self.owner
        new.end = tuple(e + (t,) if i == s else e for i, e in enumerate(self.end))
        new.done = tuple(n + (i == s) for i, n in enumerate(self.done))
        return new

    def cost(self):
        return self.free["pe"] + 0.5 * self.free["dve"] + 0.3 * self.free["act"] + 0.25 * sum(e[-1] for e in self.end if e)


class Step:
    def __init__(self, layer, position, k, name, j):
        self.k, self.name, self.j = k, name, j
        self.shares = shares(layer, k, name, j)
        self.needs = [position[need] for need in needs(layer, k, name, j)]
        self.ring = "gen" if name in GEN_STEPS else "score" if name in ("S", "ST") else None


def schedule(layer):
    position = {step: i for i, step in enumerate(chain(layer))}
    steps = [Step(layer, position, *step) for step in chain(layer)]
    merges = [Merge()]
    for _ in range(SLOTS * len(steps)):
        best = {}
        for merge in merges:
            for s in range(SLOTS):
                new = merge.then(s, steps[merge.done[s]]) if merge.done[s] < len(steps) else None
                key = new and (new.done, new.owner)
                if new and (key not in best or new.cost() < best[key].cost()):
                    best[key] = new
        merges = sorted(best.values(), key=Merge.cost)[0:BEAM]
    order, link = [], min(merges, key=lambda merge: max(merge.free.values())).order
    while link:
        link, s = link
        order.append(s)
    at = [0] * SLOTS
    result = []
    for s in reversed(order):
        step = steps[at[s]]
        at[s] += 1
        result.append((step.k, s, step.name, step.j))
    return result


def head_group(blk, u):
    return u // 2 if blk.kind == "self" else u


def group_complete(blk, u):
    return blk.kind == "cross" or u % 2 == 1


def chunks_of(blk, h):
    return [h] if blk.kind == "self" else list(range(FC))


def group_fills(blk, g):
    return (2 * g, 2 * g + 1) if blk.kind == "self" else (g,)


FROM_ONE = ("gen0", "gen1", "gen2", "max0", "max1", "exp0", "exp1", "weighed", "pv", "split")
GEN_STEPS = ("xT", "cT", "qkv", "stkQ", "stkK", "maxT", "oX", "atT", "out", "up", "down")
PROBS = 4


class Plan:

    def __init__(self, layer):
        self.layer, self.steps = layer, schedule(layer)
        self.gen = {}
        self.score = {}
        self.probs = {}
        self.weighed = {}
        self.pv = {}
        n_gen = sum(step[2] in GEN_STEPS for step in self.steps)
        depth = GEN if n_gen % GEN == 0 else GEN - 1
        n_gen, users, done = 0, [], {(q, b): 0 for q in ("S", "ST") for b in range(2)}
        fills, reader = [], {}
        for step in self.steps:
            k, s, name, j = step
            if name in GEN_STEPS:
                self.gen[step] = (n_gen % depth, n_gen // depth)
                n_gen += 1
            if name in ("S", "ST"):
                b = len(users) % 2
                before = users[-2] if len(users) > 1 else "ST"
                self.score[step] = (b, done["S", b], done["ST", b], before)
                done[name, b] += 1
                users.append(name)
            if name == "ST":
                n = len(fills)
                self.probs[step] = (n % PROBS, reader[fills[n - PROBS]] + 1 if n >= PROBS else 0)
                fills.append(step)
            if name == "W":
                for u in group_fills(layer.all[k], j):
                    reader[(k, s, "ST", u)] = len(self.weighed)
                self.weighed[step] = len(self.weighed)
                if j == 0:
                    self.pv[(k, s)] = len(self.pv)
        assert n_gen % depth == 0 and len(users) % 2 == 0 and len(fills) % PROBS == 0 and users[-2:] == ["ST", "ST"]
        links = sum(links_of(layer, b) for b in layer.all) * SLOTS
        self.count = {**{f"gen{b}": n_gen // depth if b < depth else 0 for b in range(GEN)}, "max0": done["S", 0], "max1": done["S", 1], "exp0": done["ST", 0], "exp1": done["ST", 1],
                      "score": len(users) // 2, "weighed": len(self.weighed), "pv": HALVES * len(self.pv), "link": links, "block": len(layer.all),
                      "attn": len(layer.attn), "half": HALVES * len(layer.attn), "rows": 2 * HALVES * len(layer.attn), "split": 2 * len(layer.attn), "cnorm": sum(b.ctx == "norm" for b in layer.all),
                      "copies": COPIES[layer.name] * PER_LOOP, "gated": sum(b.gate is not None and b.out_bias for b in layer.all),
                      "biased": sum(b.out_bias for b in layer.all)}


COPIES = {"L0": 3, "L1": 1, "L2": 1, "L3": 1}


def links_of(layer, blk):
    gated = blk.gate is not None
    n = 2
    if blk.kind == "mlp":
        return n + TC * gated
    n += gated
    parts = 2
    n += parts * ((1 if blk.rope else 0) + 1)
    if blk.rope and blk.kind == "cross":
        n += 1
    if blk.ctx == "norm":
        n += 2
    return n + HALVES + HALVES


def dit_stack(nc, a):
    plans = [Plan(layer) for layer in LAYERS]

    base, total = [], {key: 0 for key in plans[0].count}
    for plan in plans:
        base.append(dict(total))
        for key in total:
            total[key] += ITERS * plan.count[key]

    keep = ExitStack()
    with keep:
        def sb(name, shape, dt=F32, stack=keep):
            return stack.enter_context(nc.sbuf_tensor(name, shape, dt))

        def sem(name):
            return keep.enter_context(nc.semaphore(name))

        score = [keep.enter_context(nc.psum_tensor(f"score{b}", [P, 2, 512], F32)) for b in range(2)]
        pv = keep.enter_context(nc.psum_tensor("pv", [P, NG // HALVES, S], F32))
        gen = [keep.enter_context(nc.psum_tensor(f"gen{b}", [P, 512], F32)) for b in range(GEN)]

        ident = sb("ident", [P, P])
        ident_bf = sb("ident_bf", [P, P], BF16)
        ones_bf = sb("ones_bf", [1, P], BF16)
        minus_half = sb("minus_half", [P, TC])
        cos_t = sb("cos_t", [P, TC, HD])
        sin_t = sb("sin_t", [P, TC, HD])
        mod_all = sb("mod_all", [P, B, N_MOD * 2 * FC])
        maskq = sb("maskq", [P, TC, S], BF16)
        maskk = sb("maskk", [P, TC, S], BF16)
        kbias_row = sb("kbias_row", [1, B, CTX], BF16)
        kbias_col = sb("kbias_col", [CTX, B])
        gates_dram = nc.dram_tensor("gates_scratch", (B, N_GATE * D), F32, kind="Internal").ap()
        x_dram = nc.dram_tensor("x_scratch", (B, S, D), F32, kind="Internal").ap()

        def per_slot(name, shape, dt=F32):
            return [sb(f"{name}{s}", shape, dt) for s in range(SLOTS)]

        krow = per_slot("krow", [1, 4, CTXP], BF16)
        qk_tok = per_slot("qk_tok", [P, TC, 2, H, 4, HD], F32R)
        k_stack = per_slot("k_stack", [P, PAIRS, 2, S], F32R)
        v_one = per_slot("v_one", [P, TC, H, VW])
        max_tok = per_slot("max_tok", [P, TC, P], F32R)
        init_done = sem("init_done")
        init_zeroed = [sem(f"init_zeroed{s}") for s in range(SLOTS)]

        def prepare(eng, s):
            parts = qk_tok[s][:, :, :, :, :, :].bitcast(F32)
            for c in range(TC):
                eng.memset(parts[:, c, :, :, 0, :], 0.0)
            eng.memset(k_stack[s][:, :, :, :].bitcast(F32), 0.0)
            eng.memset(max_tok[s][:, :, :].bitcast(F32), 0.0)
            eng.memset(krow[s][:, :, :], 0.0)
            eng.memset(v_one[s][:, :, :, :], 0.0).then_inc(init_zeroed[s], 1)
            eng.wait_ge(init_zeroed[s], 1)
            eng.memset(v_one[s][:, :, :, HD:HD + 1], 1.0)
            for p in range(PAIRS):
                for part in range(2):
                    ins = eng.memset(parts[:, :, 1, 2 * p:2 * p + 2, 0, part * PAIRS + p], 1.0)
            ins.then_inc(init_done, 1)

        const_loaded = sem("const_loaded")
        adaln_loaded = {key: sem(f"adaln_loaded_{key}") for key in ("L0", "L1q", "L1kv", "L2", "L3a", "L3b", "L3c")}
        silu_exp_done = sem("silu_exp_done")
        cond_ready = sem("cond_ready")
        pro_link = sem("pro_link")
        mod_sum_done = sem("mod_sum_done")
        gate_sum_done = sem("gate_sum_done")
        gates_ready = sem("gates_ready")
        gates_stored = sem("gates_stored")

        with ExitStack() as pro:
            condT = sb("condT", [P, FC, B], F32, pro)
            siluT = sb("siluT", [P, FC, B], F32, pro)
            expT = sb("expT", [P, FC, B], F32, pro)
            ada = {"L0": sb("ada0", [P, FC, 9 * D], F32, pro), "L1q": sb("ada1q", [P, FC, 2 * D], F32, pro),
                   "L1kv": sb("ada1kv", [P, FC, 2 * D], F32, pro), "L2": sb("ada2", [P, FC, 6 * D], F32, pro),
                   "L3a": sb("ada3a", [P, FC, 2 * D], F32, pro), "L3b": sb("ada3b", [P, FC, 2 * D], F32, pro),
                   "L3c": sb("ada3c", [P, FC, 2 * D], F32, pro)}
            mod_bias = sb("mod_bias", [P, N_MOD * 2 * FC], F32, pro)
            norm_w = sb("norm_w", [P, 3, FC], F32, pro)
            gate_bias = sb("gate_bias", [1, N_GATE * D], F32, pro)
            ones16 = sb("ones16", [1, B], F32, pro)
            gates = sb("gates", [B, N_GATE * D], F32, pro)
            mask_u8 = sb("mask_u8", [P, TC, S], U8, pro)
            maskT_u8 = sb("maskT_u8", [P, TC, S], U8, pro)
            krow_u8 = sb("krow_u8", [1, B, CTX], U8, pro)
            kcol_u8 = sb("kcol_u8", [CTX, B], U8, pro)

            mod_src = [("L0", D, 0, False), ("L0", 4 * D, 3 * D, False), ("L0", 7 * D, 6 * D, False),
                       ("L1q", 0, D, True), ("L1kv", 0, D, True),
                       ("L2", D, 0, True), ("L2", 4 * D, 3 * D, True),
                       ("L3a", 0, D, False), ("L3b", 0, D, False), ("L3c", 0, D, False)]
            gate_src = [("L0", 2 * D, False), ("L0", 5 * D, False), ("L0", 8 * D, False),
                        ("L2", 2 * D, True), ("L2", 5 * D, True)]
            const_loads = [(ident[:, :], a["ident"]), (cos_t[:, :, :], a["cos"]), (sin_t[:, :, :], a["sin"]),
                           (condT[:, :, :], a["condT"].rearrange("(c p) b -> p c b", p=P)),
                           (mod_bias[:, :], a["mod_bias"]), (norm_w[:, :, :], a["norm_w"]),
                           (gate_bias[:, :], a["gate_bias"]),
                           (mask_u8[:, :, :], a["mask"].rearrange("(c p) k -> p c k", p=P)),
                           (maskT_u8[:, :, :], a["maskT"].rearrange("(c p) k -> p c k", p=P)),
                           (krow_u8[:, :, :], a["kmask"].rearrange("(o b) k -> o b k", o=1)),
                           (kcol_u8[:, :], a["kmaskT"])]
            ada_loads = [("L0", "adaln0"), ("L1q", "adaln1q"), ("L1kv", "adaln1kv"), ("L2", "adaln2"),
                         ("L3a", "adaln3a"), ("L3b", "adaln3b"), ("L3c", "adaln3c")]

            with nc.Block() as block:
                @block.sync
                def _(sp):
                    for dst, src in const_loads:
                        sp.dma_start(dst, src).then_inc(const_loaded, 16)
                    for key, name in ada_loads:
                        sp.dma_start(ada[key][:, :, :], a[name].rearrange("(c p) n -> p c n", p=P)).then_inc(adaln_loaded[key], 16)
                    sp.wait_ge(gates_ready, 3)
                    sp.dma_start(gates_dram, gates[:, :]).then_inc(gates_stored, 16)
                    sp.wait_ge(gates_stored, 16)

                @block.scalar
                def _(act):
                    act.wait_ge(const_loaded, 16 * len(const_loads))
                    act.activation(expT[:, :, :], condT[:, :, :], ACT.Exp, scale=-1.0).then_inc(silu_exp_done, 1)

                @block.vector
                def _(dve):
                    links = [0]

                    def link(ins):
                        links[0] += 1
                        ins.then_inc(pro_link, 1)
                        dve.wait_ge(pro_link, links[0])

                    for s in range(SLOTS):
                        prepare(dve, s)
                    dve.memset(ones_bf[:, :], 1.0)
                    dve.memset(minus_half[:, :], -0.5)
                    dve.memset(ones16[:, :], 1.0)
                    dve.wait_ge(const_loaded, 16 * len(const_loads))
                    dve.wait_ge(silu_exp_done, 1)
                    link(dve.tensor_scalar(expT[:, :, :], expT[:, :, :], 1.0, None, ALU.add))
                    link(dve.reciprocal(siluT[:, :, :], expT[:, :, :]))
                    dve.tensor_tensor(siluT[:, :, :], siluT[:, :, :], condT[:, :, :], ALU.mult).then_inc(cond_ready, 1)
                    dve.tensor_copy(ident_bf[:, :], ident[:, :])
                    dve.tensor_scalar(maskq[:, :, :], mask_u8[:, :, :], -1.0, MASKED, ALU.add, ALU.mult)
                    dve.tensor_scalar(maskk[:, :, :], maskT_u8[:, :, :], -1.0, MASKED, ALU.add, ALU.mult)
                    dve.tensor_scalar(kbias_row[:, :, :], krow_u8[:, :, :], -1.0, MASKED, ALU.add, ALU.mult)
                    dve.tensor_scalar(kbias_col[:, :], kcol_u8[:, :], -1.0, MASKED * SCALE, ALU.add, ALU.mult)
                    half = N_MOD * 2 * FC // 2
                    for i in range(2):
                        dve.wait_ge(mod_sum_done, i + 1)
                        cols = slice(i * half, (i + 1) * half)
                        bias = mod_bias[:, cols].unsqueeze(1).to_broadcast([P, B, half])
                        link(dve.tensor_tensor(mod_all[:, :, cols], gen[i][:, 0:half * B].rearrange("p (n b) -> p b n", b=B),
                                               bias, ALU.add))
                    pairs = mod_all[:, :, :].rearrange("p b (m two c) -> p b m two c", two=2, c=FC)
                    for m in range(N_MOD):
                        scale = pairs[:, :, m, 0, :]
                        link(dve.tensor_scalar(scale, scale, 1.0, None, ALU.add))
                        if m < 3:
                            w = norm_w[:, m, :].unsqueeze(1).to_broadcast([P, B, FC])
                            link(dve.tensor_tensor(scale, scale, w, ALU.mult))
                    for i, (bank, lo, hi) in enumerate(((score[1][:, 0], 0, 512), (score[1][:, 1], 512, 1024), (score[0][:, 0], 1024, 1280))):
                        dve.wait_ge(gate_sum_done, i + 1)
                        dve.tensor_copy(gates[:, lo:hi], bank[0:B, 0:hi - lo]).then_inc(gates_ready, 1)

                @block.tensor
                def _(pe):
                    pe.wait_ge(const_loaded, 16 * len(const_loads))
                    pe.wait_ge(cond_ready, 1)
                    half = N_MOD * 2 * FC // 2
                    for n in range(N_MOD * 2 * FC):
                        m, kind, fc = n // (2 * FC), n // FC % 2, n % FC
                        key, scale0, shift0, silu = mod_src[m]
                        col = (shift0 if kind else scale0) + fc * P
                        pe.wait_ge(adaln_loaded[key], 16)
                        c = siluT if silu else condT
                        out = gen[n // half][:, n % half * B:n % half * B + B]
                        for kc in range(FC):
                            mm = pe.matmul(out, ada[key][:, kc, col:col + P], c[:, kc, :], start=kc == 0, stop=kc == FC - 1)
                        if n % half == half - 1:
                            mm.then_inc(mod_sum_done, 1)
                    banks = [score[1][:, 0], score[1][:, 1], score[0][:, 0]]
                    for g, (key, col, silu) in enumerate(gate_src):
                        c = siluT if silu else condT
                        out = banks[g // 2][0:B, g % 2 * D:g % 2 * D + D]
                        for kc in range(FC):
                            pe.matmul(out, c[:, kc, :], ada[key][:, kc, col:col + D], start=kc == 0, stop=False)
                        mm = pe.matmul(out, ones16[:, :], gate_bias[:, g * D:g * D + D], start=False, stop=True)
                        if g % 2 or g == N_GATE - 1:
                            mm.then_inc(gate_sum_done, 1)

        w = {"qkv": sb("w_qkv", [P, FC, 3 * D]), "so": sb("w_so", [P, FC, D]), "cq": sb("w_cq", [P, FC, D]),
             "ckv": sb("w_ckv", [P, FC, 2 * D]), "co": sb("w_co", [P, FC, D]),
             "w1": sb("w_w1", [P, FC, FF]), "w2": sb("w_w2", [P, FFC, D])}
        bias = {"qkv": sb("b_qkv", [P, 3 * D]), "so": sb("b_so", [P, D]), "cq": sb("b_cq", [P, D]),
                "ckv": sb("b_ckv", [P, 2 * D]), "co": sb("b_co", [P, D]), "b2": sb("b_b2", [P, D])}
        b1 = sb("b_b1", [P, FFC])

        x_in = per_slot("x_in", [P, TC, D])
        x = per_slot("x", [P, TC, D])
        stats = per_slot("stats", [P, TC, 6])
        mean_var = per_slot("mean_var", [P, TC, 2])
        var_eps = per_slot("var_eps", [P, TC])
        rstd = per_slot("rstd", [P, TC])
        xhat = per_slot("xhat", [P, TC, D])
        xnT = per_slot("xnT", [P, FC, S])
        ctx_in = per_slot("ctx_in", [CTX, D])
        c_stats = per_slot("c_stats", [CTX, 6])
        c_mean_var = per_slot("c_mean_var", [CTX, 2])
        c_var_eps = per_slot("c_var_eps", [CTX, 1])
        c_rstd = per_slot("c_rstd", [CTX, 1])
        gated_bias = per_slot("gated_bias", [P, D])
        chat = [t[0:CTX] for t in gated_bias]
        ctxT = per_slot("ctxT", [P, FC, CTX])
        mod = per_slot("mod", [P, 3 * 2 * FC])
        kcol = per_slot("kcol", [CTX, 1])
        gate = per_slot("gate", [P, 3, D])
        q_stack = per_slot("q_stack", [P, PAIRS, S], F32R)
        row_max = per_slot("row_max", [P, TC, H])
        maxT = per_slot("maxT", [P, S], F32R)
        rsum = per_slot("rsum", [P, TC, H])
        at = xhat
        atT = xnT
        hT = per_slot("hT", [P, FFC, S])
        oT = hT
        delta = at
        pause = sb("pause", [P, 1])
        rope_a = bias["qkv"][:, 0:2 * D].rearrange("p (h d) -> p h d", d=HD)
        rope_b = sb("rope_b", [P, 2 * H, HD])
        qk_f32 = sb("qk_f32", [P, 2 * H, HD])
        probs = [sb(f"probs{b}", [P, 4, S]) for b in range(PROBS)]

        weight_loads = [
            {"qkv": ["L0_qkv"], "so": ["L0_so"], "cq": ["L0_cq"], "ckv": ["L0_ck", "L0_cv"], "co": ["L0_co"],
             "w1": ["L0_w1"], "w2": ["L0_w2"]},
            {"cq": ["L1_cq"], "ckv": ["L1_ckv"], "co": ["L1_co"]},
            {"qkv": ["L2_qkv"], "so": ["L2_so"], "cq": ["L2_cq"], "ckv": ["L2_ckv"], "co": ["L2_co"],
             "w1": ["L2_w1"], "w2": ["L2_w2"]},
            {"qkv": ["L3_qkv"], "so": ["L3_so"], "cq": ["L3_cq"], "ckv": ["L3_ck", "L3_cv"], "co": ["L3_co"],
             "w1": ["L3_w1"], "w2": ["L3_w2"]}]
        bias_loads = [
            {"b2": "L0_b2", "b1": "L0_b1"},
            {"cq": "L1_bq", "ckv": "L1_bkv", "co": "L1_bo"},
            {"qkv": "L2_bqkv", "so": "L2_bso", "cq": "L2_bq", "ckv": "L2_bkv", "co": "L2_bo", "b2": "L2_b2", "b1": "L2_b1"},
            {"b2": "L3_b2", "b1": "L3_b1"}]
        block_of = {"qkv": "self", "so": "self", "cq": "cross", "ckv": "cross", "co": "cross", "w1": "mlp", "w2": "mlp",
                    "b2": "mlp", "b1": "mlp"}
        out_bias = {"self": "so", "cross": "co", "mlp": "b2"}
        kinds = ["self", "cross", "mlp"]

        w_loaded = {kind: sem(f"w_loaded_{kind}") for kind in kinds}
        x_loaded = [sem(f"x_loaded{s}") for s in range(SLOTS)]
        ctx_loaded = [sem(f"ctx_loaded{s}") for s in range(SLOTS)]
        gate_loaded = [sem(f"gate_loaded{s}") for s in range(SLOTS)]
        x_stored = [sem(f"x_stored{s}") for s in range(SLOTS)]
        copies_done = [sem(f"copies_done{s}") for s in range(SLOTS)]
        x_ready = [sem(f"x_ready{s}") for s in range(SLOTS)]
        var_ready = [sem(f"var_ready{s}") for s in range(SLOTS)]
        rstd_ready = [sem(f"rstd_ready{s}") for s in range(SLOTS)]
        xhat_ready = [sem(f"xhat_ready{s}") for s in range(SLOTS)]
        c_var_ready = [sem(f"c_var_ready{s}") for s in range(SLOTS)]
        c_rstd_ready = [sem(f"c_rstd_ready{s}") for s in range(SLOTS)]
        chat_ready = [sem(f"chat_ready{s}") for s in range(SLOTS)]
        split_ready = [sem(f"split_ready{s}") for s in range(SLOTS)]
        max_tok_ready = [sem(f"max_tok_ready{s}") for s in range(SLOTS)]
        max_rows_ready = [sem(f"max_rows_ready{s}") for s in range(SLOTS)]
        gated = [sem(f"gated{s}") for s in range(SLOTS)]
        biased = [sem(f"biased{s}") for s in range(SLOTS)]
        gen_full = [sem(f"gen_full{b}") for b in range(GEN)]
        gen_moved = [sem(f"gen_moved{b}") for b in range(GEN)]
        score_full = [sem(f"score_full{b}") for b in range(2)]
        max_done = [sem(f"max_done{b}") for b in range(2)]
        exp_done = [sem(f"exp_done{b}") for b in range(2)]
        weighed = sem("weighed")
        pv_moved = sem("pv_moved")
        dve_link = sem("dve_link")

        def weight_dmas(li, kind):
            out = []
            for key, names in weight_loads[li].items():
                if block_of[key] == kind:
                    width = w[key].shape[2] // len(names)
                    for i, name in enumerate(names):
                        out.append((w[key][:, :, i * width:(i + 1) * width], a[name].rearrange("(c p) n -> p c n", p=P)))
            for key, name in bias_loads[li].items():
                if block_of[key] == kind:
                    out.append((b1[:, :], a[name]) if key == "b1" else (bias[key][:, :], a[name].partition_broadcast(P)))
            return out

        loads_through = {kind: [16 * sum(len(weight_dmas(j, kind)) for j in range(li + 1)) for li in range(len(LAYERS))]
                         for kind in kinds}

        class Counts:

            def __init__(self, li, it):
                self.li, self.it, self.layer, self.plan = li, it, LAYERS[li], plans[li]

            def val(self, what, n):
                start = 1 if what in FROM_ONE else 0
                return self.it * self.plan.count[what] + (base[self.li][what] + n + start)

            def loads(self, k):
                return self.it * (16 * PER_LOOP) + 16 * (self.li * ROUNDS + k // self.layer.nb + 1)

            def copies(self, k):
                return self.val("copies", COPIES[self.layer.name] * (k // self.layer.nb + 1))

            def batch(self, k, s):
                return self.it * (PER_LOOP * SLOTS) + ((k // self.layer.nb) * SLOTS + s)

            def first(self, k):
                return k % self.layer.nb == 0

            def cnorm(self, k):
                return sum(b.ctx == "norm" for b in self.layer.all[0:k + 1])

            def biased(self, k):
                return sum(b.out_bias for b in self.layer.all[0:k + 1])

            def wait_normed(self, eng, k, s):
                eng.wait_ge(xhat_ready[s], self.val("block", k + 1))

            def attn(self, k):
                return self.layer.attn.index(k)

            def wait_moved(self, eng, step):
                b, n = self.plan.gen[step]
                eng.wait_ge(gen_moved[b], self.val(f"gen{b}", n + 1))

            def wait_filled(self, eng, step):
                b, n = self.plan.gen[step]
                eng.wait_ge(gen_full[b], self.val(f"gen{b}", n + 1))
                return gen[b], gen_moved[b]

            def wait_scores(self, eng, step):
                b, n_max, n_exp, _ = self.plan.score[step]
                eng.wait_ge(score_full[b], self.val("score", n_max + n_exp + 1))
                return b

        def gates_through(counts, k):
            before = sum(layer.gates > 0 for layer in LAYERS[0:counts.li])
            return counts.it * (16 * PER_LOOP) + 16 * (before * ROUNDS + k // counts.layer.nb + 1)

        def stored_before(counts, k):
            return counts.it * (16 * PER_LOOP) + 16 * (counts.li * ROUNDS + k // counts.layer.nb + 1)

        def max_rows(s, h, t):
            rows, pairs = slice(64 * t, 64 * t + 2 * PAIRS), PAIRS // HALVES
            return (q_stack[s][rows, h * pairs:(h + 1) * pairs, :],
                    maxT[s][rows, :].bitcast(F32).unsqueeze(1).to_broadcast([2 * PAIRS, pairs, S]))

        with nc.Block() as block:
            @block.sync
            def _(sp):
                def load_kind(li, kind):
                    if not weight_dmas(li, kind):
                        return
                    before = [j for j in range(li) if weight_dmas(j, kind)]
                    if before:
                        j = before[-1]
                        k = [b.kind for b in LAYERS[j].blocks].index(kind)
                        for s in range(SLOTS):
                            sp.wait_ge(x_ready[s], base[j]["block"] + (ROUNDS - 1) * LAYERS[j].nb + k + 1)
                    for dst, src in weight_dmas(li, kind):
                        sp.dma_start(dst, src).then_inc(w_loaded[kind], 16)

                def load_x(li, s, seq):
                    src = a["x"] if li == 0 else x_dram
                    sp.dma_start(x_in[s][:, :, :], src[seq].rearrange("(c p) d -> p c d", p=P)).then_inc(x_loaded[s], 16)

                def load_ctx(s, seq):
                    sp.dma_start(ctx_in[s][:, :], a["ctx"][seq]).then_inc(ctx_loaded[s], 16)

                def load_gate(layer, s, seq):
                    src = gates_dram[seq, layer.gate0 * D:(layer.gate0 + layer.gates) * D].partition_broadcast(P)
                    sp.dma_start(gate[s][:, 0:layer.gates, :].rearrange("p g d -> p (g d)"), src).then_inc(gate_loaded[s], 16)

                def store_x(li, s, seq):
                    dst = a["out"] if li == len(LAYERS) - 1 else x_dram
                    sp.dma_start(dst[seq].rearrange("(c p) d -> p c d", p=P), x[s][:, :, :]).then_inc(x_stored[s], 16)

                blocks_before = [0]
                for layer in LAYERS:
                    blocks_before.append(blocks_before[-1] + ROUNDS * layer.nb)

                def serve(counts, k, s, name, j, final):
                    li, layer = counts.li, counts.layer
                    blk, seq, after = layer.all[k], counts.batch(k, s), counts.batch(k + layer.nb, s)
                    more = not final or k + layer.nb < len(layer.all)
                    if more and counts.first(k) and name == ("xb" if blk.out_bias else "out"):
                        if blk.out_bias:
                            sp.wait_ge(biased[s], counts.val("biased", counts.biased(k)))
                        else:
                            sp.wait_ge(x_ready[s], counts.val("block", k + 1))
                        load_x(li, s, after)
                    if more and blk.kind == "cross" and (name, j) == ("qkv", 1):
                        sp.wait_ge(split_ready[s], counts.val("split", 2 * counts.attn(k) + 1))
                        load_ctx(s, after)
                    if counts.first(k + 1) and (name, j) in (("out", 0), ("down", TC - 1)):
                        sp.wait_ge(x_ready[s], counts.val("block", k + 1))
                        store_x(li, s, seq)
                        if more and layer.gates:
                            load_gate(layer, s, after)

                for li, layer in enumerate(LAYERS):
                    start = blocks_before[li]
                    for s in range(SLOTS):
                        if li:
                            prev = LAYERS[li - 1]
                            last = blocks_before[li - 1] + (ROUNDS - 1) * prev.nb
                            sp.wait_ge(x_ready[s], last + 1)
                            sp.wait_ge(x_stored[s], 16 * ((li - 1) * ROUNDS + 2))
                        load_x(li, s, s)
                    if li == 0:
                        load_kind(li, "self")
                    for s in range(SLOTS):
                        if li:
                            sp.wait_ge(x_ready[s], last + 1 + [b.kind for b in prev.blocks].index("cross"))
                        load_ctx(s, s)
                    for s in range(SLOTS):
                        if layer.gates:
                            if li:
                                sp.wait_ge(x_ready[s], start)
                            load_gate(layer, s, s)
                    for kind in kinds:
                        if li or kind != "self":
                            load_kind(li, kind)
                    if li:
                        for s in range(SLOTS):
                            sp.wait_ge(x_stored[s], 16 * (li * ROUNDS + 1))
                    with sp.Fori(0, ITERS - 1) as it:
                        counts = Counts(li, it)
                        for step in counts.plan.steps:
                            serve(counts, *step, False)
                    counts = Counts(li, ITERS - 1)
                    for step in counts.plan.steps:
                        serve(counts, *step, True)
                for s in range(SLOTS):
                    sp.wait_ge(x_stored[s], 16 * (len(LAYERS) * ROUNDS + 1))

            @block.tensor
            def _(pe):
                pe.wait_ge(init_done, SLOTS)

                def fill(counts, step):
                    b, n = counts.plan.gen[step]
                    pe.wait_ge(gen_moved[b], counts.val(f"gen{b}", n))
                    return gen[b], gen_full[b]

                def fill_scores(counts, step):
                    b, n_max, n_exp, before = counts.plan.score[step]
                    if before == "S":
                        pe.wait_ge(max_done[b], counts.val(f"max{b}", n_max))
                    else:
                        pe.wait_ge(exp_done[b], counts.val(f"exp{b}", n_exp))
                    return score[b], score_full[b]

                def project(out, xT, weight, cols):
                    for fc in range(FC):
                        mm = pe.matmul(out, xT[:, fc], weight[:, fc, cols], start=fc == 0, stop=fc == FC - 1)
                    return mm

                def transpose_tokens(counts, step, src):
                    buf, full = fill(counts, step)
                    for fc in range(FC):
                        for c in range(TC):
                            mm = pe.transpose(buf[:, fc * S + c * P:fc * S + c * P + P], src[:, c, fc * P:fc * P + P], ident[:, :])
                    mm.then_inc(full, 1)

                def transpose_ctx(counts, k, s, blk):
                    if blk.ctx == "norm":
                        pe.wait_ge(chat_ready[s], counts.val("cnorm", counts.cnorm(k)))
                        src = chat[s]
                    else:
                        pe.wait_ge(ctx_loaded[s], counts.loads(k))
                        src = ctx_in[s]
                    buf, full = fill(counts, (k, s, "cT", 0))
                    for fc in range(FC):
                        mm = pe.transpose(buf[:, fc * P:fc * P + CTX], src[:, fc * P:fc * P + P], ident[0:CTX, 0:CTX])
                    mm.then_inc(full, 1)

                def project_in(counts, k, s, blk, j):
                    context = blk.kind == "cross" and j == 1
                    counts.wait_moved(pe, (k, s, "cT" if context else "xT", 0))
                    pe.wait_ge(w_loaded[blk.kind], loads_through[blk.kind][counts.li])
                    buf, full = fill(counts, (k, s, "qkv", j))
                    if blk.kind == "self" and j < TC:
                        mm = project(buf[:, :], xnT[s][:, :, j * P:j * P + P], w["qkv"], slice(0, 2 * D))
                    elif blk.kind == "cross" and j == 1:
                        mm = project(buf[0:CTX, :], ctxT[s], w["ckv"], slice(0, 2 * D))
                    else:
                        weight, cols = (w["qkv"], slice(2 * D, 3 * D)) if blk.kind == "self" else (w["cq"], slice(0, D))
                        for c in range(TC):
                            mm = project(buf[:, c * D:c * D + D], xnT[s][:, :, c * P:c * P + P], weight, cols)
                    mm.then_inc(full, 1)

                def stack(counts, k, s, blk, name, j):
                    tok = qk_tok[s][:, :, :, :, :, :].bitcast(F32).rearrange("p c t (q two) r d -> p c t q (two r d)", two=2)
                    if j == 0:
                        parts = 1 if blk.kind == "cross" and name == "stkK" else 2
                        pe.wait_ge(split_ready[s], counts.val("split", 2 * counts.attn(k) + parts))
                    buf, full = fill(counts, (k, s, name, j))
                    if name == "stkK" and blk.kind == "cross":
                        for i in range(4):
                            mm = pe.transpose(buf[:, i * P:i * P + CTX], tok[0:CTX, 0, 1, 4 * j + i, :], ident[0:CTX, 0:CTX])
                    else:
                        for i in range(2):
                            for c in range(TC):
                                mm = pe.transpose(buf[:, i * S + c * P:i * S + c * P + P],
                                                  tok[:, c, 0 if name == "stkQ" else 1, 2 * j + i, :], ident[:, :])
                    mm.then_inc(full, 1)

                def score_rows(counts, k, s, blk, u):
                    counts.wait_moved(pe, (k, s, "stkK", u // 2) if blk.kind == "self" else (k, s, "stkQ", u))
                    if u == 0:
                        if blk.mask and blk.kind == "cross":
                            pe.wait_ge(copies_done[s], counts.copies(k))
                    buf, full = fill_scores(counts, (k, s, "S", u))
                    for c in range(TC):
                        q = slice(c * P, c * P + P)
                        if blk.kind == "self":
                            if blk.mask:
                                pe.matmul(buf[:, c, :], ident_bf[:, :], maskq[:, c, :].unsqueeze(1).to_broadcast([P, 2, S]), start=True, stop=False)
                            mm = pe.matmul(buf[:, c, :], q_stack[s][:, u, q], k_stack[s][:, u, :, :].rearrange("p t k -> p (t k)"),
                                           start=not blk.mask, stop=True)
                        else:
                            if blk.mask:
                                pe.matmul(buf[:, c, 0:4 * CTXP], ones_bf[:, :], krow[s][:, :, :].rearrange("p t k -> p (t k)"),
                                          start=True, stop=False, skip_group_check=True)
                            for i in range(2):
                                mm = pe.matmul(buf[:, c, 2 * i * CTXP:2 * (i + 1) * CTXP], q_stack[s][:, 2 * u + i, q],
                                               k_stack[s][:, 2 * u + i, :, 0:CTXP], start=not blk.mask, stop=True, skip_group_check=True)
                    mm.then_inc(full, 1)

                def score_columns(counts, k, s, blk, u):
                    n = score_uses(blk) // HALVES
                    if u % n == 0:
                        pe.wait_ge(max_rows_ready[s], counts.val("rows", 2 * (HALVES * counts.attn(k) + u // n + 1)))
                    buf, full = fill_scores(counts, (k, s, "ST", u))
                    heads = 2 if blk.kind == "self" else 4
                    for i in range(heads):
                        p, t = (heads * u + i) // 2, i % 2
                        if blk.kind == "self":
                            if blk.mask:
                                pe.matmul(buf[:, i, :], ident_bf[:, :], maskk[:, :, :].rearrange("p c q -> p (c q)"),
                                          start=True, stop=False, skip_group_check=True)
                            for kc in range(TC):
                                mm = pe.matmul(buf[:, i, kc * S:kc * S + S], k_stack[s][:, p, t, kc * P:kc * P + P], q_stack[s][:, p, :],
                                               start=not blk.mask, stop=True, skip_group_check=True)
                        else:
                            mm = pe.matmul(buf[0:CTX, i // 2, i % 2 * S:i % 2 * S + S], k_stack[s][:, p, t, 0:CTX], q_stack[s][:, p, :],
                                           start=True, stop=True, skip_group_check=True)
                    mm.then_inc(full, 1)

                def weigh(counts, k, s, blk, g):
                    keys, chunks = (P, TC) if blk.kind == "self" else (CTX, 1)
                    fills = group_fills(blk, g)
                    b, _, n_exp, _ = counts.plan.score[(k, s, "ST", fills[-1])]
                    pe.wait_ge(exp_done[b], counts.val(f"exp{b}", n_exp + 1))
                    if g == 0:
                        counts.wait_moved(pe, (k, s, "qkv", 2 if blk.kind == "self" else 1))
                    half, within = g // (NG // HALVES), g % (NG // HALVES)
                    if within == 0:
                        pe.wait_ge(pv_moved, counts.val("pv", HALVES * counts.plan.pv[(k, s)] + half))
                    for kc in range(chunks):
                        for i in range(HG):
                            per_fill = HG // len(fills)
                            pb, _ = counts.plan.probs[(k, s, "ST", fills[i // per_fill])]
                            mm = pe.matmul(pv[VW * i:VW * i + VW, within, :], v_one[s][0:keys, kc, HG * g + i, :],
                                           probs[pb][0:keys, i % per_fill * chunks + kc, :], start=kc == 0, stop=kc == chunks - 1,
                                           skip_group_check=True)
                    mm.then_inc(weighed, 1)

                def transpose_back(counts, k, s, h):
                    pe.wait_ge(pv_moved, counts.val("pv", HALVES * counts.plan.pv[(k, s)] + h + 1))
                    buf, full = fill(counts, (k, s, "oX", h))
                    per_half = NG // HALVES
                    for c in range(TC):
                        for i in range(per_half):
                            at_col = (c * per_half + i) * P
                            mm = pe.transpose(buf[:, at_col:at_col + P], oT[s][:, h * per_half + i, c * P:c * P + P], ident[:, :])
                    mm.then_inc(full, 1)

                def transpose_output(counts, k, s, blk, h):
                    counts.wait_moved(pe, (k, s, "oX", h))
                    buf, full = fill(counts, (k, s, "atT", h))
                    for i, fc in enumerate(chunks_of(blk, h)):
                        for c in range(TC):
                            at_col = i * S + c * P
                            mm = pe.transpose(buf[:, at_col:at_col + P], at[s][:, c, fc * P:fc * P + P], ident[:, :])
                    mm.then_inc(full, 1)

                def project_out(counts, k, s, blk):
                    counts.wait_moved(pe, (k, s, "atT", HALVES - 1))
                    buf, full = fill(counts, (k, s, "out", 0))
                    for c in range(TC):
                        mm = project(buf[:, c * D:c * D + D], atT[s][:, :, c * P:c * P + P], w["so" if blk.kind == "self" else "co"], slice(0, D))
                    mm.then_inc(full, 1)

                def mlp_up(counts, k, s, j):
                    if j == 0:
                        counts.wait_moved(pe, (k, s, "xT", 0))
                        pe.wait_ge(w_loaded["mlp"], loads_through["mlp"][counts.li])
                    buf, full = fill(counts, (k, s, "up", j))
                    for i in range(2):
                        col = (2 * j + i) * P
                        for fc in range(FC):
                            mm = pe.matmul(buf[:, i * S:i * S + S], w["w1"][:, fc, col:col + P], xnT[s][:, fc, :],
                                           start=fc == 0, stop=fc == FC - 1)
                    mm.then_inc(full, 1)

                def mlp_down(counts, k, s, c):
                    counts.wait_moved(pe, (k, s, "up", FFC // 2 - 1))
                    buf, full = fill(counts, (k, s, "down", c))
                    for j in range(FFC):
                        mm = pe.matmul(buf[:, 0:D], hT[s][:, j, c * P:c * P + P], w["w2"][:, j, :], start=j == 0, stop=j == FFC - 1)
                    mm.then_inc(full, 1)

                for li in range(len(LAYERS)):
                    with pe.Fori(0, ITERS) as it:
                        counts = Counts(li, it)
                        for k, s, name, j in counts.plan.steps:
                            blk = counts.layer.all[k]
                            if name == "xT":
                                counts.wait_normed(pe, k, s)
                                transpose_tokens(counts, (k, s, name, j), xhat[s])
                            elif name == "cT":
                                transpose_ctx(counts, k, s, blk)
                            elif name == "qkv":
                                project_in(counts, k, s, blk, j)
                            elif name in ("stkQ", "stkK"):
                                stack(counts, k, s, blk, name, j)
                            elif name == "S":
                                score_rows(counts, k, s, blk, j)
                            elif name == "maxT":
                                pe.wait_ge(max_tok_ready[s], counts.val("half", HALVES * counts.attn(k) + j + 1))
                                buf, full = fill(counts, (k, s, name, j))
                                for c in range(TC):
                                    mm = pe.transpose(buf[:, c * P:c * P + P], max_tok[s][:, c, :].bitcast(F32), ident[:, :])
                                mm.then_inc(full, 1)
                            elif name == "ST":
                                score_columns(counts, k, s, blk, j)
                            elif name == "W":
                                weigh(counts, k, s, blk, j)
                            elif name == "oX":
                                transpose_back(counts, k, s, j)
                            elif name == "atT":
                                transpose_output(counts, k, s, blk, j)
                            elif name == "out":
                                project_out(counts, k, s, blk)
                            elif name == "up":
                                mlp_up(counts, k, s, j)
                            elif name == "down":
                                mlp_down(counts, k, s, j)

            @block.scalar
            def _(act):
                act.wait_ge(init_done, SLOTS)

                def modulated(counts, out, buf, s, pair, width, stride, moved):
                    for fc in range(FC):
                        col = (pair * 2) * FC + fc
                        ins = act.activation(out[:, fc, :], buf[:, fc * stride:fc * stride + width], ACT.Identity,
                                             bias=mod[s][:, col + FC:col + FC + 1], scale=mod[s][:, col:col + 1])
                    ins.then_inc(moved, 1)

                for li, layer in enumerate(LAYERS):
                    with act.Fori(0, ITERS) as it:
                        counts = Counts(li, it)
                        for step in counts.plan.steps:
                            k, s, name, j = step
                            blk = counts.layer.all[k]
                            if name == "cp":
                                seq, width, col = counts.batch(k, s), layer.mods * 2 * FC, layer.mod0 * 2 * FC
                                act.copy(mod[s][:, 0:width], mod_all[:, seq, col:col + width]).then_inc(copies_done[s], 1)
                                if li == 0:
                                    act.copy(krow[s][:, :, 0:CTX], kbias_row[:, seq, :].unsqueeze(1).to_broadcast([1, 4, CTX])).then_inc(copies_done[s], 1)
                                    act.copy(kcol[s][:, :], kbias_col[:, bass.ds(seq, 1)]).then_inc(copies_done[s], 1)
                            elif name in ("xT", "cT") and (blk.mod if name == "xT" else blk.ctx_mod) is not None:
                                act.wait_ge(copies_done[s], counts.copies(k))
                                buf, moved = counts.wait_filled(act, step)
                                if name == "xT":
                                    modulated(counts, xnT[s], buf, s, blk.mod, S, S, moved)
                                else:
                                    modulated(counts, ctxT[s], buf, s, blk.ctx_mod, CTX, P, moved)
                            elif name == "xT":
                                buf, moved = counts.wait_filled(act, step)
                                act.copy(xnT[s][:, :, :], buf[:, :].rearrange("p (f t) -> p f t", f=FC)).then_inc(moved, 1)
                            elif name == "cT":
                                buf, moved = counts.wait_filled(act, step)
                                act.copy(ctxT[s][:, :, :], buf[:, 0:FC * P].rearrange("p (f t) -> p f t", f=FC)[:, :, 0:CTX]).then_inc(moved, 1)
                            elif name == "qkv" and j == 2 and not blk.qkv_bias:
                                buf, moved = counts.wait_filled(act, step)
                                act.copy(v_one[s][:, :, :, 0:HD], buf[:, :].rearrange("p (c h d) -> p c h d", c=TC, h=H)).then_inc(moved, 1)
                            elif name == "stkQ":
                                buf, moved = counts.wait_filled(act, step)
                                act.copy(q_stack[s][:, 2 * j:2 * j + 2, :], buf[:, :].rearrange("p (i t) -> p i t", i=2)).then_inc(moved, 1)
                            elif name == "stkK":
                                buf, moved = counts.wait_filled(act, step)
                                n, width = (2, S) if blk.kind == "self" else (4, CTX)
                                src = buf[:, :].rearrange("p (i t) -> p i t", i=n)
                                for t in range(2):
                                    half = slice(64 * t, 64 * t + 64)
                                    ins = act.copy(k_stack[s][half, n * j:n * j + n, t, 0:width], src[half, :, 0:width])
                                ins.then_inc(moved, 1)
                            elif name == "maxT":
                                counts.wait_moved(act, step)
                                act.copy(*max_rows(s, j, 1)).then_inc(max_rows_ready[s], 1)
                            elif name == "ST":
                                if blk.mask and blk.kind == "cross" and j == 0:
                                    act.wait_ge(copies_done[s], counts.copies(k))
                                b = counts.wait_scores(act, step)
                                pb, n = counts.plan.probs[step]
                                act.wait_ge(weighed, counts.val("weighed", n))
                                keys = P if blk.kind == "self" else CTX
                                kbias = kcol[s][:, 0:1] if blk.mask and blk.kind == "cross" else 0.0
                                act.activation(probs[pb][0:keys, :, :], score[b][0:keys, :, :].rearrange("p a (r q) -> p (a r) q", r=2), ACT.Exp,
                                               bias=kbias, scale=SCALE).then_inc(exp_done[b], 1)
                            elif name == "pv":
                                per_half = NG // HALVES
                                act.wait_ge(weighed, counts.val("weighed", counts.plan.weighed[(k, s, "W", (j + 1) * per_half - 1)] + 1))
                                act.copy(oT[s][:, j * per_half:(j + 1) * per_half, :], pv[:, :, :]).then_inc(pv_moved, 1)
                            elif name == "atT":
                                buf, moved = counts.wait_filled(act, step)
                                chunks = chunks_of(blk, j)
                                act.copy(atT[s][:, chunks[0]:chunks[-1] + 1, :], buf[:, 0:len(chunks) * S].rearrange("p (f t) -> p f t", t=S)).then_inc(moved, 1)
                            elif name == "up":
                                if j == 0:
                                    act.wait_ge(w_loaded["mlp"], loads_through["mlp"][li])
                                buf, moved = counts.wait_filled(act, step)
                                for i in range(2):
                                    fn = ACT.Gelu_apprx_tanh if blk.gelu == "tanh" else ACT.Gelu
                                    ins = act.activation(hT[s][:, 2 * j + i, :], buf[:, i * S:i * S + S], fn, bias=b1[:, 2 * j + i:2 * j + i + 1])
                                ins.then_inc(moved, 1)

            @block.gpsimd
            def _(pool):
                def add_bias(counts, k, s, blk):
                    counts.wait_normed(pool, k, s)
                    old = x_in[s] if counts.first(k) else x[s]
                    if counts.first(k):
                        pool.wait_ge(x_stored[s], stored_before(counts, k))
                    pool.wait_ge(w_loaded[blk.kind], loads_through[blk.kind][counts.li])
                    add = bias[out_bias[blk.kind]]
                    if blk.gate is not None:
                        pool.wait_ge(gate_loaded[s], gates_through(counts, k))
                        n = sum(b.gate is not None and b.out_bias for b in counts.layer.all[0:k + 1])
                        pool.tensor_tensor(gated_bias[s][:, :], add[:, :], gate[s][:, blk.gate, :], ALU.mult).then_inc(gated[s], 1)
                        pool.wait_ge(gated[s], counts.val("gated", n))
                        add = gated_bias[s]
                    pool.tensor_tensor(x[s][:, :, :], old[:, :, :], add[:, :].unsqueeze(1).to_broadcast([P, TC, D]), ALU.add).then_inc(biased[s], 1)

                for li, layer in enumerate(LAYERS):
                    with pool.Fori(0, ITERS) as it:
                        counts = Counts(li, it)
                        for k, s, name, j in counts.plan.steps:
                            blk = layer.all[k]
                            if name == "ln":
                                pool.wait_ge(var_ready[s], counts.val("block", k + 1))
                                pool.tensor_tensor(rstd[s][:, :], var_eps[s][:, :], minus_half[:, :], ALU.pow).then_inc(rstd_ready[s], 1)
                            elif name == "cn" and blk.ctx == "norm":
                                pool.wait_ge(c_var_ready[s], counts.val("cnorm", counts.cnorm(k)))
                                pool.tensor_tensor(c_rstd[s][:, :], c_var_eps[s][:, :], minus_half[0:CTX, 0:1], ALU.pow).then_inc(c_rstd_ready[s], 1)
                            elif name == "xb":
                                add_bias(counts, k, s, blk)

            @block.vector
            def _(dve):
                for signal in gen_full + gen_moved + max_done + exp_done + split_ready + [weighed, pv_moved]:
                    dve.sem_inc(signal, 1)
                for s in range(SLOTS):
                    dve.sem_inc(x_stored[s], 16)

                links = {"n": 0}
                splits = {}

                def link(counts, ins):
                    links["n"] += 1
                    ins.then_inc(dve_link, 1)
                    dve.wait_ge(dve_link, counts.val("link", links["n"]))

                def statistics(counts, k, s):
                    src = x_in[s] if counts.first(k) else x[s]
                    if counts.first(k):
                        dve.wait_ge(x_loaded[s], counts.loads(k))
                    else:
                        dve.wait_ge(x_ready[s], counts.val("block", k))
                    for c in range(TC):
                        ins = dve.bn_stats(stats[s][:, c, :], src[:, c, :])
                    link(counts, ins)
                    dve.memset(pause[:, :], 0.0)
                    for c in range(TC):
                        ins = dve.bn_aggr(mean_var[s][:, c, :], stats[s][:, c, :])
                    link(counts, ins)
                    dve.tensor_scalar(var_eps[s][:, :], mean_var[s][:, :, 1], counts.layer.eps, None, ALU.add).then_inc(var_ready[s], 1)

                def normalise(counts, k, s):
                    src = x_in[s] if counts.first(k) else x[s]
                    dve.wait_ge(rstd_ready[s], counts.val("block", k + 1))
                    if k and counts.layer.all[k - 1].kind == "mlp":
                        counts.wait_moved(dve, (k - 1, s, "xT", 0))
                    for c in range(TC):
                        ins = dve.tensor_scalar(xhat[s][:, c, :], src[:, c, :], mean_var[s][:, c, 0:1], rstd[s][:, c:c + 1],
                                                ALU.subtract, ALU.mult)
                    ins.then_inc(xhat_ready[s], 1)

                def context_norm(counts, k, s):
                    dve.wait_ge(ctx_loaded[s], counts.loads(k))
                    if counts.layer.gates:
                        dve.wait_ge(biased[s], counts.val("biased", counts.biased(k - 1)))
                    link(counts, dve.bn_stats(c_stats[s][:, :], ctx_in[s][:, :]))
                    dve.memset(pause[:, :], 0.0)
                    link(counts, dve.bn_aggr(c_mean_var[s][:, :], c_stats[s][:, :]))
                    dve.tensor_scalar(c_var_eps[s][:, :], c_mean_var[s][:, 1:2], counts.layer.eps, None, ALU.add).then_inc(c_var_ready[s], 1)
                    dve.wait_ge(c_rstd_ready[s], counts.val("cnorm", counts.cnorm(k)))
                    dve.tensor_scalar(chat[s][:, :], ctx_in[s][:, :], c_mean_var[s][:, 0:1], c_rstd[s][:, 0:1],
                                      ALU.subtract, ALU.mult).then_inc(chat_ready[s], 1)

                def rotate(counts, out, src, cos, sin, moved):
                    n = len(src.shape)
                    lo, hi = (slice(None),) * (n - 1) + (slice(0, HD // 2),), (slice(None),) * (n - 1) + (slice(HD // 2, HD),)
                    ra, rb = like(rope_a, src), like(rope_b, src)
                    dve.tensor_tensor(ra, src, cos, ALU.mult)
                    dve.tensor_tensor(rb[lo], src[hi], sin[lo], ALU.mult)
                    ins = dve.tensor_tensor(rb[hi], src[lo], sin[hi], ALU.mult)
                    if moved is not None:
                        ins.then_inc(moved[0], 1)
                        dve.wait_ge(moved[0], moved[1])
                    else:
                        link(counts, ins)
                    link(counts, dve.tensor_tensor(out, ra, rb, ALU.add))

                def like(t, src):
                    if len(src.shape) == 3:
                        return t[0:src.shape[0], 0:src.shape[1], :]
                    return t[:, :, :].rearrange("p (c h) d -> p c h d", c=src.shape[1])

                def moved_value(counts, step):
                    b, n = counts.plan.gen[step]
                    return gen_moved[b], counts.val(f"gen{b}", n + 1)

                def split(counts, s, jobs):
                    tok = qk_tok[s]
                    for src, n, c, t in jobs:
                        rows = slice(1, 3) if t == 0 else slice(1, 4, 2)
                        ins = dve.tensor_copy(tok[0:n, c, t, :, rows, :], src.unsqueeze(2).to_broadcast([n, H, 2, HD]))
                    link(counts, ins)
                    for src, n, c, t in jobs:
                        ins = dve.tensor_tensor(tok[0:n, c, t, :, 3 if t == 0 else 2, :], src, tok[0:n, c, t, :, 1, :].bitcast(F32), ALU.subtract)
                    ins.then_inc(split_ready[s], 1)
                    splits[s] += 1
                    splits["last"] = s

                def inputs(counts, k, s, blk, j):
                    step = (k, s, "qkv", j)
                    before = splits["last"]
                    for slot in range(SLOTS) if before is None else [before]:
                        dve.wait_ge(split_ready[slot], counts.val("split", splits[slot]))
                    if blk.kind == "self" and j < TC:
                        buf, moved = counts.wait_filled(dve, step)
                        src = buf[:, :].rearrange("p (h d) -> p h d", d=HD)
                        if blk.rope:
                            at_chunk = j if counts.layer.rope_period == S else 0
                            cos, sin = (t[:, at_chunk, :].unsqueeze(1).to_broadcast([P, 2 * H, HD]) for t in (cos_t, sin_t))
                            rotate(counts, qk_f32[:, :, :], src, cos, sin, moved_value(counts, step))
                        else:
                            dve.wait_ge(w_loaded["self"], loads_through["self"][counts.li])
                            dve.tensor_tensor(qk_f32[:, :, :], src, bias["qkv"][:, 0:2 * D].rearrange("p (h d) -> p h d", d=HD), ALU.add).then_inc(moved, 1)
                            counts.wait_moved(dve, step)
                        split(counts, s, [(qk_f32[:, t * H:t * H + H, :], P, j, t) for t in range(2)])
                    elif blk.kind == "self" and blk.qkv_bias:
                        buf, moved = counts.wait_filled(dve, step)
                        vb = bias["qkv"][:, 2 * D:3 * D].rearrange("p (h d) -> p h d", d=HD)
                        for c in range(TC):
                            ins = dve.tensor_tensor(v_one[s][:, c, :, 0:HD], buf[:, c * D:c * D + D].rearrange("p (h d) -> p h d", d=HD), vb, ALU.add)
                        ins.then_inc(moved, 1)
                    elif blk.kind == "cross" and j == 0:
                        buf, moved = counts.wait_filled(dve, step)
                        q = qk_f32[:, :, :].rearrange("p (c h) d -> p c h d", c=TC)
                        src = buf[:, :].rearrange("p (c h d) -> p c h d", c=TC, d=HD)
                        if blk.rope:
                            cos, sin = (t[:, :, :].unsqueeze(2).to_broadcast([P, TC, H, HD]) for t in (cos_t, sin_t))
                            rotate(counts, q, src, cos, sin, moved_value(counts, step))
                        elif blk.qkv_bias:
                            dve.wait_ge(w_loaded["cross"], loads_through["cross"][counts.li])
                            qb = bias["cq"][:, :].rearrange("p (h d) -> p h d", d=HD).unsqueeze(1).to_broadcast([P, TC, H, HD])
                            dve.tensor_tensor(q, src, qb, ALU.add).then_inc(moved, 1)
                            counts.wait_moved(dve, step)
                        else:
                            dve.tensor_copy(q, src).then_inc(moved, 1)
                            counts.wait_moved(dve, step)
                        split(counts, s, [(q[:, c, :, :], P, c, 0) for c in range(TC)])
                    elif blk.kind == "cross":
                        buf, moved = counts.wait_filled(dve, step)
                        src = buf[0:CTX, 0:D].rearrange("p (h d) -> p h d", d=HD)
                        v = buf[0:CTX, D:2 * D].rearrange("p (h d) -> p h d", d=HD)
                        ck = qk_f32[0:CTX, 0:H, :]
                        if blk.qkv_bias:
                            cb = bias["ckv"][0:CTX, :].rearrange("p (h d) -> p h d", d=HD)
                            dve.tensor_tensor(ck, src, cb[:, 0:H, :], ALU.add)
                            dve.tensor_tensor(v_one[s][0:CTX, 0, :, 0:HD], v, cb[:, H:2 * H, :], ALU.add).then_inc(moved, 1)
                        elif blk.rope:
                            cos, sin = (t[0:CTX, 0, :].unsqueeze(1).to_broadcast([CTX, H, HD]) for t in (cos_t, sin_t))
                            rotate(counts, ck, src, cos, sin, None)
                            dve.tensor_copy(v_one[s][0:CTX, 0, :, 0:HD], v).then_inc(moved, 1)
                        else:
                            dve.tensor_copy(ck, src)
                            dve.tensor_copy(v_one[s][0:CTX, 0, :, 0:HD], v).then_inc(moved, 1)
                        counts.wait_moved(dve, step)
                        split(counts, s, [(ck, CTX, 0, 1)])

                def maximum(counts, k, s, blk, u):
                    step = (k, s, "S", u)
                    b = counts.wait_scores(dve, step)
                    if blk.kind == "self":
                        src, n = score[b][:, :, :].rearrange("p c (h k) -> p c h k", h=2), 2
                    else:
                        src, n = score[b][:, :, 0:4 * CTXP].rearrange("p c (h k) -> p c h k", h=4)[:, :, :, 0:CTX], 4
                    dve.tensor_reduce(row_max[s][:, :, n * u:n * u + n], src, AX_X, ALU.max).then_inc(max_done[b], 1)

                def negate_maximum(counts, k, s, blk, h):
                    n, pairs = score_uses(blk) // HALVES, PAIRS // HALVES
                    b, n_max, _, _ = counts.plan.score[(k, s, "S", h * n + n - 1)]
                    dve.wait_ge(max_done[b], counts.val(f"max{b}", n_max + 1))
                    src = row_max[s][:, :, :].rearrange("p c (q two) -> p c two q", two=2)[:, :, :, h * pairs:(h + 1) * pairs]
                    dst = max_tok[s][:, :, :].rearrange("p c (two n) -> p c two n", two=2)
                    high, low = (dst[:, :, :, part * PAIRS + h * pairs:part * PAIRS + (h + 1) * pairs] for part in range(2))
                    link(counts, dve.tensor_scalar(high, src, -1.0, None, ALU.mult))
                    for c in range(TC):
                        ins = dve.scalar_tensor_tensor(out=low[:, c], in0=src[:, c], scalar=-1.0, in1=high[:, c].bitcast(F32),
                                                       op0=ALU.mult, op1=ALU.subtract)
                    ins.then_inc(max_tok_ready[s], 1)

                def spread_maximum(counts, k, s, h):
                    step = (k, s, "maxT", h)
                    buf, moved = counts.wait_filled(dve, step)
                    dve.tensor_copy(maxT[s][:, :], buf[:, 0:S]).then_inc(moved, 1)
                    counts.wait_moved(dve, step)
                    dve.tensor_copy(*max_rows(s, h, 0)).then_inc(max_rows_ready[s], 1)

                def divide(counts, k, s, h):
                    buf, moved = counts.wait_filled(dve, (k, s, "oX", h))
                    heads = buf[:, :].rearrange("p (c h v) -> p c h v", c=TC, v=VW)
                    total = rsum[s][:, :, h * H // HALVES:(h + 1) * H // HALVES]
                    link(counts, dve.reciprocal(total, heads[:, :, :, HD]))
                    dve.tensor_tensor(at[s][:, :, h * P:h * P + P].rearrange("p c (h d) -> p c h d", d=HD), heads[:, :, :, 0:HD],
                                      total.unsqueeze(3).to_broadcast([P, TC, H // HALVES, HD]), ALU.mult).then_inc(moved, 1)

                def residual(counts, k, s, blk, step):
                    buf, moved = counts.wait_filled(dve, step)
                    if blk.kind == "mlp":
                        c = step[3]
                        n, chunks, src = 1, slice(c, c + 1), buf[:, 0:D].unsqueeze(1)
                    else:
                        n, chunks, src = TC, slice(0, TC), buf[:, :].rearrange("p (c d) -> p c d", c=TC)
                    if blk.out_bias:
                        dve.wait_ge(biased[s], counts.val("biased", counts.biased(k)))
                        old = x[s]
                    else:
                        old = x_in[s] if counts.first(k) else x[s]
                        if counts.first(k):
                            dve.wait_ge(x_stored[s], stored_before(counts, k))
                    if blk.gate is not None:
                        dve.wait_ge(gate_loaded[s], gates_through(counts, k))
                        link(counts, dve.tensor_tensor(delta[s][:, chunks, :], src, gate[s][:, blk.gate, :].unsqueeze(1).to_broadcast([P, n, D]), ALU.mult))
                        src = delta[s][:, chunks, :]
                    dve.tensor_tensor(x[s][:, chunks, :], src, old[:, chunks, :], ALU.add).then_inc(moved, 1)
                    if chunks.stop == TC:
                        counts.wait_moved(dve, step)
                        dve.sem_inc(x_ready[s], 1)

                for li in range(len(LAYERS)):
                    with dve.Fori(0, ITERS) as it:
                        counts = Counts(li, it)
                        links["n"] = 0
                        splits.update({s: 0 for s in range(SLOTS)}, last=None)
                        for k, s, name, j in counts.plan.steps:
                            blk = counts.layer.all[k]
                            if name == "ln":
                                statistics(counts, k, s)
                            elif name == "nx":
                                normalise(counts, k, s)
                            elif name == "cn" and blk.ctx == "norm":
                                context_norm(counts, k, s)
                            elif name == "qkv":
                                inputs(counts, k, s, blk, j)
                            elif name == "S":
                                maximum(counts, k, s, blk, j)
                            elif name == "mx":
                                negate_maximum(counts, k, s, blk, j)
                            elif name == "maxT":
                                spread_maximum(counts, k, s, j)
                            elif name == "oX":
                                divide(counts, k, s, j)
                            elif name in ("out", "down"):
                                residual(counts, k, s, blk, (k, s, name, j))
                        assert links["n"] == counts.plan.count["link"], (li, links["n"], counts.plan.count["link"])


def kernel(**inputs):
    import numpy as np
    import concourse.bacc as bacc
    from concourse.bass_utils import run_bass_kernel_spmd

    def get(name):
        return np.ascontiguousarray(inputs[name])

    def turned(name):
        return np.ascontiguousarray(np.asarray(inputs[name]).T)

    def columns(v):
        return np.ascontiguousarray(np.asarray(v).reshape(-1, P).T)

    L = {n: f"L{n}_xcond_" for n in range(4)}
    inv_freq = 1.0 / 10000.0 ** (np.arange(0, HD, 2, dtype=np.float32) / HD)
    angle = np.outer(np.arange(S, dtype=np.float32), inv_freq).astype(np.float32)
    cos = np.concatenate([np.cos(angle)] * 2, axis=-1).astype(np.float32)
    sin = np.concatenate([-np.sin(angle), np.sin(angle)], axis=-1).astype(np.float32)

    ada_b, mod_b = np.asarray(inputs[L[0] + "adaLN_b"]), np.asarray(inputs[L[2] + "b_mod"])
    ssq, sskv = np.asarray(inputs[L[1] + "bss_q"]), np.asarray(inputs[L[1] + "bss_kv"])
    ln_b = [np.asarray(inputs[L[3] + f"ln{i}_b"]) for i in (1, 2, 3)]

    def part(v, i):
        return v[i * D:(i + 1) * D]

    mod_bias = np.concatenate([part(ada_b, 1), part(ada_b, 0), part(ada_b, 4), part(ada_b, 3), part(ada_b, 7), part(ada_b, 6),
                               ssq, sskv, part(mod_b, 1), part(mod_b, 0), part(mod_b, 4), part(mod_b, 3)] + ln_b)
    gate_bias = np.concatenate([part(ada_b, 2), part(ada_b, 5), part(ada_b, 8), part(mod_b, 2), part(mod_b, 5)])
    norm_w = np.concatenate([np.asarray(inputs[L[0] + n]) for n in ("norm1_w", "normc_w", "norm2_w")])
    mask = np.asarray(inputs["mask_SxS_bk0"])
    kmask = np.asarray(inputs["mask_BxS2_bf1"])

    arrays = {
        "x": get("x"), "ctx": get("ctx_1024"), "condT": turned("cond_1024"),
        "mask": np.ascontiguousarray(mask), "maskT": np.ascontiguousarray(mask.T),
        "kmask": np.ascontiguousarray(kmask), "kmaskT": np.ascontiguousarray(kmask.T),
        "ident": np.eye(P, dtype=np.float32),
        "cos": np.ascontiguousarray(cos.reshape(TC, P, HD).transpose(1, 0, 2)),
        "sin": np.ascontiguousarray(sin.reshape(TC, P, HD).transpose(1, 0, 2)),
        "mod_bias": columns(mod_bias), "gate_bias": gate_bias.reshape(1, -1), "norm_w": columns(norm_w).reshape(P, 3, FC),
        "adaln0": get(L[0] + "adaLN_W"), "adaln1q": get(L[1] + "Wss_q"), "adaln1kv": get(L[1] + "Wss_kv"), "adaln2": get(L[2] + "W_mod"),
        "adaln3a": turned(L[3] + "ln1_w"), "adaln3b": turned(L[3] + "ln2_w"), "adaln3c": turned(L[3] + "ln3_w"),
        "L0_qkv": get(L[0] + "qkv_W"), "L0_so": get(L[0] + "attn_out_W"), "L0_cq": get(L[0] + "cq_W"), "L0_ck": get(L[0] + "ck_W"),
        "L0_cv": get(L[0] + "cv_W"), "L0_co": get(L[0] + "co_W"), "L0_w1": get(L[0] + "mlp_W1"), "L0_w2": get(L[0] + "mlp_W2"),
        "L0_b1": columns(inputs[L[0] + "mlp_b1"]), "L0_b2": get(L[0] + "mlp_b2"),
        "L1_cq": get(L[1] + "Wq"), "L1_ckv": get(L[1] + "Wkv"), "L1_co": get(L[1] + "Wp"),
        "L1_bq": get(L[1] + "bq"), "L1_bkv": get(L[1] + "bkv"), "L1_bo": get(L[1] + "bp"),
        "L2_qkv": get(L[2] + "W_qkv"), "L2_so": get(L[2] + "W_proj"), "L2_cq": get(L[2] + "W_qc"), "L2_ckv": get(L[2] + "W_kvc"),
        "L2_co": get(L[2] + "W_cproj"), "L2_w1": get(L[2] + "W_mlp1"), "L2_w2": get(L[2] + "W_mlp2"),
        "L2_bqkv": get(L[2] + "b_qkv"), "L2_bso": get(L[2] + "b_proj"), "L2_bq": get(L[2] + "b_qc"), "L2_bkv": get(L[2] + "b_kvc"),
        "L2_bo": get(L[2] + "b_cproj"), "L2_b1": columns(inputs[L[2] + "b_mlp1"]), "L2_b2": get(L[2] + "b_mlp2"),
        "L3_qkv": turned(L[3] + "qkv_w"), "L3_so": turned(L[3] + "sa_out_w"), "L3_cq": turned(L[3] + "q_w"), "L3_ck": turned(L[3] + "k_w"),
        "L3_cv": turned(L[3] + "v_w"), "L3_co": turned(L[3] + "ca_out_w"), "L3_w1": turned(L[3] + "ffn_w1"), "L3_w2": turned(L[3] + "ffn_w2"),
        "L3_b1": columns(inputs[L[3] + "ffn_b1"]), "L3_b2": get(L[3] + "ffn_b2"),
    }
    nc = bacc.Bacc("TRN2", target_bir_lowering=False, num_devices=1)
    feed, aps = {}, {}
    for name, v in arrays.items():
        feed[f"in_{name}"] = v
        aps[name] = nc.dram_tensor(f"in_{name}", v.shape, mybir.dt.from_np(v.dtype), kind="ExternalInput").ap()
    aps["out"] = nc.dram_tensor("out_x", (B, S, D), F32, kind="ExternalOutput").ap()
    dit_stack(nc, aps)
    r = run_bass_kernel_spmd(nc, [feed], core_ids=[0])
    return r.results[0]["out_x"]
```
